# Optimizing a Trainium2 kernel written in Bass

```python
import numpy as np
import jax
import jax.numpy as jnp

def _softmax(x, axis=-1):
    return jax.nn.softmax(x, axis=axis)

def _gelu(x):
    return jax.nn.gelu(x, approximate=True)

def _silu(x):
    return jax.nn.silu(x)

def _sigmoid(x):
    return jax.nn.sigmoid(x)

def _layernorm(x, axis=-1, eps=1e-05):
    m = jnp.mean(x, axis=axis, keepdims=True)
    v = jnp.var(x, axis=axis, keepdims=True)
    return (x - m) / jnp.sqrt(v + eps)

def _scatter_add(tgt, idx, src, axis=0):
    return tgt.at[idx].add(src)

def _segment_sum(src, seg, n):
    return jax.ops.segment_sum(src, seg, n)
kernel_name = 'mk_decoder_postln_d1_seqx_r2_e2dfc6'

def setup_inputs(seed: int=0):
    np.random.seed(seed)
    _w = jnp.asarray

    def _rec_inputs():
        import jax
        import jax.numpy as jnp
        _rk = jax.random.key(seed)
        x = 7.22e-05 + 1 * jax.random.normal(jax.random.fold_in(_rk, 1), (2, 2048, 512), jnp.float32)
        _lenS = 2048 - jax.random.randint(jax.random.fold_in(_rk, 7), (2,), 0, max(1, 2048 // 4) + 1, jnp.int32)
        _lenS2 = 77 - jax.random.randint(jax.random.fold_in(_rk, 8), (2,), 0, max(1, 77 // 4) + 1, jnp.int32)
        _ctx_1024P = jax.random.normal(jax.random.fold_in(_rk, 11), (2, 16, 512), jnp.float32)
        _ctx_1024c = jax.random.dirichlet(jax.random.fold_in(_rk, 511), 0.3 * jnp.ones((16,), jnp.float32), (2, 77))
        _ctx_1024t = jnp.einsum('bsk,bkd->bsd', _ctx_1024c, _ctx_1024P)
        _ctx_1024t = _ctx_1024t * jax.lax.rsqrt(jnp.mean(jnp.square(_ctx_1024t)) + 1e-12) * 0.953939
        ctx_1024 = 4.13588e-05 + 0.999923 * (_ctx_1024t + 0.3 * jax.random.normal(jax.random.fold_in(_rk, 611), (2, 77, 512), jnp.float32))
        _validS = jnp.arange(2048)[None, :] < _lenS[:, None]
        _validS2 = jnp.arange(77)[None, :] < _lenS2[:, None]
        _causal = jnp.tril(jnp.ones((2048, 2048), dtype=bool))
        mask_Bx1x1xS2_ff0 = jnp.where(jnp.ones((2, 1, 1, 77), dtype=bool), 0.0, -1000000000.0).astype(jnp.float32)
        return (x, ctx_1024, mask_Bx1x1xS2_ff0)
    x, ctx_1024, mask_Bx1x1xS2_ff0 = _rec_inputs()

    def _L0_attn_setup():
        import jax, jax.numpy as jnp
        import numpy as np
        B, T, D, H = (2, 1024, 512, 16)
        key = jax.random.key(seed)
        k0, k1, k2, k3 = jax.random.split(key, 4)
        s = 0.02
        return {'x': jax.random.normal(k0, (B, T, D), dtype=jnp.float32), 'Wqkv': jax.random.normal(k1, (3 * D, D), dtype=jnp.float32) * s, 'Wout': jax.random.normal(k2, (D, D), dtype=jnp.float32) * s, 'bout': jax.random.normal(k3, (D,), dtype=jnp.float32) * s}
    _L0_attn_all = _L0_attn_setup()
    _L0_attn_in = {k: v for k, v in _L0_attn_all.items() if k in ('Wqkv', 'Wout', 'bout')}
    del _L0_attn_all

    def _L0_xattn_setup():
        import jax, jax.numpy as jnp
        import numpy as np
        D_MODEL = 512
        NUM_HEADS = 16
        HEAD_DIM = D_MODEL // NUM_HEADS
        NEG = -1000000000.0

        def _split_heads(x):
            B, S, _ = x.shape
            return x.reshape(B, S, NUM_HEADS, HEAD_DIM).transpose(0, 2, 1, 3)
        key = jax.random.key(seed)
        ks = jax.random.split(key, 12)
        B, S = (4, 1024)
        scale = 1.0 / np.sqrt(D_MODEL)
        return {'q': jax.random.normal(ks[0], (B, S, D_MODEL), jnp.float32), 'k': jax.random.normal(ks[1], (B, S, D_MODEL), jnp.float32), 'v': jax.random.normal(ks[2], (B, S, D_MODEL), jnp.float32), 'mask': jnp.zeros((B, 1, 1, S), jnp.float32), 'Wq': jax.random.normal(ks[3], (D_MODEL, D_MODEL), jnp.float32) * scale, 'bq': jnp.zeros((D_MODEL,), jnp.float32), 'Wk': jax.random.normal(ks[4], (D_MODEL, D_MODEL), jnp.float32) * scale, 'bk': jnp.zeros((D_MODEL,), jnp.float32), 'Wv': jax.random.normal(ks[5], (D_MODEL, D_MODEL), jnp.float32) * scale, 'bv': jnp.zeros((D_MODEL,), jnp.float32), 'Wo': jax.random.normal(ks[6], (D_MODEL, D_MODEL), jnp.float32) * scale, 'bo': jnp.zeros((D_MODEL,), jnp.float32)}
    _L0_xattn_all = _L0_xattn_setup()
    _L0_xattn_in = {k: v for k, v in _L0_xattn_all.items() if k in ('Wq', 'bq', 'Wk', 'bk', 'Wv', 'bv', 'Wo', 'bo')}
    del _L0_xattn_all

    def _L0_ffn_setup():
        import jax, jax.numpy as jnp
        import numpy as np
        D_MODEL = 512
        D_FF = 2048
        N_EXPERTS = 8
        D_EXPERT = D_FF // N_EXPERTS
        TOP_K = 2
        LB_WEIGHT = 0.01
        B, S = (4, 1024)

        def _top_k_softmax(logits, k):
            vals, _ = jax.lax.top_k(logits, k)
            thresh = vals[..., -1:]
            masked = jnp.where(logits >= thresh, logits, -jnp.inf)
            return jax.nn.softmax(masked, axis=-1)
        key = jax.random.key(seed)
        ks = jax.random.split(key, 8)
        x = jax.random.normal(ks[0], (B, S, D_MODEL), dtype=jnp.float32)
        w1 = jax.random.normal(ks[1], (N_EXPERTS, D_MODEL, D_EXPERT), dtype=jnp.float32) * (1.0 / np.sqrt(D_MODEL))
        b1 = jnp.zeros((N_EXPERTS, D_EXPERT), dtype=jnp.float32)
        w2 = jax.random.normal(ks[2], (N_EXPERTS, D_EXPERT, D_MODEL), dtype=jnp.float32) * (1.0 / np.sqrt(D_EXPERT))
        b2 = jnp.zeros((N_EXPERTS, D_MODEL), dtype=jnp.float32)
        centroids = jax.random.normal(ks[3], (N_EXPERTS, D_MODEL), dtype=jnp.float32) * 0.02
        w_route = jax.random.normal(ks[4], (N_EXPERTS, D_MODEL), dtype=jnp.float32) * (1.0 / np.sqrt(D_MODEL))
        return {'x': x, 'w1': w1, 'b1': b1, 'w2': w2, 'b2': b2, 'centroids': centroids, 'w_route': w_route}
    _L0_ffn_all = _L0_ffn_setup()
    _L0_ffn_in = {k: v for k, v in _L0_ffn_all.items() if k in ('w1', 'b1', 'w2', 'b2', 'centroids', 'w_route')}
    del _L0_ffn_all
    return {'x': x, 'ctx_1024': ctx_1024, 'mask_Bx1x1xS2_ff0': mask_Bx1x1xS2_ff0, 'L0_attn_Wqkv': _L0_attn_in['Wqkv'], 'L0_attn_Wout': _L0_attn_in['Wout'], 'L0_attn_bout': _L0_attn_in['bout'], 'L0_xattn_Wq': _L0_xattn_in['Wq'], 'L0_xattn_bq': _L0_xattn_in['bq'], 'L0_xattn_Wk': _L0_xattn_in['Wk'], 'L0_xattn_bk': _L0_xattn_in['bk'], 'L0_xattn_Wv': _L0_xattn_in['Wv'], 'L0_xattn_bv': _L0_xattn_in['bv'], 'L0_xattn_Wo': _L0_xattn_in['Wo'], 'L0_xattn_bo': _L0_xattn_in['bo'], 'L0_ffn_w1': _L0_ffn_in['w1'], 'L0_ffn_b1': _L0_ffn_in['b1'], 'L0_ffn_w2': _L0_ffn_in['w2'], 'L0_ffn_b2': _L0_ffn_in['b2'], 'L0_ffn_centroids': _L0_ffn_in['centroids'], 'L0_ffn_w_route': _L0_ffn_in['w_route']}

def reference(x, ctx_1024, mask_Bx1x1xS2_ff0, L0_attn_Wqkv, L0_attn_Wout, L0_attn_bout, L0_xattn_Wq, L0_xattn_bq, L0_xattn_Wk, L0_xattn_bk, L0_xattn_Wv, L0_xattn_bv, L0_xattn_Wo, L0_xattn_bo, L0_ffn_w1, L0_ffn_b1, L0_ffn_w2, L0_ffn_b2, L0_ffn_centroids, L0_ffn_w_route):
    import jax
    import jax.numpy as jnp

    def _L0_attn_ref(x, Wqkv, Wout, bout):
        import jax, jax.numpy as jnp
        import numpy as np
        B, T, D, H = (2, 1024, 512, 16)
        b, t, d = x.shape
        h = H
        dh = d // h
        qkv = x @ Wqkv.T
        q, k, v = jnp.split(qkv, 3, axis=-1)

        def merge_heads(z):
            return z.reshape(b, t, h, dh).transpose(0, 2, 1, 3)
        q, k, v = map(merge_heads, (q, k, v))
        scale = dh ** (-0.5)
        dots = jnp.einsum('bhid,bhjd->bhij', q, k) * scale
        causal_mask = jnp.triu(jnp.ones((t, t), dtype=bool), 1)
        dots = jnp.where(causal_mask, -jnp.inf, dots)
        attn = jax.nn.softmax(dots, axis=-1)
        out = jnp.einsum('bhij,bhjd->bhid', attn, v)
        out = out.transpose(0, 2, 1, 3).reshape(b, t, d)
        return out @ Wout.T + bout

    def _L0_xattn_ref(q, k, v, mask, Wq, bq, Wk, bk, Wv, bv, Wo, bo):
        import jax, jax.numpy as jnp
        import numpy as np
        D_MODEL = 512
        NUM_HEADS = 16
        HEAD_DIM = D_MODEL // NUM_HEADS
        NEG = -1000000000.0

        def _split_heads(x):
            B, S, _ = x.shape
            return x.reshape(B, S, NUM_HEADS, HEAD_DIM).transpose(0, 2, 1, 3)
        qh = _split_heads(q @ Wq + bq)
        kh = _split_heads(k @ Wk + bk)
        vh = _split_heads(v @ Wv + bv)
        scores = jnp.einsum('bhqd,bhkd->bhqk', qh, kh) / jnp.sqrt(jnp.asarray(HEAD_DIM, jnp.float32))
        attn = jax.nn.softmax(scores + mask * NEG, axis=-1)
        out = jnp.einsum('bhqk,bhkd->bhqd', attn, vh)
        B, H, Sq, Dh = out.shape
        out = out.transpose(0, 2, 1, 3).reshape(B, Sq, H * Dh)
        return out @ Wo + bo

    def _L0_ffn_ref(x, w1, b1, w2, b2, centroids, w_route):
        import jax, jax.numpy as jnp
        import numpy as np
        D_MODEL = 512
        D_FF = 2048
        N_EXPERTS = 8
        D_EXPERT = D_FF // N_EXPERTS
        TOP_K = 2
        LB_WEIGHT = 0.01
        B, S = (4, 1024)

        def _top_k_softmax(logits, k):
            vals, _ = jax.lax.top_k(logits, k)
            thresh = vals[..., -1:]
            masked = jnp.where(logits >= thresh, logits, -jnp.inf)
            return jax.nn.softmax(masked, axis=-1)
        eps = 1e-12
        x_norm = x / jnp.maximum(jnp.linalg.norm(x, axis=-1, keepdims=True), eps)
        c_norm = centroids / jnp.maximum(jnp.linalg.norm(centroids, axis=-1, keepdims=True), eps)
        cos_scores = jnp.einsum('bsd,ed->bse', x_norm, c_norm)
        route_scores = jnp.einsum('bsd,ed->bse', x, w_route)
        logits = cos_scores + route_scores
        gates = _top_k_softmax(logits, TOP_K)
        h = jax.nn.gelu(jnp.einsum('bsd,edh->bseh', x, w1) + b1, approximate=False)
        expert_out = jnp.einsum('bseh,ehd->bsed', h, w2) + b2
        out = jnp.einsum('bse,bsed->bsd', gates, expert_out)
        return out
    x = _layernorm(x + _L0_attn_ref(x, L0_attn_Wqkv, L0_attn_Wout, L0_attn_bout), axis=-1)
    x = _layernorm(x + _L0_xattn_ref(x, ctx_1024, ctx_1024, mask_Bx1x1xS2_ff0, L0_xattn_Wq, L0_xattn_bq, L0_xattn_Wk, L0_xattn_bk, L0_xattn_Wv, L0_xattn_bv, L0_xattn_Wo, L0_xattn_bo), axis=-1)
    x = _layernorm(x + _L0_ffn_ref(x, L0_ffn_w1, L0_ffn_b1, L0_ffn_w2, L0_ffn_b2, L0_ffn_centroids, L0_ffn_w_route), axis=-1)
    return x

_drawn_inputs = setup_inputs


def setup_inputs(seed=0):
    import zlib

    import numpy as np

    out = dict(_drawn_inputs(seed))
    spreads = {'L0_xattn_bq': (0.0, 0.1),
     'L0_xattn_bk': (0.0, 0.1),
     'L0_xattn_bv': (0.0, 0.1),
     'L0_xattn_bo': (0.0, 0.1),
     'L0_ffn_b1': (0.0, 0.1),
     'L0_ffn_b2': (0.0, 0.1)}
    factors = {}
    for name, (base, spread) in spreads.items():
        noise = np.random.default_rng([zlib.crc32(name.encode()), seed]).standard_normal(out[name].shape)
        drawn = base * np.exp(spread * noise) if base else spread * noise
        out[name] = jnp.asarray(drawn.astype(out[name].dtype))
    for name, factor in factors.items():
        out[name] = (out[name] * factor).astype(out[name].dtype)
    return out
```

```python
from contextlib import ExitStack

import concourse.bass as bass
from concourse import mybir

F32, F16, BF16 = mybir.dt.float32, mybir.dt.float16, mybir.dt.bfloat16
ALU, ACT, AX = mybir.AluOpType, mybir.ActivationFunctionType, mybir.AxisListType

B, T, D, H, DH = 2, 2048, 512, 16, 32
S2 = 77
E, DE = 8, 256
N = B * T
P = 128
KT = D // P
HG = P // DH
NG = H // HG
CH = 512
NC = N // CH
CPB = T // CH
TT = CH // P
FT = E * DE // P
EPS = 1e-5
NEG = -1e9

XS = 32.0
WS = 512.0
UN = 1.0 / (XS * WS)
QK = XS * XS
MASKED = -1e30
TERMS = ((0, 0), (1, 0), (0, 1))


class Count:

    def __init__(self, nc, stack, name, per):
        self.sem, self.per = stack.enter_context(nc.semaphore(name)), per

    def lead(self, engine, made=0):
        engine.sem_inc(self.sem, self.per - made)

    def at(self, lap, k):
        return (lap + 1) * self.per + k + 1


def sems(nc, stack, name, n):
    return [stack.enter_context(nc.semaphore(f"{name}{s}")) for s in range(n)]


def project_qkv(nc, xT, wqkvT, q_parts, k_parts, v_rows):
    NU = 2
    LAPS = NC // NU
    OT = 2 * KT
    PER = OT + TT
    NB, NQ, NV = 8, 4, 2
    QL, VL = NU * OT // NQ, NU * TT // NV
    with ExitStack() as stack:
        sb = lambda *a: stack.enter_context(nc.sbuf_tensor(*a))
        w_raw = sb("w_raw", [P, KT, 3 * D], F32)
        w_parts = sb("w_hi", [P, KT, 3 * D], F16), sb("w_lo", [P, KT, 3 * D], F16)
        x_raw = sb("x_raw", [P, NU, KT, CH], F32)
        x_parts = sb("x_hi", [P, NU, KT, CH], F16), sb("x_lo", [P, NU, KT, CH], F16)
        qk_out = sb("qk_out", [P, NQ, 2, CH], F16)
        v_out = sb("v_out", [P, NV, D], F32)
        prod = stack.enter_context(nc.psum_tensor("prod", [P, NB, CH], F32))
        w_loaded, w_hi_ready, w_lo_ready = (stack.enter_context(nc.semaphore(s)) for s in
                                            ("w_loaded", "w_hi_ready", "w_lo_ready"))
        x_loaded = sems(nc, stack, "x_loaded", NU)
        qk_stored, v_stored = sems(nc, stack, "qk_stored", NQ), sems(nc, stack, "v_stored", NV)
        x_hi_ready = Count(nc, stack, "x_hi_ready", NU)
        x_lo_ready = Count(nc, stack, "x_lo_ready", NU)
        prod_ready = Count(nc, stack, "prod_ready", NU * PER)
        hi_ready = Count(nc, stack, "hi_ready", NU * OT)
        prod_read = Count(nc, stack, "prod_read", NU * PER)
        block = stack.enter_context(nc.Block())

        @block.sync
        def _(sp):
            def load(i, u):
                sp.wait_ge(x_lo_ready.sem, x_lo_ready.at(i, u - NU))
                sp.dma_start(x_raw[:, u], xT[:, bass.ds((NU * i + u) * CH, CH)].rearrange(
                    "(t p) n -> p t n", p=P)).then_inc(x_loaded[u], 16)

            def store(i, u):
                at = (NU * i + u) * CH
                for o in range(OT):
                    sp.wait_ge(prod_read.sem, prod_read.at(i, u * PER + o))
                    parts = q_parts if o < KT else k_parts
                    f = (o % KT) * P
                    sp.dma_start(parts[:, f:f + P, bass.ds(at, CH)].rearrange("s p n -> p s n"),
                                 qk_out[:, o % NQ]).then_inc(qk_stored[o % NQ], 16)
                for j in range(TT):
                    sp.wait_ge(prod_read.sem, prod_read.at(i, u * PER + OT + j))
                    sp.dma_start(v_rows[bass.ds(at + j * P, P), :], v_out[:, j % NV]).then_inc(v_stored[j % NV], 16)

            sp.dma_start(w_raw[:], wqkvT.rearrange("(t p) n -> p t n", p=P)).then_inc(w_loaded, 16)
            for u in range(NU):
                load(0, u)
            with sp.Fori(0, LAPS - 1) as i:
                for u in range(NU):
                    store(i, u)
                    load(i + 1, u)
            for u in range(NU):
                store(LAPS - 1, u)
            for s in qk_stored:
                sp.wait_ge(s, 16 * QL * LAPS)
            for s in v_stored:
                sp.wait_ge(s, 16 * VL * LAPS)

        @block.scalar
        def _(act):
            x_hi_ready.lead(act)
            hi_ready.lead(act)
            act.wait_ge(w_loaded, 16)
            nc.scalar.activation(w_parts[0][:], w_raw[:], ACT.Copy, scale=WS).then_inc(w_hi_ready, 1)
            with act.Fori(0, LAPS) as i:
                for u in range(NU):
                    act.wait_ge(x_loaded[u], 16 * i + 16)
                    act.wait_ge(prod_ready.sem, prod_ready.at(i, (u - NU) * PER + PER - 1))
                    nc.scalar.activation(x_parts[0][:, u], x_raw[:, u], ACT.Copy, scale=XS).then_inc(x_hi_ready.sem, 1)
                    for o in range(OT):
                        k = u * PER + o
                        act.wait_ge(prod_ready.sem, prod_ready.at(i, k))
                        act.wait_ge(qk_stored[o % NQ], 16 * (QL * i + (u * OT + o) // NQ))
                        nc.scalar.activation(qk_out[:, o % NQ, 0], prod[:, k % NB], ACT.Copy,
                                             scale=UN * XS).then_inc(hi_ready.sem, 1)

        @block.vector
        def _(dve):
            x_lo_ready.lead(dve)
            prod_read.lead(dve)
            dve.wait_ge(w_hi_ready, 1)
            nc.vector.scalar_tensor_tensor(w_parts[1][:], w_raw[:], WS, w_parts[0][:], ALU.mult,
                                           ALU.subtract).then_inc(w_lo_ready, 1)
            with dve.Fori(0, LAPS) as i:
                for u in range(NU):
                    dve.wait_ge(x_hi_ready.sem, x_hi_ready.at(i, u))
                    nc.vector.scalar_tensor_tensor(x_parts[1][:, u], x_raw[:, u], XS, x_parts[0][:, u], ALU.mult,
                                                   ALU.subtract).then_inc(x_lo_ready.sem, 1)
                    for o in range(OT):
                        k = u * PER + o
                        dve.wait_ge(hi_ready.sem, hi_ready.at(i, u * OT + o))
                        nc.vector.scalar_tensor_tensor(qk_out[:, o % NQ, 1], prod[:, k % NB], UN * XS,
                                                       qk_out[:, o % NQ, 0], ALU.mult,
                                                       ALU.subtract).then_inc(prod_read.sem, 1)
                    for j in range(TT):
                        k = u * PER + OT + j
                        dve.wait_ge(prod_ready.sem, prod_ready.at(i, k))
                        dve.wait_ge(v_stored[j % NV], 16 * (VL * i + (u * TT + j) // NV))
                        nc.vector.tensor_scalar(v_out[:, j % NV], prod[:, k % NB], UN, None,
                                                ALU.mult).then_inc(prod_read.sem, 1)

        @block.tensor
        def _(pe):
            prod_ready.lead(pe)
            pe.wait_ge(w_lo_ready, 1)
            with pe.Fori(0, LAPS) as i:
                for u in range(NU):
                    pe.wait_ge(x_lo_ready.sem, x_lo_ready.at(i, u))
                    for m in range(PER):
                        k = u * PER + m
                        pe.wait_ge(prod_read.sem, prod_read.at(i, k - NB))
                        for s, (t, (a, b)) in enumerate((t, ab) for t in range(KT) for ab in TERMS):
                            if m < OT:
                                lhs, rhs = w_parts[a][:, t, m * P:(m + 1) * P], x_parts[b][:, u, t]
                            else:
                                j = m - OT
                                lhs, rhs = x_parts[a][:, u, t, j * P:(j + 1) * P], w_parts[b][:, t, 2 * D:3 * D]
                            last = nc.tensor.matmul(prod[:, k % NB], lhs, rhs, start=(s == 0), stop=(s == 3 * KT - 1))
                        last.then_inc(prod_ready.sem, 1)


def self_attention(nc, q_parts, k_parts, v_rows, o_parts):
    NR = 3 * DH
    NM = NR + 2
    GROUPS = B * NG
    PAIR = 2
    NP = 4
    VU = [(c, kt, pr) for c in range(CPB) for kt in range((c + 1) * TT) for pr in range(HG // PAIR)]
    MU = [(c, j, h, s) for c in range(CPB) for j in range(TT) for h in range(HG) for s in range(c + 1)]
    KU = [(c, kt) for c in range(CPB) for kt in range((c + 1) * TT)]
    NVU, NMU, NKU = len(VU), len(MU), len(KU)
    POOLED = [[n for n, (k, kt) in enumerate(KU) if k == c and kt < c * TT and kt % 4 != 3] for c in range(CPB)]
    ADDS = [n for tiles in POOLED for n in tiles[1:]]
    START = 4
    MROW_LAG = 6
    SCALE = DH ** -0.5 / QK

    def schedule():
        after, done, rows = [], 0, []
        ends = [max(n for n, m in enumerate(MU) if m[0] == c) for c in range(CPB)]
        for u in range(NVU):
            upto = 0 if u < START else -(-(u - START + 1) * NMU // (NVU - START))
            todo = []
            while done < upto:
                todo.append(("max", done))
                done += 1
                for c in range(CPB):
                    if done == min(ends[c] + MROW_LAG, NMU):
                        todo.append(("rows", c))
            after.append(todo)
        return after

    AFTER = schedule()
    with ExitStack() as stack:
        sb = lambda *a: stack.enter_context(nc.sbuf_tensor(*a))
        ps = lambda *a: stack.enter_context(nc.psum_tensor(*a))
        q_pair = [sb(f"q_pair{a}", [NM, HG, T], F16) for a in range(2)]
        k_pair = [sb(f"k_pair{a}", [NM, HG, T], F16) for a in range(2)]
        v_sb = [sb(f"v_sb{a}", [P, T // P, P], F32) for a in range(2)]
        probs = sb("probs", [P, NP, HG, CH], F32)
        total = sb("total", [P, 2, HG, CH], F32)
        ones = sb("ones", [P, DH], F32)
        ident_f = sb("ident_f", [P, P], F32)
        ident = sb("ident_bf", [P, P], BF16)
        ident16 = sb("ident16", [P, P], F16)
        future_f = sb("future_f", [P, 2, P], F32)
        future = sb("future", [P, 2, P], BF16)
        seg_max = sb("seg_max", [P, HG, TT, CPB], F32)
        row_max = sb("row_max", [P, HG, TT], F32)
        max_parts = sb("max_parts", [P, HG, TT, 2], F16)
        recip = sb("recip", [P, CH], F32)
        o_sb = sb("o_sb", [P, CH], F32)
        o_out = sb("o_out", [P, 2, 2, CH], F16)
        st_ps = ps("st_ps", [P, 2, PAIR, CH], F32)
        s_ps = ps("s_ps", [P, 2, CH], F32)
        o_ps = ps("o_ps", [P, CH], F32)
        den_ps = ps("den_ps", [P, CH], F32)
        made, const_ready, factors_ready = (stack.enter_context(nc.semaphore(s)) for s in
                                            ("made", "const_ready", "factors_ready"))
        qk_loaded = [sems(nc, stack, f"qk_loaded{a}_", CPB) for a in range(2)]
        v_loaded = sems(nc, stack, "v_loaded", 2)
        o_stored = sems(nc, stack, "o_stored", 2)
        st_ready = Count(nc, stack, "st_ready", 2 * NVU)
        exp_done = Count(nc, stack, "exp_done", 2 * NVU)
        pv_done = Count(nc, stack, "pv_done", 2 * NKU)
        added = Count(nc, stack, "added", 2 * len(ADDS))
        s_ready = Count(nc, stack, "s_ready", 2 * NMU)
        s_read = Count(nc, stack, "s_read", 2 * NMU)
        max_ready = Count(nc, stack, "max_ready", 2 * CPB)
        rows_ready = Count(nc, stack, "rows_ready", 2 * CPB * HG)
        rows_read = Count(nc, stack, "rows_read", 2 * CPB * HG)
        norm_done = Count(nc, stack, "norm_done", 2 * CPB)
        o_hi_done = Count(nc, stack, "o_hi_done", 2 * CPB)
        split_done = Count(nc, stack, "split_done", 2 * CPB)
        steps = Count(nc, stack, "steps", 2 * 2 * CPB)
        recips = Count(nc, stack, "recips", 2 * CPB)
        block = stack.enter_context(nc.Block())
        LAPS = GROUPS // 2

        def m_slot(m):
            return m % 2

        def last_tile(c):
            return max(n for n, k in enumerate(KU) if k[0] == c)

        def adds_upto(k):
            return sum(max(sum(n <= k for n in tiles[1:]), tiles[0] <= k) for tiles in POOLED if tiles)

        def max_base(a):
            return 0 if a == 1 else NMU

        @block.gpsimd
        def _(pool):
            split_done.lead(pool)
            nc.gpsimd.memset(ones[:], 1.0).then_inc(made, 1)
            nc.gpsimd.memset(ident_f[:], 0.0).then_inc(made, 1)
            nc.gpsimd.memset(future_f[:], 0.0).then_inc(made, 1)
            pool.wait_ge(made, 3)
            nc.gpsimd.affine_select(out=ident_f[:], in_=ident_f[:], compare_op=ALU.not_equal, fill=1.0, base=0,
                                    pattern=[[-1, P]], channel_multiplier=1).then_inc(made, 1)
            for n, sign in enumerate((1, -1)):
                nc.gpsimd.affine_select(out=future_f[:, n], in_=future_f[:, n], compare_op=ALU.is_ge, fill=MASKED,
                                        base=0, pattern=[[-sign, P]], channel_multiplier=sign).then_inc(made, 1)
            pool.wait_ge(made, 6)
            nc.gpsimd.tensor_copy(ident[:], ident_f[:]).then_inc(const_ready, 1)
            nc.gpsimd.tensor_copy(ident16[:], ident_f[:]).then_inc(const_ready, 1)
            nc.gpsimd.tensor_copy(future[:], future_f[:]).then_inc(const_ready, 1)
            added.lead(pool)

            def lo_part(i, n):
                pool.wait_ge(o_hi_done.sem, o_hi_done.at(i, n))
                nc.gpsimd.tensor_tensor(o_out[:, n % 2, 1], o_sb[:], o_out[:, n % 2, 0],
                                        ALU.subtract).then_inc(split_done.sem, 1)

            with pool.Fori(0, LAPS) as i:
                for a in range(2):
                    n = a * len(ADDS)
                    for c in range(CPB):
                        for k, tile in enumerate(POOLED[c][1:]):
                            pool.wait_ge(exp_done.sem, exp_done.at(i, a * NVU + PAIR * tile + PAIR - 1))
                            if k == 0:
                                before = last_tile(c - 2) if c >= 2 else last_tile(c + 2) - NKU
                                pool.wait_ge(pv_done.sem, pv_done.at(i, a * NKU + before))
                                first = probs[:, (a * NKU + POOLED[c][0]) % NP]
                            else:
                                pool.wait_ge(added.sem, added.at(i, n - 1))
                                first = total[:, c % 2]
                            nc.gpsimd.tensor_tensor(total[:, c % 2], first, probs[:, (a * NKU + tile) % NP],
                                                    ALU.add).then_inc(added.sem, 1)
                            n += 1
                            if k == 0:
                                lo_part(i, a * CPB + c - 1)
                    lo_part(i, a * CPB + CPB - 1)

        @block.sync
        def _(sp):
            def load(g, a, c):
                b, f = g // NG, (g % NG) * P
                cols = bass.ds(b * T + c * CH, CH)
                for pair, parts, order in ((k_pair[a], k_parts, (0, 0, 1)), (q_pair[a], q_parts, (0, 1, 0))):
                    for r, part in enumerate(order):
                        sp.dma_start(pair[r * DH:(r + 1) * DH, :, c * CH:(c + 1) * CH],
                                     parts[part, bass.ds(f, P), cols].rearrange("(h p) n -> p h n", p=DH)).then_inc(
                                         qk_loaded[a][c], 16)
                if c == CPB - 1:
                    sp.dma_start(v_sb[a][:], v_rows[bass.ds(b * T, T), bass.ds(f, P)].rearrange(
                        "(t p) f -> p t f", p=P)).then_inc(v_loaded[a], 16)

            def store(i, a, c):
                n = a * CPB + c
                sp.wait_ge(split_done.sem, split_done.at(i, n))
                g = 2 * i + a
                b, f = g // NG, (g % NG) * P
                sp.dma_start(o_parts[:, bass.ds(f, P), bass.ds(b * T + c * CH, CH)].rearrange("s p n -> p s n"),
                             o_out[:, c % 2]).then_inc(o_stored[c % 2], 16)

            def lap(i, last):
                for a in range(2):
                    for c in range(CPB):
                        store(i, a, c)
                    if not last:
                        sp.wait_ge(pv_done.sem, pv_done.at(i, (a + 1) * NKU - 1))
                        for c in range(CPB):
                            load(2 * i + 2 + a, a, c)

            for a in range(2):
                for c in range(CPB):
                    load(a, a, c)
            with sp.Fori(0, LAPS - 1) as i:
                lap(i, False)
            lap(LAPS - 1, True)
            for s in o_stored:
                sp.wait_ge(s, 16 * CPB * LAPS)

        @block.scalar
        def _(act):
            exp_done.lead(act)
            rows_read.lead(act, CPB * HG)

            def rows(i, a, c):
                for h in range(HG):
                    n = (CPB * HG if a == 0 else 0) + c * HG + h
                    act.wait_ge(rows_ready.sem, rows_ready.at(i, n))
                    nc.scalar.activation(q_pair[a][NR:NM, h, c * CH:(c + 1) * CH], s_ps[NR:NM, h % 2],
                                         ACT.Copy).then_inc(rows_read.sem, 1)

            def group(i, a, ahead):
                for u, (c, kt, pr) in enumerate(VU):
                    n = a * NVU + u
                    off = max(kt - c * TT, 0) * P
                    act.wait_ge(st_ready.sem, st_ready.at(i, n))
                    k = u // 2
                    slot = (a * NKU + k) % NP
                    if pr == 0:
                        act.wait_ge(pv_done.sem, pv_done.at(i, a * NKU + k - NP))
                        upto = adds_upto(k - NP) if k >= NP else adds_upto(NKU + k - NP) - len(ADDS)
                        act.wait_ge(added.sem, added.at(i, a * len(ADDS) + upto - 1))
                    nc.scalar.activation(probs[:, slot, pr * PAIR:(pr + 1) * PAIR, off:], st_ps[:, n % 2, :, off:], ACT.Exp,
                                         scale=SCALE).then_inc(exp_done.sem, 1)
                    if ahead:
                        for what, m in AFTER[u]:
                            if what == "rows":
                                rows(i, 1 - a, m)

            for c in range(CPB):
                rows(-1, 0, c)
            with act.Fori(0, LAPS - 1) as i:
                group(i, 0, True)
                group(i, 1, True)
            group(LAPS - 1, 0, True)
            group(LAPS - 1, 1, False)

        @block.vector
        def _(dve):
            s_read.lead(dve, NMU)
            max_ready.lead(dve, CPB)
            norm_done.lead(dve)
            o_hi_done.lead(dve)

            def maximum(i, a, m):
                c, j, h, s = MU[m]
                n = max_base(a) + m
                width = CH if s < c else (j + 1) * P
                dve.wait_ge(s_ready.sem, s_ready.at(i, n))
                nc.vector.reduce_max(seg_max[:, h, j, s:s + 1], s_ps[:, m_slot(m), 0:width],
                                     AX.X).then_inc(s_read.sem, 1)
                if m + 1 == NMU or MU[m + 1][0] > c:
                    k = (CPB if a == 0 else 0) + c
                    dve.wait_ge(s_read.sem, s_read.at(i, n))
                    dve.wait_ge(rows_ready.sem, rows_ready.at(i, (k - 1) * HG + HG - 1))
                    nc.vector.reduce_max(row_max[:], seg_max[:, :, :, 0:c + 1], AX.X).then_inc(steps.sem, 1)
                    dve.wait_ge(steps.sem, steps.at(i, 2 * k))
                    nc.vector.tensor_scalar(max_parts[:, :, :, 0], row_max[:], -1.0 / QK, None,
                                            ALU.mult).then_inc(steps.sem, 1)
                    dve.wait_ge(steps.sem, steps.at(i, 2 * k + 1))
                    nc.vector.scalar_tensor_tensor(max_parts[:, :, :, 1], row_max[:], -1.0 / QK,
                                                   max_parts[:, :, :, 0], ALU.mult,
                                                   ALU.subtract).then_inc(max_ready.sem, 1)

            def normalise(i, a, c):
                n = a * CPB + c
                dve.wait_ge(pv_done.sem, pv_done.at(i, a * NKU + last_tile(c)))
                nc.vector.reciprocal(recip[:], den_ps[:]).then_inc(recips.sem, 1)
                dve.wait_ge(recips.sem, recips.at(i, n))
                dve.wait_ge(split_done.sem, split_done.at(i, n - 1))
                nc.vector.scalar_tensor_tensor(o_sb[:], o_ps[:], XS, recip[:], ALU.mult,
                                               ALU.mult).then_inc(norm_done.sem, 1)
                dve.wait_ge(norm_done.sem, norm_done.at(i, n))
                dve.wait_ge(o_stored[c % 2], 16 * (CPB * i + n // 2))
                nc.vector.tensor_copy(o_out[:, c % 2, 0], o_sb[:]).then_inc(o_hi_done.sem, 1)

            def group(i, a, ahead):
                for u, (c, kt, pr) in enumerate(VU):
                    if ahead:
                        for what, m in AFTER[u]:
                            if what == "max":
                                maximum(i, 1 - a, m)
                    if pr == PAIR - 1 and kt == 0 and c > 0:
                        normalise(i, a, c - 1)
                normalise(i, a, CPB - 1)

            steps.lead(dve, 2 * CPB)
            recips.lead(dve)
            for a in range(2):
                nc.vector.memset(k_pair[a][NR:NM], QK).then_inc(factors_ready, 1)
            for m in range(NMU):
                maximum(-1, 0, m)
            with dve.Fori(0, LAPS - 1) as i:
                group(i, 0, True)
                group(i, 1, True)
            group(LAPS - 1, 0, True)
            group(LAPS - 1, 1, False)

        @block.tensor
        def _(pe):
            st_ready.lead(pe)
            pv_done.lead(pe)
            s_ready.lead(pe, NMU)
            rows_ready.lead(pe, CPB * HG)

            def keys_there(i, a, c):
                pe.wait_ge(qk_loaded[a][c], 6 * 16 * (i + (1 if a == 1 else 2)))

            def maximum(i, a, m):
                c, j, h, s = MU[m]
                n = max_base(a) + m
                if m == 0 or MU[m - 1][0] < c:
                    keys_there(i, a, c)
                slot_free(i, a, m_slot(m), n)
                width = CH if s < c else (j + 1) * P
                q0 = c * CH + j * P
                diagonal = s == c
                last = nc.tensor.matmul(s_ps[:, m_slot(m), 0:width], q_pair[a][0:NR, h, q0:q0 + P],
                                        k_pair[a][0:NR, h, s * CH:s * CH + width], start=True, stop=not diagonal)
                if diagonal:
                    last = nc.tensor.matmul(s_ps[:, m_slot(m), width - P:width], ident[:], future[:, 0],
                                            start=False, stop=True)
                last.then_inc(s_ready.sem, 1)

            def slot_free(i, a, slot, n):
                pe.wait_ge(s_read.sem, s_read.at(i, n - 2))

            def rows(i, a, c, n):
                k = (CPB if a == 0 else 0) + c
                pe.wait_ge(max_ready.sem, max_ready.at(i, k))
                for h in range(HG):
                    if h < 2:
                        pe.wait_ge(s_read.sem, s_read.at(i, n - 1))
                    else:
                        pe.wait_ge(rows_read.sem, rows_read.at(i, k * HG + h - 2))
                    for j in range(TT):
                        last = nc.tensor.matmul(s_ps[NR:NM, h % 2, j * P:(j + 1) * P], max_parts[:, h, j, :],
                                                ident16[:], start=(j == 0), stop=(j == TT - 1),
                                                skip_group_check=True)
                    last.then_inc(rows_ready.sem, 1)
                pe.wait_ge(rows_read.sem, rows_read.at(i, k * HG + HG - 1))

            def scores(i, a, u):
                c, kt, pr = VU[u]
                n = a * NVU + u
                if u == 0:
                    back = 0 if a == 1 else -CPB * HG
                    pe.wait_ge(rows_read.sem, rows_read.at(i, back + CPB * HG - 1))
                off = max(kt - c * TT, 0) * P
                pe.wait_ge(exp_done.sem, exp_done.at(i, n - 2))
                for e in range(PAIR):
                    h = pr * PAIR + e
                    diagonal = kt >= c * TT
                    last = nc.tensor.matmul(st_ps[:, n % 2, e, off:], k_pair[a][:, h, kt * P:(kt + 1) * P],
                                            q_pair[a][:, h, c * CH + off:(c + 1) * CH], start=True, stop=not diagonal)
                    if diagonal:
                        last = nc.tensor.matmul(st_ps[:, n % 2, e, off:off + P], ident[:], future[:, 1],
                                                start=False, stop=True)
                last.then_inc(st_ready.sem, 1)

            def values(i, a, k):
                c, kt = KU[k]
                off = max(kt - c * TT, 0) * P
                slot = (a * NKU + k) % NP
                first, final = kt == 0, k == last_tile(c)
                if first:
                    if c == 0:
                        pe.wait_ge(v_loaded[a], 16 * (i + 1))
                    pe.wait_ge(norm_done.sem, norm_done.at(i, a * CPB + c - 1))
                pe.wait_ge(exp_done.sem, exp_done.at(i, a * NVU + PAIR * k + PAIR - 1))
                heads = [slice(h * DH, (h + 1) * DH) for h in range(HG)]
                for h, out in enumerate(heads):
                    last = nc.tensor.matmul(o_ps[out, off:], v_sb[a][:, kt, out], probs[:, slot, h, off:],
                                            start=first, stop=final)
                if k in POOLED[c]:
                    last.then_inc(pv_done.sem, 1)

            def sums(i, a, k):
                c, kt = KU[k]
                off = max(kt - c * TT, 0) * P
                slot = (a * NKU + k) % NP
                heads = [slice(h * DH, (h + 1) * DH) for h in range(HG)]
                final, pooled, last = k == last_tile(c), POOLED[c], None
                if k not in pooled:
                    opens = all(n in pooled for n, (x, _) in enumerate(KU) if x == c and n < k)
                    for h, out in enumerate(heads):
                        last = nc.tensor.matmul(den_ps[out, off:], ones[:], probs[:, slot, h, off:], start=opens,
                                                stop=final and not pooled)
                if final and pooled:
                    pe.wait_ge(added.sem, added.at(i, a * len(ADDS) + adds_upto(k) - 1))
                    for h, out in enumerate(heads):
                        last = nc.tensor.matmul(den_ps[out, :], ones[:], total[:, c % 2, h], start=False, stop=True)
                if last is not None:
                    last.then_inc(pv_done.sem, 1)

            def group(i, a, ahead):
                scores(i, a, 0)
                for u in range(NVU):
                    if u + 1 < NVU:
                        scores(i, a, u + 1)
                    todo = AFTER[u] if ahead else []
                    for n in range(max(len(todo), 2)):
                        if n < len(todo):
                            what, m = todo[n]
                            if what == "max":
                                maximum(i, 1 - a, m)
                                done = m
                            else:
                                rows(i, 1 - a, m, max_base(1 - a) + done + 1)
                        if n == 0 and u >= PAIR:
                            (values if u % PAIR == 0 else sums)(i, a, u // PAIR - 1)
                values(i, a, NKU - 1)
                sums(i, a, NKU - 1)

            pe.wait_ge(const_ready, 3)
            pe.wait_ge(factors_ready, 2)
            for m in range(NMU):
                maximum(-1, 0, m)
                for c in range(CPB):
                    if m + 1 == min(max(n for n, x in enumerate(MU) if x[0] == c) + MROW_LAG, NMU):
                        rows(-1, 0, c, max_base(0) + m + 1)
            with pe.Fori(0, LAPS - 1) as i:
                group(i, 0, True)
                group(i, 1, True)
            group(LAPS - 1, 0, True)
            group(LAPS - 1, 1, False)


def prepare(nc, W, ctxT, wk, bk, wv, bv, weights, centroids, routeT, bout, bo, bq, b1, b2, k_blocks, v_ctx):
    KS = HG * S2
    raws = [wk, wv] + [w for w, _ in weights]
    with ExitStack() as stack:
        sb = lambda *a: stack.enter_context(nc.sbuf_tensor(*a))
        sem = lambda s: stack.enter_context(nc.semaphore(s))
        kv_ps = stack.enter_context(nc.psum_tensor("kv_ps", [P, KT + B, CH], F32))
        t_ps = stack.enter_context(nc.psum_tensor("t_ps", [P, CH], F32))
        ctx_sb = sb("ctx_sb", [P, KT, B * S2], F32)
        bk_sb, bv_bc = sb("bk_sb", [P, KT], F32), sb("bv_bc", [S2, D], F32)
        cent, cent_sq = sb("cent", [E, D], F32), sb("cent_sq", [E, D], F32)
        cent_ss = sb("cent_ss", [E, 1], F32)
        cent_rn = sb("cent_rn", [E, 1], F32)
        blocks = W["soft"][:].rearrange("p j h s -> p (j h s)")[:, 0:B * NG * KS].rearrange(
            "p (b g n) -> p b g n", b=B, g=NG)
        vals = W["x1"][0:S2, 0:B]
        small, cleared, consts = sem("small_loaded"), sem("blocks_cleared"), sem("consts_made")
        raw_loaded = sems(nc, stack, "raw_loaded", 5)
        kv_done, keys_done, vals_done, kv_stored = sem("kv_done"), sem("keys_done"), sem("vals_done"), sem("kv_stored")
        hi_done, lo_done = sem("hi_done"), sem("lo_done")
        squared, norm_ready, cent_ready, cent_turned, route_ready = (
            sem(s) for s in ("squared", "norm_ready", "cent_ready", "cent_turned", "route_ready"))
        block = stack.enter_context(nc.Block())

        NS = 5
        more = sb("staging", [P, NS - 2, TT * D], F32)

        def raw(n):
            return W["work"][:, n % NS] if n % NS < 2 else more[:, n % NS - 2]

        @block.sync
        def _(sp):
            smalls = [(ctx_sb[:], ctxT.rearrange("(t p) n -> p t n", p=P)),
                      (bk_sb[:], bk),
                      (bv_bc[:], bv.partition_broadcast(S2)),
                      (cent[:], centroids), (W["route_raw"][:, :, E:2 * E], routeT.rearrange("(t p) e -> p t e", p=P)),
                      (W["bout_bc"][:], bout.partition_broadcast(P)), (W["bo_bc"][:], bo.partition_broadcast(P)),
                      (W["bq_sb"][:], bq),
                      (W["b1_sb"][:], b1), (W["b2_sb"][:], b2)]
            for dst, src in smalls:
                sp.dma_start(dst, src).then_inc(small, 16)
            assert len(smalls) == SMALLS
            for n, src in enumerate(raws):
                if n in (NS, NS + 1):
                    sp.wait_ge(kv_done, 1)
                elif n > NS + 1:
                    sp.wait_ge(lo_done, n - NS - 1)
                sp.dma_start(raw(n).rearrange("p (a b) -> p a b", a=src.shape[1]), src).then_inc(
                    raw_loaded[n % NS], 16)
            sp.wait_ge(keys_done, NG * HG)
            sp.dma_start(k_blocks.rearrange("b p n -> p b n"), blocks.rearrange("p b g n -> p b (g n)")).then_inc(kv_stored, 16)
            sp.wait_ge(vals_done, B)
            sp.dma_start(v_ctx.rearrange("b p n -> p b n"), vals).then_inc(kv_stored, 16)
            sp.wait_ge(kv_stored, 32)

        @block.gpsimd
        def _(pool):
            nc.gpsimd.memset(W["ident"][:], 0.0).then_inc(consts, 1)
            nc.gpsimd.memset(W["power"][:], -0.5).then_inc(consts, 1)
            pool.wait_ge(consts, 2)
            nc.gpsimd.affine_select(out=W["ident"][:], in_=W["ident"][:], compare_op=ALU.not_equal, fill=1.0, base=0,
                                    pattern=[[-1, P]], channel_multiplier=1).then_inc(consts, 1)
            pool.wait_ge(squared, 2)
            nc.gpsimd.tensor_tensor(cent_rn[:], cent_ss[:], W["power"][0:E, 0:1], ALU.pow).then_inc(norm_ready, 1)

        @block.scalar
        def _(act):
            act.wait_ge(small, 16 * SMALLS)
            nc.scalar.activation(cent_sq[:], cent[:], ACT.Square, accum_out=cent_ss[:]).then_inc(squared, 1)
            act.wait_ge(cleared, 1)
            act.wait_ge(kv_done, 1)
            for g in range(NG):
                for h in range(HG):
                    rows = slice(h * DH, (h + 1) * DH)
                    nc.scalar.activation(blocks[rows, :, g, h * S2:(h + 1) * S2],
                                         kv_ps[rows, g, 0:B * S2].rearrange("p (b s) -> p b s", b=B), ACT.Identity,
                                         bias=bk_sb[rows, g:g + 1]).then_inc(keys_done, 1)
            for n in range(2, len(raws)):
                act.wait_ge(raw_loaded[n % NS], 16 * (n // NS + 1))
                nc.scalar.activation(weights[n - 2][1][0], raw(n), ACT.Copy, scale=WS).then_inc(hi_done, 1)

        @block.vector
        def _(dve):
            nc.vector.memset(blocks, 0.0).then_inc(cleared, 1)
            dve.wait_ge(squared, 1)
            nc.vector.tensor_scalar(cent_ss[:], cent_ss[:], 1e-24, None, ALU.max).then_inc(squared, 1)
            dve.wait_ge(norm_ready, 1)
            nc.vector.tensor_scalar(cent[:], cent[:], cent_rn[:], None, ALU.mult).then_inc(cent_ready, 1)
            dve.wait_ge(cent_turned, 1)
            nc.vector.tensor_copy(W["route_raw"][:, :, 0:E], t_ps[:, 0:KT * E].rearrange(
                "p (t e) -> p t e", t=KT)).then_inc(route_ready, 1)
            dve.wait_ge(route_ready, 1)
            nc.vector.tensor_scalar(W["route_p"][0][:], W["route_raw"][:], WS, None, ALU.mult).then_inc(route_ready, 1)
            dve.wait_ge(route_ready, 2)
            nc.vector.scalar_tensor_tensor(W["route_p"][1][:], W["route_raw"][:], WS, W["route_p"][0][:], ALU.mult,
                                           ALU.subtract).then_inc(route_ready, 1)
            dve.wait_ge(kv_done, 1)
            for b in range(B):
                nc.vector.tensor_tensor(vals[:, b], kv_ps[0:S2, KT + b], bv_bc[:], ALU.add).then_inc(vals_done, 1)
            for n in range(2, len(raws)):
                dve.wait_ge(hi_done, n - 1)
                nc.vector.scalar_tensor_tensor(weights[n - 2][1][1], raw(n), WS, weights[n - 2][1][0], ALU.mult,
                                               ALU.subtract).then_inc(lo_done, 1)

        @block.tensor
        def _(pe):
            pe.wait_ge(small, 16 * SMALLS)
            pe.wait_ge(raw_loaded[0], 16)
            for g in range(NG):
                for t in range(KT):
                    nc.tensor.matmul(kv_ps[:, g, 0:B * S2], raw(0)[:, t * D + g * P:t * D + (g + 1) * P],
                                     ctx_sb[:, t], start=(t == 0), stop=(t == KT - 1))
            pe.wait_ge(raw_loaded[1], 16)
            for b in range(B):
                for t in range(KT):
                    last = nc.tensor.matmul(kv_ps[0:S2, KT + b], ctx_sb[:, t, b * S2:(b + 1) * S2],
                                            raw(1)[:, t * D:(t + 1) * D], start=(t == 0), stop=(t == KT - 1))
            last.then_inc(kv_done, 1)
            pe.wait_ge(consts, 3)
            pe.wait_ge(cent_ready, 1)
            for t in range(KT):
                last = nc.tensor.transpose(t_ps[:, t * E:(t + 1) * E], cent[:, t * P:(t + 1) * P],
                                           W["ident"][0:E, 0:E])
            last.then_inc(cent_turned, 1)


SMALLS = 10


def chains(nc, W, x_rows, o_parts, mask, k_blocks, v_ctx, out):
    KS = HG * S2
    SCALE = DH ** -0.5
    USES = (["dve"] * TT + ["dve"] * TT + ["act"] * KT + ["dve"] * (TT * NG)
            + ["act"] * HG + (["act"] * HG + ["dve"]) * (NG - 1) + ["dve"] + ["dve"] * TT + ["dve"] * TT + ["dve"] + ["act"])
    AT_OUT, AT_T1, AT_Q = 0, TT, 2 * TT
    AT_S = AT_Q + KT
    AT_PV = AT_S + TT * NG
    AT_O = AT_PV + (HG + 1) * NG
    AT_TURN = [AT_PV + max(g * (HG + 1) - 1, 0) for g in range(NG)]
    AT_VAL = [AT_TURN[g + 1] + HG for g in range(NG - 1)] + [AT_O - 1]
    AT_T2 = AT_O + TT
    AT_R = AT_T2 + TT
    AT_G = AT_R + 1
    NUSE, CB, FB = len(USES), 4, 4
    UNITS = [("bias", 0, j) for j in range(TT)]
    for e in range(E):
        UNITS += [("hidden", e, 0), ("hidden", e, 1)] + [("expert", e, j) for j in range(TT)]
    NUNIT = len(UNITS)
    F_USES = ["act" if kind == "hidden" else "dve" for kind, _, _ in UNITS]
    assert 2 * NUSE % CB == 0 and 2 * NUNIT % FB == 0
    PLAN = [("out", 5), ("norm1", 0), ("turn1", 2), ("query", 1), ("scores0", 4), ("scores1", 4), ("scores2", 4),
            ("scores3", 7), ("probs0", 1), ("probs1", 1), ("pv0", 1), ("probs2", 1), ("pv1", 1), ("probs3", 1),
            ("pv2", 1), ("pv3", 3), ("out2", 5), ("norm2", 0), ("turn2", 3), ("route", 6), ("gate", 1)]
    STAGES, FILL = zip(*PLAN)
    assert sum(FILL) == NUNIT
    FROM = [sum(FILL[:n]) for n in range(len(FILL))]
    LOOPED = (NC - 2) // 2

    x1, x2, x2T, oT, soft, hT, hidden = (W[k] for k in ("x1", "x2", "x2T", "oT", "soft", "hT", "hidden"))
    x1T = W["work"][:, 0].bitcast(F16).rearrange("p (s t n) -> p s t n", s=2, t=KT)
    xq = W["work"][:, 1].rearrange("p (t n) -> p t n", t=KT)
    ident, power = W["ident"], W["power"]

    def turned(g):
        return W["work"][0:S2, g % 2].rearrange("p (h n) -> p h n", h=HG)

    def nth(uses, k):
        return uses[:k].count(uses[k])

    with ExitStack() as stack:
        sb = lambda *a: stack.enter_context(nc.sbuf_tensor(*a))
        keys, vals = sb("keys", [P, NG, KS], F32), sb("vals", [S2, D], F32)
        mask_sb = sb("mask_sb", [P, S2], F32)
        stats, agg, rstd = sb("stats", [P, TT, 6], F32), sb("agg", [P, TT, 2], F32), sb("rstd", [P, TT], F32)
        stats3, agg3, rstd3 = sb("stats3", [P, TT, 6], F32), sb("agg3", [P, TT, 2], F32), sb("rstd3", [P, TT], F32)
        smax, ssum = sb("smax", [P, TT, H], F32), sb("ssum", [P, TT, H], F32)
        square, rnorm = sb("square", [P, TT], F32), sb("rnorm", [P, TT], F32)
        logit, weight = sb("logit", [P, TT, E], F32), sb("weight", [P, TT, E], F32)
        top, chosen, gsum = sb("top", [P, TT, 8], F32), sb("chosen", [P, TT, E], F32), sb("gsum", [P, TT], F32)
        gates = sb("gates", [P, TT, E], F32)
        gates_un = [sb(f"gates_un{a}", [P, TT, E], F32) for a in range(2)]
        gT = [sb(f"gT{a}", [E, TT, P], F32) for a in range(2)]
        cps = stack.enter_context(nc.psum_tensor("cps", [P, CB, CH], F32))
        fps = stack.enter_context(nc.psum_tensor("fps", [P, FB, CH], F32))

        def count(name, per):
            return Count(nc, stack, name, 2 * per)

        def sem(name):
            return stack.enter_context(nc.semaphore(name))

        x_loaded, oT_loaded, kv_loaded = sem("x_loaded"), sem("oT_loaded"), sem("kv_loaded")
        stored = sems(nc, stack, "stored", 2)
        c_ready = count("c_ready", NUSE)
        act_read = count("act_read", USES.count("act"))
        dve_read = count("dve_read", USES.count("dve"))
        hi_ready = count("hi_ready", TT + NG + TT)
        biased = count("biased", 2)
        summed, spread, varied = count("summed", 2 * TT), count("spread", 2 * TT), count("varied", 2)
        rooted = count("rooted", 2)
        normed = count("normed", 2 * TT)
        masked = count("masked", 1)
        smaxed, shifted, exped = count("smaxed", TT), count("shifted", TT), count("exped", TT)
        ssummed, inverted, probs_ready = count("ssummed", TT), count("inverted", TT), count("probs_ready", TT)
        squared, square_held, norm_rooted = count("squared", TT), count("square_held", 1), count("norm_rooted", 1)
        routed = count("routed", 13)
        gate_exped, gated = count("gate_exped", 1), count("gated", 1)
        f_ready = count("f_ready", NUNIT)
        gelu_done = count("gelu_done", 2 * E)
        h_hi, h_lo = count("h_hi", 2 * E), count("h_lo", 2 * E)
        added = count("acc_added", TT * (E + 1))
        summed3, spread3, varied3 = count("summed3", TT), count("spread3", TT), count("varied3", 1)
        rooted3, normed3 = count("rooted3", 1), count("normed3", TT)
        block = stack.enter_context(nc.Block())

        def at(c, i, u, k):
            return c.at(i, u * (c.per // 2) + k)

        def chunk(i, u):
            return 2 * i + u + 1

        def parity(u):
            return 1 - u

        def program(chain, experts, finish):
            def slot(i, u, with_chain=True, with_experts=True):
                for n, stage in enumerate(STAGES):
                    if with_chain:
                        chain(i, u, stage)
                    if with_experts:
                        for f in range(FROM[n], FROM[n] + FILL[n]):
                            experts(i, u, f, *UNITS[f])
                if with_experts:
                    finish(i, u)
            return slot

        def run(engine, slot):
            slot(-1, 1, with_experts=False)
            with engine.Fori(0, LOOPED) as i:
                slot(i, 0)
                slot(i, 1)
            slot(LOOPED, 0)
            slot(LOOPED, 1, with_chain=False)

        def lead(engine, chain_counts, expert_counts):
            for c in chain_counts:
                c.lead(engine, made=c.per // 2)
            for c in expert_counts:
                c.lead(engine)

        @block.sync
        def _(sp):
            def load(n):
                rows = bass.ds(n * CH, CH)
                sp.dma_start(x1[:], x_rows[rows, :].rearrange("(j p) d -> p j d", p=P)).then_inc(x_loaded, 16)
                sp.dma_start(oT[:], o_parts[:, :, rows].rearrange("s (t p) n -> p s t n", p=P)).then_inc(oT_loaded, 16)
                b = n // CPB
                sp.dma_start(keys[:].rearrange("p g n -> p (g n)"), k_blocks[bass.ds(b, 1)].rearrange(
                    "b p n -> (b p) n")).then_inc(kv_loaded, 16)
                sp.dma_start(vals[:], v_ctx[bass.ds(b, 1)].rearrange("b p n -> (b p) n")).then_inc(kv_loaded, 16)
                sp.dma_start(mask_sb[:], mask[bass.ds(b, 1)].rearrange("b a c s -> (b a c s)").partition_broadcast(
                    P)).then_inc(kv_loaded, 16)

            def load_next(i, u):
                sp.wait_ge(dve_read.sem, at(dve_read, i, u, nth(USES, AT_O + TT - 1)))
                load(chunk(i, u) + 1)

            def store(i, u):
                sp.wait_ge(normed3.sem, at(normed3, i, u, TT - 1))
                sp.dma_start(out[bass.ds((chunk(i, u) - 1) * CH, CH), :].rearrange("(j p) d -> p j d", p=P),
                             x2[u][:]).then_inc(stored[u], 16)

            load(0)
            load_next(-1, 1)
            with sp.Fori(0, LOOPED) as i:
                for u in range(2):
                    load_next(i, u)
                    store(i, u)
            store(LOOPED, 0)
            store(LOOPED, 1)
            for s in stored:
                sp.wait_ge(s, 16 * NC // 2)

        @block.gpsimd
        def _(pool):
            lead(pool, (biased, rooted, probs_ready, norm_rooted), (rooted3,))

            def add_row(row, c, k, i, u):
                nc.gpsimd.tensor_tensor(x1[:], x1[:], row[:].rearrange("p (a n) -> p a n", a=1).broadcast_to(
                    [P, TT, D]), ALU.add).then_inc(c.sem, 1)

            def root(var, c, width):
                nc.gpsimd.tensor_tensor(var, var, power[:, 0:width], ALU.pow).then_inc(c.sem, 1)

            def chain(i, u, stage):
                if stage == "out":
                    pool.wait_ge(x_loaded, 16 * (chunk(i, u) + 1))
                    add_row(W["bout_bc"], biased, 0, i, u)
                    pool.wait_ge(varied.sem, at(varied, i, u, 0))
                    root(rstd[:], rooted, TT)
                elif stage == "turn1":
                    pool.wait_ge(c_ready.sem, at(c_ready, i, u, AT_T1 + TT - 1))
                    add_row(W["bo_bc"], biased, 1, i, u)
                elif stage.startswith("scores"):
                    at_end = int(stage[-1])
                    for j in ([at_end - 1] if at_end else []) + ([at_end] if at_end == TT - 1 else []):
                        pool.wait_ge(inverted.sem, at(inverted, i, u, j))
                        nc.gpsimd.tensor_tensor(soft[:, j], soft[:, j], ssum[:, j, :].rearrange(
                            "p (h a) -> p h a", a=1).broadcast_to([P, H, S2]), ALU.mult).then_inc(probs_ready.sem, 1)
                elif stage == "out2":
                    pool.wait_ge(varied.sem, at(varied, i, u, 1))
                    root(rstd[:], rooted, TT)
                elif stage == "route":
                    pool.wait_ge(square_held.sem, at(square_held, i, u, 0))
                    nc.gpsimd.tensor_tensor(rnorm[:], square[:], power[:, 0:TT], ALU.pow).then_inc(norm_rooted.sem, 1)

            def experts(i, u, f, kind, e, j):
                pass

            def finish(i, u):
                pool.wait_ge(varied3.sem, at(varied3, i, u, 0))
                root(rstd3[:], rooted3, TT)

            run(pool, program(chain, experts, finish))

        @block.scalar
        def _(act):
            lead(act, (act_read, hi_ready, exped, squared, gate_exped), (gelu_done,))

            def wait_product(i, u, k):
                act.wait_ge(c_ready.sem, at(c_ready, i, u, k))
                return cps[:, (u * NUSE + k) % CB]

            def chain(i, u, stage):
                p = parity(u)
                if stage in ("turn1", "turn2"):
                    k0, dst = (AT_T1, x1T) if stage == "turn1" else (AT_T2, x2T[p])
                    for j in range(TT):
                        bank = wait_product(i, u, k0 + j)
                        nc.scalar.activation(dst[:, 0, :, j * P:(j + 1) * P], bank.rearrange("p (t n) -> p t n", t=KT),
                                             ACT.Copy, scale=XS).then_inc(hi_ready.sem, 1)
                elif stage == "query":
                    for o in range(KT):
                        bank = wait_product(i, u, AT_Q + o)
                        nc.scalar.activation(xq[:, o], bank, ACT.Identity, bias=W["bq_sb"][:, o:o + 1],
                                             scale=UN).then_inc(act_read.sem, 1)
                elif stage.startswith("scores"):
                    j = int(stage[-1])
                    act.wait_ge(shifted.sem, at(shifted, i, u, j))
                    nc.scalar.activation(soft[:, j], soft[:, j], ACT.Exp).then_inc(exped.sem, 1)
                elif stage.startswith("probs"):
                    g = int(stage[-1])
                    for h in range(HG):
                        bank = wait_product(i, u, AT_TURN[g] + h)
                        nc.scalar.activation(turned(g)[:, h], bank[0:S2], ACT.Copy).then_inc(act_read.sem, 1)
                elif stage.startswith("pv"):
                    g = int(stage[-1])
                    bank = wait_product(i, u, AT_VAL[g])
                    nc.scalar.activation(oT[:, 0, g], bank, ACT.Copy, scale=XS).then_inc(hi_ready.sem, 1)
                elif stage == "route":
                    for j in range(TT):
                        act.wait_ge(normed.sem, at(normed, i, u, TT + j))
                        nc.scalar.activation(soft[:].rearrange("p j h s -> p (j h s)")[:, j * D:(j + 1) * D],
                                             x2[p][:, j], ACT.Square, accum_out=square[:, j:j + 1]).then_inc(squared.sem, 1)
                elif stage == "gate":
                    act.wait_ge(routed.sem, at(routed, i, u, 8))
                    nc.scalar.activation(weight[:], logit[:], ACT.Exp).then_inc(gate_exped.sem, 1)
                    bank = wait_product(i, u, AT_G)
                    nc.scalar.activation(gT[p][:], bank[0:E].rearrange("e (j n) -> e j n", j=TT),
                                         ACT.Copy).then_inc(act_read.sem, 1)

            def experts(i, u, f, kind, e, j):
                if kind == "hidden":
                    n = 2 * e + j
                    act.wait_ge(f_ready.sem, at(f_ready, i, u, f))
                    act.wait_ge(h_lo.sem, at(h_lo, i, u, n - 2))
                    nc.scalar.activation(hidden[:, n % 2], fps[:, (u * NUNIT + f) % FB], ACT.Gelu,
                                         bias=W["b1_sb"][:, n:n + 1], scale=UN).then_inc(gelu_done.sem, 1)

            def finish(i, u):
                pass

            run(act, program(chain, experts, finish))

        @block.vector
        def _(dve):
            lead(dve, (dve_read, summed, spread, varied, normed, masked, smaxed, shifted, ssummed, inverted,
                       square_held, routed), (h_hi, h_lo, added, summed3, spread3, varied3, normed3))

            def wait_product(i, u, k):
                dve.wait_ge(c_ready.sem, at(c_ready, i, u, k))
                return cps[:, (u * NUSE + k) % CB]

            def lo_part(i, u, k, hi_index, dst, hi):
                bank = cps[:, (u * NUSE + k) % CB]
                if len(dst.shape) == 3:
                    bank = bank.rearrange("p (t n) -> p t n", t=KT)
                dve.wait_ge(hi_ready.sem, at(hi_ready, i, u, hi_index))
                nc.vector.scalar_tensor_tensor(dst, bank, XS, hi, ALU.mult, ALU.subtract).then_inc(dve_read.sem, 1)

            def spreads(rows, st, ag, rs, c, i, u, which, source, k0):
                c_sum, c_spread, c_var, _, _ = c
                for j in range(TT):
                    if j > 0:
                        dve.wait_ge(c_sum.sem, at(c_sum, i, u, which * TT + j - 1))
                    dve.wait_ge(source.sem, at(source, i, u, k0 + j))
                    nc.vector.bn_stats(st[:, j], rows[:, j]).then_inc(c_sum.sem, 1)
                    if j > 0:
                        nc.vector.bn_aggr(ag[:, j - 1], st[:, j - 1]).then_inc(c_spread.sem, 1)
                dve.wait_ge(c_sum.sem, at(c_sum, i, u, which * TT + TT - 1))
                dve.wait_ge(c_spread.sem, at(c_spread, i, u, which * TT + TT - 2))
                nc.vector.tensor_scalar(rs[:, 0:TT - 1], ag[:, 0:TT - 1, 1], EPS, None, ALU.add)
                nc.vector.bn_aggr(ag[:, TT - 1], st[:, TT - 1]).then_inc(c_spread.sem, 1)
                dve.wait_ge(c_spread.sem, at(c_spread, i, u, which * TT + TT - 1))
                nc.vector.tensor_scalar(rs[:, TT - 1:TT], ag[:, TT - 1:TT, 1], EPS, None,
                                        ALU.add).then_inc(c_var.sem, 1)

            def norm(rows, ag, rs, c, i, u, which):
                c_root, c_norm = c[3:]
                dve.wait_ge(c_root.sem, at(c_root, i, u, which))
                for j in range(TT):
                    nc.vector.tensor_scalar(rows[:, j], rows[:, j], ag[:, j, 0:1], rs[:, j:j + 1], ALU.subtract,
                                            ALU.mult).then_inc(c_norm.sem, 1)

            chain_norm = (summed, spread, varied, rooted, normed)

            def softmax_start(i, u, j):
                for g in range(NG):
                    bank = wait_product(i, u, AT_S + j * NG + g)
                    nc.vector.scalar_tensor_tensor(
                        soft[:, j, g * HG:(g + 1) * HG], bank[:, 0:KS].rearrange("p (h s) -> p h s", h=HG), SCALE,
                        mask_sb[:].rearrange("p (a s) -> p a s", a=1).broadcast_to([P, HG, S2]), ALU.mult,
                        ALU.add).then_inc(dve_read.sem, 1)
                dve.wait_ge(dve_read.sem, at(dve_read, i, u, nth(USES, AT_S + j * NG + NG - 1)))
                nc.vector.reduce_max(smax[:, j], soft[:, j], AX.X).then_inc(smaxed.sem, 1)
                dve.wait_ge(smaxed.sem, at(smaxed, i, u, j))
                nc.vector.tensor_tensor(soft[:, j], soft[:, j], smax[:, j].rearrange("p (h a) -> p h a", a=1)
                                        .broadcast_to([P, H, S2]), ALU.subtract).then_inc(shifted.sem, 1)

            def softmax_end(i, u, j):
                dve.wait_ge(exped.sem, at(exped, i, u, j))
                nc.vector.reduce_sum(ssum[:, j], soft[:, j], AX.X).then_inc(ssummed.sem, 1)
                dve.wait_ge(ssummed.sem, at(ssummed, i, u, j))
                nc.vector.reciprocal(ssum[:, j], ssum[:, j]).then_inc(inverted.sem, 1)

            def chain(i, u, stage):
                p = parity(u)
                if stage == "out":
                    dve.wait_ge(biased.sem, at(biased, i, u, 0))
                    for j in range(TT):
                        bank = wait_product(i, u, AT_OUT + j)
                        nc.vector.scalar_tensor_tensor(x1[:, j], bank, UN, x1[:, j], ALU.mult,
                                                       ALU.add).then_inc(dve_read.sem, 1)
                    spreads(x1, stats, agg, rstd, chain_norm, i, u, 0, dve_read, nth(USES, AT_OUT))
                elif stage == "norm1":
                    norm(x1, agg, rstd, chain_norm, i, u, 0)
                elif stage == "turn1":
                    for j in range(TT):
                        cols = slice(j * P, (j + 1) * P)
                        lo_part(i, u, AT_T1 + j, j, x1T[:, 1, :, cols], x1T[:, 0, :, cols])
                elif stage.startswith("scores"):
                    j = int(stage[-1])
                    if j == 0:
                        dve.wait_ge(kv_loaded, 48 * (chunk(i, u) + 1))
                        nc.vector.tensor_scalar(mask_sb[:], mask_sb[:], NEG, None, ALU.mult).then_inc(masked.sem, 1)
                        dve.wait_ge(masked.sem, at(masked, i, u, 0))
                    softmax_start(i, u, j)
                    if j > 0:
                        softmax_end(i, u, j - 1)
                    if j == TT - 1:
                        softmax_end(i, u, j)
                elif stage.startswith("pv"):
                    g = int(stage[-1])
                    lo_part(i, u, AT_VAL[g], TT + g, oT[:, 1, g], oT[:, 0, g])
                elif stage == "out2":
                    dve.wait_ge(biased.sem, at(biased, i, u, 1))
                    dve.wait_ge(stored[p], 16 * (i + u))
                    for j in range(TT):
                        bank = wait_product(i, u, AT_O + j)
                        nc.vector.scalar_tensor_tensor(x2[p][:, j], bank, UN, x1[:, j], ALU.mult,
                                                       ALU.add).then_inc(dve_read.sem, 1)
                    spreads(x2[p], stats, agg, rstd, chain_norm, i, u, 1, dve_read, nth(USES, AT_O))
                elif stage == "norm2":
                    norm(x2[p], agg, rstd, chain_norm, i, u, 1)
                elif stage == "turn2":
                    for j in range(TT):
                        cols = slice(j * P, (j + 1) * P)
                        lo_part(i, u, AT_T2 + j, TT + NG + j, x2T[p][:, 1, :, cols], x2T[p][:, 0, :, cols])
                elif stage == "route":
                    dve.wait_ge(squared.sem, at(squared, i, u, TT - 1))
                    nc.vector.tensor_scalar(square[:], square[:], 1e-24, None, ALU.max).then_inc(square_held.sem, 1)
                    dve.wait_ge(norm_rooted.sem, at(norm_rooted, i, u, 0))
                    bank = wait_product(i, u, AT_R)[:, 0:TT * 2 * E].rearrange("p (j n) -> p j n", j=TT)
                    wide = lambda a: a.rearrange("p (j a) -> p j a", a=1).broadcast_to([P, TT, E])
                    nc.vector.scalar_tensor_tensor(weight[:], bank[:, :, 0:E], UN, wide(rnorm[:]), ALU.mult,
                                                   ALU.mult).then_inc(routed.sem, 1)
                    dve.wait_ge(routed.sem, at(routed, i, u, 0))
                    half = TT // 2
                    nc.vector.scalar_tensor_tensor(logit[:, 0:half], bank[:, 0:half, E:2 * E], UN, weight[:, 0:half],
                                                   ALU.mult, ALU.add).then_inc(routed.sem, 1)
                    dve.wait_ge(routed.sem, at(routed, i, u, 1))
                    nc.vector.scalar_tensor_tensor(logit[:, half:], bank[:, half:, E:2 * E], UN, weight[:, half:],
                                                   ALU.mult, ALU.add).then_inc(dve_read.sem, 1)
                    for r, step in ((0, 4), (half, 7)):
                        for j in range(r, r + half):
                            nc.vector.max(top[:, j], logit[:, j]).then_inc(routed.sem, 1)
                        dve.wait_ge(dve_read.sem, at(dve_read, i, u, nth(USES, AT_R)))
                        dve.wait_ge(routed.sem, at(routed, i, u, step - 1))
                        nc.vector.tensor_tensor(chosen[:, r:r + half], logit[:, r:r + half],
                                                top[:, r:r + half, 1:2].broadcast_to([P, half, E]),
                                                ALU.is_ge).then_inc(routed.sem, 1)
                    dve.wait_ge(routed.sem, at(routed, i, u, 7))
                    nc.vector.tensor_tensor(logit[:], logit[:], top[:, :, 0:1].broadcast_to([P, TT, E]),
                                            ALU.subtract).then_inc(routed.sem, 1)
                elif stage == "gate":
                    dve.wait_ge(gate_exped.sem, at(gate_exped, i, u, 0))
                    nc.vector.tensor_tensor(weight[:], weight[:], chosen[:], ALU.mult).then_inc(routed.sem, 1)
                    dve.wait_ge(routed.sem, at(routed, i, u, 9))
                    nc.vector.reduce_sum(gsum[:], weight[:], AX.X).then_inc(routed.sem, 1)
                    dve.wait_ge(routed.sem, at(routed, i, u, 10))
                    nc.vector.reciprocal(gsum[:], gsum[:]).then_inc(routed.sem, 1)
                    dve.wait_ge(routed.sem, at(routed, i, u, 11))
                    wide = gsum[:].rearrange("p (j a) -> p j a", a=1).broadcast_to([P, TT, E])
                    nc.vector.tensor_tensor(gates[:], weight[:], wide, ALU.mult).then_inc(routed.sem, 1)
                    nc.vector.scalar_tensor_tensor(gates_un[p][:], weight[:], UN, wide, ALU.mult,
                                                   ALU.mult).then_inc(gated.sem, 1)

            def experts(i, u, f, kind, e, j):
                bank = fps[:, (u * NUNIT + f) % FB]
                q = u
                if kind == "hidden":
                    n = 2 * e + j
                    dve.wait_ge(gelu_done.sem, at(gelu_done, i, u, n))
                    if j == 0:
                        dve.wait_ge(f_ready.sem, at(f_ready, i, u, UNITS.index(("expert", e - 2, TT - 1)) if e >= 2
                                                    else UNITS.index(("expert", E + e - 2, TT - 1)) - NUNIT))
                    nc.vector.tensor_scalar(hT[:, 0, e % 2, j], hidden[:, n % 2], XS, None,
                                            ALU.mult).then_inc(h_hi.sem, 1)
                    dve.wait_ge(h_hi.sem, at(h_hi, i, u, n))
                    nc.vector.scalar_tensor_tensor(hT[:, 1, e % 2, j], hidden[:, n % 2], XS, hT[:, 0, e % 2, j],
                                                   ALU.mult, ALU.subtract).then_inc(h_lo.sem, 1)
                    return
                dve.wait_ge(f_ready.sem, at(f_ready, i, u, f))
                if kind == "bias":
                    nc.vector.tensor_tensor(x2[q][:, j], bank, x2[q][:, j], ALU.add).then_inc(added.sem, 1)
                else:
                    dve.wait_ge(added.sem, at(added, i, u, e * TT + j))
                    nc.vector.scalar_tensor_tensor(x2[q][:, j], bank, gates_un[q][:, j, e:e + 1], x2[q][:, j],
                                                   ALU.mult, ALU.add).then_inc(added.sem, 1)

            def finish(i, u):
                c = summed3, spread3, varied3, rooted3, normed3
                spreads(x2[u], stats3, agg3, rstd3, c, i, u, 0, added, E * TT)
                norm(x2[u], agg3, rstd3, c, i, u, 0)

            gated.lead(dve, made=1)
            run(dve, program(chain, experts, finish))

        @block.tensor
        def _(pe):
            lead(pe, (c_ready,), (f_ready,))

            def chain_bank(i, u, k):
                if k >= CB:
                    who = USES[k - CB]
                    c, n = (act_read if who == "act" else dve_read), nth(USES, k - CB)
                else:
                    who = USES[NUSE + k - CB]
                    c = act_read if who == "act" else dve_read
                    n = nth(USES, NUSE + k - CB) - c.per // 2
                pe.wait_ge(c.sem, at(c, i, u, n))
                return cps[:, (u * NUSE + k) % CB]

            def experts_bank(i, u, f):
                who = F_USES[f - FB]
                c = gelu_done if who == "act" else added
                n = nth(F_USES, (f - FB) % NUNIT) - (0 if f >= FB else c.per // 2)
                pe.wait_ge(c.sem, at(c, i, u, n))
                return fps[:, (u * NUNIT + f) % FB]

            def product(bank, lhs, rhs, tiles):
                steps = [(t, a, b) for t in range(tiles) for a, b in TERMS]
                for n, (t, a, b) in enumerate(steps):
                    last = nc.tensor.matmul(bank, lhs(a, t), rhs(b, t), start=(n == 0), stop=(n == len(steps) - 1))
                return last

            def chain(i, u, stage):
                p = parity(u)
                if stage in ("out", "out2"):
                    if stage == "out":
                        pe.wait_ge(oT_loaded, 16 * (chunk(i, u) + 1))
                        k0, w = AT_OUT, W["wout_p"]
                    else:
                        pe.wait_ge(dve_read.sem, at(dve_read, i, u, nth(USES, AT_O - 1)))
                        k0, w = AT_O, W["wo_p"]
                    for j in range(TT):
                        bank = chain_bank(i, u, k0 + j)
                        product(bank, lambda a, t: oT[:, a, t, j * P:(j + 1) * P], lambda b, t: w[b][:, t],
                                KT).then_inc(c_ready.sem, 1)
                elif stage in ("turn1", "turn2"):
                    k0, src, done = (AT_T1, x1, 0) if stage == "turn1" else (AT_T2, x2[p], TT)
                    for j in range(TT):
                        pe.wait_ge(normed.sem, at(normed, i, u, done + j))
                        bank = chain_bank(i, u, k0 + j)
                        for t in range(KT):
                            last = nc.tensor.transpose(bank[:, t * P:(t + 1) * P], src[:, j, t * P:(t + 1) * P], ident[:])
                        last.then_inc(c_ready.sem, 1)
                elif stage == "query":
                    pe.wait_ge(dve_read.sem, at(dve_read, i, u, nth(USES, AT_T1 + TT - 1)))
                    for o in range(KT):
                        bank = chain_bank(i, u, AT_Q + o)
                        product(bank, lambda a, t: W["wq_p"][a][:, t, o * P:(o + 1) * P], lambda b, t: x1T[:, b, t],
                                KT).then_inc(c_ready.sem, 1)
                elif stage.startswith("scores"):
                    j = int(stage[-1])
                    if j == 0:
                        pe.wait_ge(kv_loaded, 48 * (chunk(i, u) + 1))
                        pe.wait_ge(act_read.sem, at(act_read, i, u, KT - 1))
                    for g in range(NG):
                        bank = chain_bank(i, u, AT_S + j * NG + g)
                        nc.tensor.matmul(bank[:, 0:KS], xq[:, g, j * P:(j + 1) * P], keys[:, g], start=True,
                                         stop=True).then_inc(c_ready.sem, 1)
                elif stage.startswith("probs"):
                    g = int(stage[-1])
                    pe.wait_ge(probs_ready.sem, at(probs_ready, i, u, TT - 1))
                    for h in range(HG):
                        bank = chain_bank(i, u, AT_TURN[g] + h)
                        for j in range(TT):
                            last = nc.tensor.transpose(bank[0:S2, j * P:(j + 1) * P], soft[:, j, g * HG + h], ident[:])
                        last.then_inc(c_ready.sem, 1)
                elif stage.startswith("pv"):
                    g = int(stage[-1])
                    bank = chain_bank(i, u, AT_VAL[g])
                    pe.wait_ge(act_read.sem, at(act_read, i, u, nth(USES, AT_TURN[g] + HG - 1)))
                    for h in range(HG):
                        f = (g * HG + h) * DH
                        last = nc.tensor.matmul(bank[h * DH:(h + 1) * DH], vals[:, f:f + DH], turned(g)[:, h],
                                                start=True, stop=True)
                    last.then_inc(c_ready.sem, 1)
                elif stage == "route":
                    pe.wait_ge(dve_read.sem, at(dve_read, i, u, nth(USES, AT_T2 + TT - 1)))
                    bank = chain_bank(i, u, AT_R)
                    for j in range(TT):
                        last = product(bank[:, j * 2 * E:(j + 1) * 2 * E],
                                       lambda a, t: x2T[p][:, a, t, j * P:(j + 1) * P],
                                       lambda b, t: W["route_p"][b][:, t], KT)
                    last.then_inc(c_ready.sem, 1)
                elif stage == "gate":
                    pe.wait_ge(routed.sem, at(routed, i, u, 12))
                    bank = chain_bank(i, u, AT_G)
                    for j in range(TT):
                        last = nc.tensor.transpose(bank[0:E, j * P:(j + 1) * P], gates[:, j], ident[:])
                    last.then_inc(c_ready.sem, 1)

            def experts(i, u, f, kind, e, j):
                bank = experts_bank(i, u, f)
                if kind == "bias":
                    pe.wait_ge(act_read.sem, at(act_read, i, u, nth(USES, AT_G) - act_read.per // 2))
                    last = nc.tensor.matmul(bank, gT[u][:, j], W["b2_sb"][:], start=True, stop=True)
                elif kind == "hidden":
                    n = 2 * e + j
                    last = product(bank, lambda a, t: W["w1_p"][a][:, t, n * P:(n + 1) * P],
                                   lambda b, t: x2T[u][:, b, t], KT)
                else:
                    pe.wait_ge(h_lo.sem, at(h_lo, i, u, 2 * e + 1))
                    last = product(bank, lambda a, t: hT[:, a, e % 2, t, j * P:(j + 1) * P],
                                   lambda b, t: W["w2_p"][b][:, 2 * e + t], DE // P)
                last.then_inc(f_ready.sem, 1)

            def finish(i, u):
                pass

            run(pe, program(chain, experts, finish))


def layer(nc, x_rows, xT, ctxT, mask, wqkvT, woutT, bout, wq, bq, wk, bk, wv, bv, wo, bo, w1, b1, w2, b2, centroids,
          routeT, out):
    dram = lambda name, shape, dt: nc.dram_tensor(name, shape, dt).ap()
    q_parts, k_parts, o_parts = (dram(n, [2, D, N], F16) for n in ("q_parts", "k_parts", "o_parts"))
    v_rows = dram("v_rows", [N, D], F32)
    project_qkv(nc, xT, wqkvT, q_parts, k_parts, v_rows)
    self_attention(nc, q_parts, k_parts, v_rows, o_parts)
    second_half(nc, x_rows, o_parts, ctxT, mask, woutT, bout, wq, bq, wk, bk, wv, bv, wo, bo, w1, b1, w2, b2,
                centroids, routeT, out)


def second_half(nc, x_rows, o_parts, ctxT, mask, woutT, bout, wq, bq, wk, bk, wv, bv, wo, bo, w1, b1, w2, b2,
                centroids, routeT, out):
    dram = lambda name, shape, dt: nc.dram_tensor(name, shape, dt).ap()
    k_blocks, v_ctx = dram("k_blocks", [B, P, NG * HG * S2], F32), dram("v_ctx", [B, S2, D], F32)
    with ExitStack() as stack:
        W = {}

        def resident(name, shape, dt):
            W[name] = stack.enter_context(nc.sbuf_tensor(name, shape, dt))

        def parts(name, shape):
            W[name] = [stack.enter_context(nc.sbuf_tensor(f"{name}_{s}", shape, F16)) for s in ("hi", "lo")]

        for name in ("wout_p", "wq_p", "wo_p"):
            parts(name, [P, KT, D])
        parts("w1_p", [P, KT, E * DE])
        parts("w2_p", [P, FT, D])
        parts("route_p", [P, KT, 2 * E])
        resident("route_raw", [P, KT, 2 * E], F32)
        resident("work", [P, 2, TT * D], F32)
        resident("ident", [P, P], F32)
        resident("power", [P, H], F32)
        resident("oT", [P, 2, KT, CH], F16)
        resident("x1", [P, TT, D], F32)
        resident("soft", [P, TT, H, S2], F32)
        resident("hidden", [P, 2, CH], F32)
        resident("hT", [P, 2, 2, 2, CH], F16)
        resident("bout_bc", [P, D], F32)
        resident("bo_bc", [P, D], F32)
        resident("bq_sb", [P, KT], F32)
        resident("b1_sb", [P, FT], F32)
        resident("b2_sb", [E, D], F32)
        flat = lambda a: a.rearrange("(t p) n -> p t n", p=P)
        cols = lambda t: t.rearrange("p t n -> p (t n)")
        weights = []
        for name, src in (("wout_p", woutT), ("wq_p", wq), ("wo_p", wo)):
            weights.append((flat(src), [cols(part[:]) for part in W[name]]))
        for t in range(KT):
            weights.append((w1[:, t * P:(t + 1) * P, :].rearrange("e p h -> p e h"),
                            [part[:, t] for part in W["w1_p"]]))
        for n in range(FT // KT):
            weights.append((w2.rearrange("e (t p) n -> p (e t) n", p=P)[:, n * KT:(n + 1) * KT],
                            [cols(part[:, n * KT:(n + 1) * KT]) for part in W["w2_p"]]))
        prepare(nc, W, ctxT, flat(wk), bk, flat(wv), bv, weights, centroids, routeT, bout, bo, bq, b1, b2, k_blocks,
                v_ctx)
        for name in ("x2", "x2T"):
            shape, dt = ([P, TT, D], F32) if name == "x2" else ([P, 2, KT, CH], F16)
            W[name] = [stack.enter_context(nc.sbuf_tensor(f"{name}_{a}", shape, dt)) for a in range(2)]
        chains(nc, W, x_rows, o_parts, mask, k_blocks, v_ctx, out)


_INPUTS = ["x", "ctx_1024", "mask_Bx1x1xS2_ff0", "L0_attn_Wqkv", "L0_attn_Wout", "L0_attn_bout", "L0_xattn_Wq",
           "L0_xattn_bq", "L0_xattn_Wk", "L0_xattn_bk", "L0_xattn_Wv", "L0_xattn_bv", "L0_xattn_Wo", "L0_xattn_bo",
           "L0_ffn_w1", "L0_ffn_b1", "L0_ffn_w2", "L0_ffn_b2", "L0_ffn_centroids", "L0_ffn_w_route"]


def kernel(**inputs):
    import numpy as np
    import concourse.bacc as bacc
    from concourse.bass_utils import run_bass_kernel_spmd

    a = {k: np.asarray(inputs[k]) for k in _INPUTS}
    arrays = {
        "x_rows": a["x"].reshape(N, D), "xT": a["x"].reshape(N, D).T, "ctxT": a["ctx_1024"].reshape(B * S2, D).T,
        "mask": a["mask_Bx1x1xS2_ff0"], "wqkvT": a["L0_attn_Wqkv"].T, "woutT": a["L0_attn_Wout"].T,
        "bout": a["L0_attn_bout"], "wq": a["L0_xattn_Wq"], "bq": a["L0_xattn_bq"].reshape(KT, P).T,
        "wk": a["L0_xattn_Wk"], "bk": a["L0_xattn_bk"].reshape(KT, P).T, "wv": a["L0_xattn_Wv"], "bv": a["L0_xattn_bv"], "wo": a["L0_xattn_Wo"],
        "bo": a["L0_xattn_bo"], "w1": a["L0_ffn_w1"], "b1": a["L0_ffn_b1"].reshape(FT, P).T, "w2": a["L0_ffn_w2"],
        "b2": a["L0_ffn_b2"], "centroids": a["L0_ffn_centroids"], "routeT": a["L0_ffn_w_route"].T,
    }
    arrays = {k: np.ascontiguousarray(v) for k, v in arrays.items()}
    nc = bacc.Bacc("TRN2", target_bir_lowering=False, num_devices=1)
    handles = {k: nc.dram_tensor(f"{k}_in", v.shape, F32, kind="ExternalInput").ap() for k, v in arrays.items()}
    out = nc.dram_tensor("out", [N, D], F32, kind="ExternalOutput").ap()
    layer(nc, out=out, **handles)
    r = run_bass_kernel_spmd(nc, [{f"{k}_in": v for k, v in arrays.items()}], core_ids=[0])
    return r.results[0]["out"].reshape(B, T, D)
```

```python
from contextlib import ExitStack

import concourse.bass as bass
from concourse import mybir

F32, F16, BF16 = mybir.dt.float32, mybir.dt.float16, mybir.dt.bfloat16
ALU, ACT, AX = mybir.AluOpType, mybir.ActivationFunctionType, mybir.AxisListType

B, T, D, H, DH = 2, 2048, 512, 16, 32
S2 = 77
E, DE = 8, 256
N = B * T
P = 128
KT = D // P
HG = P // DH
NG = H // HG
CH = 512
NC = N // CH
CPB = T // CH
TT = CH // P
FT = E * DE // P
EPS = 1e-5
NEG = -1e9

XS = 32.0
WS = 512.0
UN = 1.0 / (XS * WS)
QK = XS * XS
MASKED = -1e30
TERMS = ((0, 0), (1, 0), (0, 1))


class Count:

    def __init__(self, nc, stack, name, per):
        self.sem, self.per = stack.enter_context(nc.semaphore(name)), per

    def lead(self, engine, made=0):
        engine.sem_inc(self.sem, self.per - made)

    def at(self, lap, k):
        return (lap + 1) * self.per + k + 1


def sems(nc, stack, name, n):
    return [stack.enter_context(nc.semaphore(f"{name}{s}")) for s in range(n)]


def project_qkv(nc, xT, wqkvT, q_parts, k_parts, v_rows):
    NU = 2
    LAPS = NC // NU
    OT = 2 * KT
    PER = OT + TT
    NB, NQ, NV = 8, 4, 2
    QL, VL = NU * OT // NQ, NU * TT // NV
    with ExitStack() as stack:
        sb = lambda *a: stack.enter_context(nc.sbuf_tensor(*a))
        w_raw = sb("w_raw", [P, KT, 3 * D], F32)
        w_parts = sb("w_hi", [P, KT, 3 * D], F16), sb("w_lo", [P, KT, 3 * D], F16)
        x_raw = sb("x_raw", [P, NU, KT, CH], F32)
        x_parts = sb("x_hi", [P, NU, KT, CH], F16), sb("x_lo", [P, NU, KT, CH], F16)
        qk_out = sb("qk_out", [P, NQ, 2, CH], F16)
        v_out = sb("v_out", [P, NV, D], F32)
        prod = stack.enter_context(nc.psum_tensor("prod", [P, NB, CH], F32))
        w_loaded = sems(nc, stack, "w_loaded", 3)
        w_hi_ready, w_lo_ready = (stack.enter_context(nc.semaphore(s)) for s in ("w_hi_ready", "w_lo_ready"))
        x_loaded = sems(nc, stack, "x_loaded", NU)
        qk_stored, v_stored = sems(nc, stack, "qk_stored", NQ), sems(nc, stack, "v_stored", NV)
        x_hi_ready = Count(nc, stack, "x_hi_ready", NU)
        x_lo_ready = Count(nc, stack, "x_lo_ready", NU)
        prod_ready = Count(nc, stack, "prod_ready", NU * PER)
        hi_ready = Count(nc, stack, "hi_ready", NU * OT)
        prod_read = Count(nc, stack, "prod_read", NU * PER)
        block = stack.enter_context(nc.Block())

        @block.sync
        def _(sp):
            def load(i, u):
                sp.wait_ge(x_lo_ready.sem, x_lo_ready.at(i, u - NU))
                sp.dma_start(x_raw[:, u], xT[:, bass.ds((NU * i + u) * CH, CH)].rearrange(
                    "(t p) n -> p t n", p=P)).then_inc(x_loaded[u], 16)

            def store(i, u):
                at = (NU * i + u) * CH
                for o in range(OT):
                    sp.wait_ge(prod_read.sem, prod_read.at(i, u * PER + o))
                    parts = q_parts if o < KT else k_parts
                    f = (o % KT) * P
                    sp.dma_start(parts[:, f:f + P, bass.ds(at, CH)].rearrange("s p n -> p s n"),
                                 qk_out[:, o % NQ]).then_inc(qk_stored[o % NQ], 16)
                for j in range(TT):
                    sp.wait_ge(prod_read.sem, prod_read.at(i, u * PER + OT + j))
                    sp.dma_start(v_rows[bass.ds(at + j * P, P), :], v_out[:, j % NV]).then_inc(v_stored[j % NV], 16)

            for n in range(3):
                cols = slice(n * D, (n + 1) * D)
                sp.dma_start(w_raw[:, :, cols], wqkvT[:, cols].rearrange("(t p) n -> p t n", p=P)).then_inc(w_loaded[n], 16)
                if n < NU:
                    load(0, n)
            with sp.Fori(0, LAPS - 1) as i:
                for u in range(NU):
                    store(i, u)
                    load(i + 1, u)
            for u in range(NU):
                store(LAPS - 1, u)
            for s in qk_stored:
                sp.wait_ge(s, 16 * QL * LAPS)
            for s in v_stored:
                sp.wait_ge(s, 16 * VL * LAPS)

        @block.scalar
        def _(act):
            x_hi_ready.lead(act)
            hi_ready.lead(act)

            def weights(n):
                act.wait_ge(w_loaded[n], 16)
                cols = slice(n * D, (n + 1) * D)
                nc.scalar.activation(w_parts[0][:, :, cols], w_raw[:, :, cols], ACT.Copy, scale=WS).then_inc(w_hi_ready, 1)

            def x_hi(i, u):
                act.wait_ge(x_loaded[u % NU], 16 * (i + u // NU) + 16)
                act.wait_ge(prod_ready.sem, prod_ready.at(i, (u - NU) * PER + PER - 1))
                nc.scalar.activation(x_parts[0][:, u % NU], x_raw[:, u % NU], ACT.Copy, scale=XS).then_inc(x_hi_ready.sem, 1)

            def chunk(i, u, last):
                for o in range(OT):
                    k = u * PER + o
                    act.wait_ge(prod_ready.sem, prod_ready.at(i, k))
                    act.wait_ge(qk_stored[o % NQ], 16 * (QL * i + (u * OT + o) // NQ))
                    nc.scalar.activation(qk_out[:, o % NQ, 0], prod[:, k % NB], ACT.Copy,
                                         scale=UN * XS).then_inc(hi_ready.sem, 1)
                    if o == OT // 2 - 1 and not last:
                        x_hi(i, u + 1)

            weights(0)
            x_hi(0, 0)
            weights(1)
            weights(2)
            with act.Fori(0, LAPS - 1) as i:
                for u in range(NU):
                    chunk(i, u, False)
            for u in range(NU):
                chunk(LAPS - 1, u, u == NU - 1)

        @block.vector
        def _(dve):
            x_lo_ready.lead(dve)
            prod_read.lead(dve)

            def weights(n):
                dve.wait_ge(w_hi_ready, n + 1)
                cols = slice(n * D, (n + 1) * D)
                nc.vector.scalar_tensor_tensor(w_parts[1][:, :, cols], w_raw[:, :, cols], WS, w_parts[0][:, :, cols],
                                               ALU.mult, ALU.subtract).then_inc(w_lo_ready, 1)

            def x_lo(i, u):
                dve.wait_ge(x_hi_ready.sem, x_hi_ready.at(i, u))
                nc.vector.scalar_tensor_tensor(x_parts[1][:, u % NU], x_raw[:, u % NU], XS, x_parts[0][:, u % NU],
                                               ALU.mult, ALU.subtract).then_inc(x_lo_ready.sem, 1)

            def chunk(i, u, last):
                for o in range(OT):
                    k = u * PER + o
                    dve.wait_ge(hi_ready.sem, hi_ready.at(i, u * OT + o))
                    nc.vector.scalar_tensor_tensor(qk_out[:, o % NQ, 1], prod[:, k % NB], UN * XS,
                                                   qk_out[:, o % NQ, 0], ALU.mult,
                                                   ALU.subtract).then_inc(prod_read.sem, 1)
                    if o == OT // 2 and not last:
                        x_lo(i, u + 1)
                for j in range(TT):
                    k = u * PER + OT + j
                    dve.wait_ge(prod_ready.sem, prod_ready.at(i, k))
                    dve.wait_ge(v_stored[j % NV], 16 * (VL * i + (u * TT + j) // NV))
                    nc.vector.tensor_scalar(v_out[:, j % NV], prod[:, k % NB], UN, None,
                                            ALU.mult).then_inc(prod_read.sem, 1)

            weights(0)
            x_lo(0, 0)
            weights(1)
            weights(2)
            with dve.Fori(0, LAPS - 1) as i:
                for u in range(NU):
                    chunk(i, u, False)
            for u in range(NU):
                chunk(LAPS - 1, u, u == NU - 1)

        @block.tensor
        def _(pe):
            prod_ready.lead(pe)
            with pe.Fori(0, LAPS) as i:
                for u in range(NU):
                    pe.wait_ge(x_lo_ready.sem, x_lo_ready.at(i, u))
                    for m in range(PER):
                        k = u * PER + m
                        if m % KT == 0:
                            pe.wait_ge(w_lo_ready, m // KT + 1)
                        pe.wait_ge(prod_read.sem, prod_read.at(i, k - NB))
                        for s, (t, (a, b)) in enumerate((t, ab) for t in range(KT) for ab in TERMS):
                            if m < OT:
                                lhs, rhs = w_parts[a][:, t, m * P:(m + 1) * P], x_parts[b][:, u, t]
                            else:
                                j = m - OT
                                lhs, rhs = x_parts[a][:, u, t, j * P:(j + 1) * P], w_parts[b][:, t, 2 * D:3 * D]
                            last = nc.tensor.matmul(prod[:, k % NB], lhs, rhs, start=(s == 0), stop=(s == 3 * KT - 1))
                        last.then_inc(prod_ready.sem, 1)


def self_attention(nc, q_parts, k_parts, v_rows, o_parts):
    NR = 3 * DH
    NM = NR + 2
    GROUPS = B * NG
    LAPS = GROUPS // 2
    KU = [(c, kt) for c in range(CPB) for kt in range((c + 1) * TT)]
    VU = [(c, kt, h) for c, kt in KU for h in range(HG)]
    AUX = []
    for c in range(CPB):
        AUX += [("max", c, (j, h, s)) for j in range(TT) for h in range(HG) for s in range(c + 1)] + [("rows", c, None)]
    NKU, NVU, NAUX = len(KU), len(VU), len(AUX)
    POOLED = [[n for n, (k, kt) in enumerate(KU) if k == c and kt < c * TT and kt % 3 != 2]
              for c in range(CPB)]
    ADDS = [n for tiles in POOLED for n in tiles[1:]]
    NP = 8
    RING = 3
    PIECES = 4
    VALUES, SUMS = 4, 6
    TAKEN = VALUES + 1, SUMS + 1
    RECIPS = [SUMS + 3 + 2 * n for n in range(PIECES)]
    SCALED = RECIPS[-1] + 1
    STORED = SCALED + 4
    TAIL = STORED + 1
    READY = 6
    SCALE = DH ** -0.5 / QK
    LAST_TILE = [max(n for n, k in enumerate(KU) if k[0] == c) for c in range(CPB)]
    CHUNK_OF = {t: c for c, t in enumerate(LAST_TILE)}

    def schedule():
        off = lambda c, kt: max(kt - c * TT, 0) * P
        steps = [0.06 + 0.6 * (CH - off(c, kt)) / CH for c, kt, _ in VU]
        busy = [0.0] * NVU
        for t in LAST_TILE:
            for lag in RECIPS:
                busy[(t * HG + HG - 1 + lag) % NVU] += 0.85
        cost = []
        for what, c, unit in AUX:
            if what == "rows":
                cost.append(2.4)
            else:
                j, _, s = unit
                cost.append(0.06 + 0.53 * (1.0 if s < c else (j + 1) / TT))
        rate = (sum(cost) + sum(busy)) / sum(steps)
        ends = [sum(cost[:n + 1]) for n in range(NAUX)]
        spent = [sum(rate * a - b for a, b in zip(steps[:u], busy[:u])) for u in range(NVU + 1)]

        def done(u, lead):
            t = spent[u % NVU] + lead + (u // NVU) * ends[-1]
            laps, rest = divmod(t, ends[-1])
            return int(laps) * NAUX + sum(e <= rest + 1e-9 for e in ends)

        lead = 0.0
        starts = [min(n for n, v in enumerate(VU) if v[0] == c) for c in range(CPB)]
        turns = [n for n, x in enumerate(AUX) if x[0] == "rows"]
        while any(done(starts[c] - READY, lead) <= turns[c] for c in range(CPB)):
            lead += 0.2
        most = 0
        out = []
        for u in range(NVU + 1):
            most = max(most, done(u, lead))
            out.append(most)
        out[NVU] = out[0] + NAUX
        return out

    DONE = schedule()

    def done_by(p):
        return DONE[p % NVU] + p // NVU * NAUX

    def before(n, ring, per):
        k = n % per
        return n - ring if k >= ring else n - k - 1 - (per - 1 - k) % ring

    def adds_upto(k):
        return k // NKU * len(ADDS) + sum(
            max(sum(n <= k % NKU for n in tiles[1:]), tiles[0] <= k % NKU) for tiles in POOLED if tiles)

    def laps(engine, step):
        for s in range(TAIL):
            step(0, s, 0, None)
        with engine.Fori(0, LAPS - 1) as i:
            for s in range(TAIL, TAIL + 2 * NVU):
                step(i, s, None, None)
        for s in range(TAIL, TAIL + 2 * NVU):
            step(LAPS - 1, s, None, 2 * NVU)

    def unit_at(s, lag, first, end):
        p = s - lag
        return None if (first is not None and p < first) or (end is not None and p >= end) else p

    def tile_at(s, lag, first, end):
        p = unit_at(s, lag, first, end)
        return p // HG if p is not None and p % HG == HG - 1 else None

    def chunk_at(s, lag, first, end):
        k = tile_at(s, lag, first, end)
        return k // NKU * CPB + CHUNK_OF[k % NKU] if k is not None and k % NKU in CHUNK_OF else None

    def aux_at(s, end):
        return [n for n in range(done_by(s), done_by(s + 1)) if end is None or n < 2 * NAUX]

    with ExitStack() as stack:
        sb = lambda *a: stack.enter_context(nc.sbuf_tensor(*a))
        ps = lambda *a: stack.enter_context(nc.psum_tensor(*a))
        q_pair = [sb(f"q_pair{a}", [NM, HG, T], F16) for a in range(2)]
        k_pair = [sb(f"k_pair{a}", [NM, HG, T], F16) for a in range(2)]
        v_sb = [sb(f"v_sb{a}", [P, T // P, P], F32) for a in range(2)]
        probs = sb("probs", [P, NP, HG, CH], F32)
        total = sb("total", [P, HG, CH], F32)
        ones = sb("ones", [P, DH], F32)
        ident_f = sb("ident_f", [P, P], F32)
        ident = sb("ident_bf", [P, P], BF16)
        ident16 = sb("ident16", [P, P], F16)
        future_f = sb("future_f", [P, 2, P], F32)
        future = sb("future", [P, 2, P], BF16)
        seg_max = sb("seg_max", [P, HG, TT, CPB], F32)
        row_max = sb("row_max", [P, HG, TT], F32)
        max_parts = sb("max_parts", [P, 2, HG, TT], F16)
        max_rows = sb("max_rows", [2 * HG, 2, CH], F16)
        o_raw = sb("o_raw", [P, CH], F32)
        den = sb("den", [P, CH], F32)
        o_sb = sb("o_sb", [P, CH], F32)
        o_out = sb("o_out", [P, 2, 2, CH], F16)
        st_ps = ps("st_ps", [P, RING, CH], F32)
        s_ps = ps("s_ps", [P, RING, CH], F32)
        o_ps = ps("o_ps", [P, CH], F32)
        den_ps = ps("den_ps", [P, CH], F32)
        made, const_ready, factors_ready = (stack.enter_context(nc.semaphore(s)) for s in
                                            ("made", "const_ready", "factors_ready"))
        qk_loaded = [sems(nc, stack, f"qk_loaded{a}_", CPB) for a in range(2)]
        v_loaded = sems(nc, stack, "v_loaded", 2)
        o_stored = sems(nc, stack, "o_stored", 2)
        rows_moved = sems(nc, stack, "rows_moved", 2)
        st_ready = Count(nc, stack, "st_ready", 2 * NVU)
        exp_done = Count(nc, stack, "exp_done", 2 * NVU)
        pv_done = Count(nc, stack, "pv_done", 2 * NKU)
        o_ready = Count(nc, stack, "o_ready", 2 * CPB)
        o_taken = Count(nc, stack, "o_taken", 2 * CPB)
        den_taken = Count(nc, stack, "den_taken", 2 * CPB)
        added = Count(nc, stack, "added", 2 * len(ADDS))
        s_ready = Count(nc, stack, "s_ready", 2 * NAUX)
        s_read = Count(nc, stack, "s_read", 2 * NAUX)
        max_ready = Count(nc, stack, "max_ready", 2 * CPB)
        steps = Count(nc, stack, "steps", 2 * 2 * CPB)
        recips = Count(nc, stack, "recips", 2 * CPB * PIECES)
        scaled = Count(nc, stack, "scaled", 2 * CPB)
        o_hi_done = Count(nc, stack, "o_hi_done", 2 * CPB)
        split_done = Count(nc, stack, "split_done", 2 * CPB)
        block = stack.enter_context(nc.Block())

        def rows_at(k):
            return 16 * (k // 2 + 1)

        @block.gpsimd
        def _(pool):
            nc.gpsimd.memset(ones[:], 1.0).then_inc(made, 1)
            nc.gpsimd.memset(ident_f[:], 0.0).then_inc(made, 1)
            nc.gpsimd.memset(future_f[:], 0.0).then_inc(made, 1)
            pool.wait_ge(made, 3)
            nc.gpsimd.affine_select(out=ident_f[:], in_=ident_f[:], compare_op=ALU.not_equal, fill=1.0, base=0,
                                    pattern=[[-1, P]], channel_multiplier=1).then_inc(made, 1)
            for n, sign in enumerate((1, -1)):
                nc.gpsimd.affine_select(out=future_f[:, n], in_=future_f[:, n], compare_op=ALU.is_ge, fill=MASKED,
                                        base=0, pattern=[[-sign, P]], channel_multiplier=sign).then_inc(made, 1)
            pool.wait_ge(made, 6)
            nc.gpsimd.tensor_copy(ident[:], ident_f[:]).then_inc(const_ready, 1)
            nc.gpsimd.tensor_copy(ident16[:], ident_f[:]).then_inc(const_ready, 1)
            nc.gpsimd.tensor_copy(future[:], future_f[:]).then_inc(const_ready, 1)
            pool.wait_ge(const_ready, 3)
            nc.gpsimd.memset(k_pair[0][NR:NM], QK).then_inc(factors_ready, 1)
            pool.wait_ge(factors_ready, 1)
            nc.gpsimd.memset(k_pair[1][NR:NM], QK).then_inc(factors_ready, 1)
            pool.wait_ge(factors_ready, 2)
            added.lead(pool)
            scaled.lead(pool)
            split_done.lead(pool)

            def step(i, s, first, end):
                k = tile_at(s, 1, first, end)
                if k is not None and k % NKU in ADDS:
                    c, n = KU[k % NKU][0], adds_upto(k) - 1
                    starts = k % NKU == POOLED[c][1]
                    pool.wait_ge(exp_done.sem, exp_done.at(i, HG * k + HG - 1))
                    if starts:
                        pool.wait_ge(pv_done.sem, pv_done.at(i, k // NKU * NKU + LAST_TILE[c - 1]))
                        other = probs[:, (k // NKU * NKU + POOLED[c][0]) % NP]
                    else:
                        pool.wait_ge(added.sem, added.at(i, n - 1))
                        other = total[:]
                    nc.gpsimd.tensor_tensor(total[:], other, probs[:, k % NP], ALU.add).then_inc(added.sem, 1)
                c = chunk_at(s, SCALED, first, end)
                if c is not None:
                    pool.wait_ge(recips.sem, recips.at(i, c * PIECES + PIECES - 1))
                    pool.wait_ge(split_done.sem, split_done.at(i, c - 1))
                    nc.gpsimd.tensor_tensor(o_sb[:], o_raw[:], den[:], ALU.mult).then_inc(scaled.sem, 1)
                c = chunk_at(s, SCALED + 3, first, end)
                if c is not None:
                    pool.wait_ge(o_hi_done.sem, o_hi_done.at(i, c))
                    nc.gpsimd.tensor_tensor(o_out[:, c % 2, 1], o_sb[:], o_out[:, c % 2, 0],
                                            ALU.subtract).then_inc(split_done.sem, 1)

            laps(pool, step)

        @block.sync
        def _(sp):
            def load(g, a, c):
                b, f = g // NG, (g % NG) * P
                cols = bass.ds(b * T + c * CH, CH)
                for pair, parts, order in ((k_pair[a], k_parts, (0, 0, 1)), (q_pair[a], q_parts, (0, 1, 0))):
                    for r, part in enumerate(order):
                        sp.dma_start(pair[r * DH:(r + 1) * DH, :, c * CH:(c + 1) * CH],
                                     parts[part, bass.ds(f, P), cols].rearrange("(h p) n -> p h n", p=DH)).then_inc(
                                         qk_loaded[a][c], 16)
                if c == CPB - 1:
                    sp.dma_start(v_sb[a][:], v_rows[bass.ds(b * T, T), bass.ds(f, P)].rearrange(
                        "(t p) f -> p t f", p=P)).then_inc(v_loaded[a], 16)

            def turn(i, n):
                c = n // NAUX * CPB + AUX[n % NAUX][1]
                sp.wait_ge(s_read.sem, s_read.at(i, n))
                at = c % CPB * CH
                for part in range(2):
                    sp.dma_start(q_pair[c // CPB % 2][NR + part:NR + part + 1, :, at:at + CH],
                                 max_rows[part * HG:(part + 1) * HG, c % 2]).then_inc(rows_moved[c % 2], 16)

            def step(i, s, first, end):
                for n in aux_at(s, end):
                    if AUX[n % NAUX][0] == "rows":
                        turn(i, n)
                k = tile_at(s, SUMS, first, end)
                if k is not None and k % NKU == NKU - 1 and end is None:
                    sp.wait_ge(pv_done.sem, pv_done.at(i, k))
                    for c in range(CPB):
                        load(2 * i + k // NKU + 2, k // NKU % 2, c)
                c = chunk_at(s, STORED, first, end)
                if c is not None:
                    sp.wait_ge(split_done.sem, split_done.at(i, c))
                    g = 2 * i + c // CPB
                    b, f = g // NG, (g % NG) * P
                    sp.dma_start(o_parts[:, bass.ds(f, P), bass.ds(b * T + c % CPB * CH, CH)].rearrange(
                        "s p n -> p s n"), o_out[:, c % 2]).then_inc(o_stored[c % 2], 16)

            for a in range(2):
                for c in range(CPB):
                    load(a, a, c)
            for n in range(done_by(0)):
                if AUX[n][0] == "rows":
                    turn(0, n)
            laps(sp, step)
            for a in range(2):
                sp.wait_ge(o_stored[a], 16 * CPB * LAPS)
                sp.wait_ge(rows_moved[a], 2 * 16 * CPB * LAPS)

        @block.scalar
        def _(act):
            exp_done.lead(act)
            o_taken.lead(act)
            den_taken.lead(act)

            def step(i, s, first, end):
                p = unit_at(s, 0, first, end)
                if p is not None:
                    c, kt, h = VU[p % NVU]
                    off = max(kt - c * TT, 0) * P
                    k = p // HG
                    act.wait_ge(st_ready.sem, st_ready.at(i, p))
                    if h == 0:
                        act.wait_ge(pv_done.sem, pv_done.at(i, k - NP))
                        act.wait_ge(added.sem, added.at(i, adds_upto(k - NP) - 1))
                    nc.scalar.activation(probs[:, k % NP, h, off:], st_ps[:, p % (2 * NVU) % RING, off:], ACT.Exp,
                                         scale=SCALE).then_inc(exp_done.sem, 1)
                c = chunk_at(s, TAKEN[0], first, end)
                if c is not None:
                    act.wait_ge(o_ready.sem, o_ready.at(i, c))
                    act.wait_ge(scaled.sem, scaled.at(i, c - 1))
                    nc.scalar.activation(o_raw[:], o_ps[:], ACT.Copy).then_inc(o_taken.sem, 1)
                c = chunk_at(s, TAKEN[1], first, end)
                if c is not None:
                    act.wait_ge(pv_done.sem, pv_done.at(i, c // CPB * NKU + LAST_TILE[c % CPB]))
                    nc.scalar.activation(den[:], den_ps[:], ACT.Copy, scale=1.0 / XS).then_inc(den_taken.sem, 1)

            laps(act, step)

        @block.vector
        def _(dve):
            for count in (s_read, max_ready, steps, recips, o_hi_done):
                count.lead(dve)

            def aux(i, n):
                what, c, unit = AUX[n % NAUX]
                slot = n % (2 * NAUX) % RING
                k = n // NAUX * CPB + c
                dve.wait_ge(s_ready.sem, s_ready.at(i, n))
                if what == "rows":
                    dve.wait_ge(rows_moved[k % 2], 2 * 16 * (CPB * i + k // 2))
                    nc.vector.tensor_copy(max_rows[:, k % 2], s_ps[0:2 * HG, slot]).then_inc(s_read.sem, 1)
                    return
                j, h, s = unit
                width = CH if s < c else (j + 1) * P
                nc.vector.reduce_max(seg_max[:, h, j, s:s + 1], s_ps[:, slot, 0:width], AX.X).then_inc(s_read.sem, 1)
                if AUX[(n + 1) % NAUX][0] == "rows":
                    dve.wait_ge(s_read.sem, s_read.at(i, n))
                    nc.vector.reduce_max(row_max[:], seg_max[:, :, :, 0:c + 1], AX.X).then_inc(steps.sem, 1)
                    dve.wait_ge(steps.sem, steps.at(i, 2 * k))
                    nc.vector.tensor_scalar(max_parts[:, 0], row_max[:], -1.0 / QK, None, ALU.mult).then_inc(steps.sem, 1)
                    dve.wait_ge(steps.sem, steps.at(i, 2 * k + 1))
                    nc.vector.scalar_tensor_tensor(max_parts[:, 1], row_max[:], -1.0 / QK, max_parts[:, 0], ALU.mult,
                                                   ALU.subtract).then_inc(max_ready.sem, 1)

            def step(i, s, first, end):
                for n in aux_at(s, end):
                    aux(i, n)
                for n, lag in enumerate(RECIPS):
                    c = chunk_at(s, lag, first, end)
                    if c is not None:
                        if n == 0:
                            dve.wait_ge(den_taken.sem, den_taken.at(i, c))
                        piece = den[:, n * CH // PIECES:(n + 1) * CH // PIECES]
                        nc.vector.reciprocal(piece, piece).then_inc(recips.sem, 1)
                c = chunk_at(s, SCALED + 2, first, end)
                if c is not None:
                    dve.wait_ge(scaled.sem, scaled.at(i, c))
                    dve.wait_ge(o_stored[c % 2], 16 * (CPB * i + c // 2))
                    nc.vector.tensor_copy(o_out[:, c % 2, 0], o_sb[:]).then_inc(o_hi_done.sem, 1)

            for n in range(done_by(0)):
                aux(0, n)
            laps(dve, step)

        @block.tensor
        def _(pe):
            for count in (st_ready, pv_done, o_ready, s_ready):
                count.lead(pe)

            def aux(i, n):
                what, c, unit = AUX[n % NAUX]
                k = n // NAUX * CPB + c
                slot, a = n % (2 * NAUX) % RING, k // CPB % 2
                pe.wait_ge(s_read.sem, s_read.at(i, before(n, RING, 2 * NAUX)))
                if what == "rows":
                    pe.wait_ge(max_ready.sem, max_ready.at(i, k))
                    for j in range(TT):
                        last = nc.tensor.matmul(s_ps[0:2 * HG, slot, j * P:(j + 1) * P], max_parts[:, :, :, j],
                                                ident16[:], start=(j == 0), stop=(j == TT - 1), skip_group_check=True)
                    last.then_inc(s_ready.sem, 1)
                    return
                j, h, s = unit
                if j == h == s == 0:
                    pe.wait_ge(qk_loaded[a][c], 6 * 16 * (i + k // (2 * CPB) + 1))
                width = CH if s < c else (j + 1) * P
                q0 = c * CH + j * P
                diagonal = s == c
                last = nc.tensor.matmul(s_ps[:, slot, 0:width], q_pair[a][0:NR, h, q0:q0 + P],
                                        k_pair[a][0:NR, h, s * CH:s * CH + width], start=True, stop=not diagonal)
                if diagonal:
                    last = nc.tensor.matmul(s_ps[:, slot, width - P:width], ident[:], future[:, 0],
                                            start=False, stop=True)
                last.then_inc(s_ready.sem, 1)

            def scores(i, p):
                c, kt, h = VU[p % NVU]
                a, slot = p // NVU % 2, p % (2 * NVU) % RING
                if kt == h == 0:
                    k = p // NVU * CPB + c
                    pe.wait_ge(rows_moved[k % 2], 2 * 16 * (CPB * i + k // 2 + 1))
                off = max(kt - c * TT, 0) * P
                pe.wait_ge(exp_done.sem, exp_done.at(i, before(p, RING, 2 * NVU)))
                diagonal = kt >= c * TT
                last = nc.tensor.matmul(st_ps[:, slot, off:], k_pair[a][:, h, kt * P:(kt + 1) * P],
                                        q_pair[a][:, h, c * CH + off:(c + 1) * CH], start=True, stop=not diagonal)
                if diagonal:
                    last = nc.tensor.matmul(st_ps[:, slot, off:off + P], ident[:], future[:, 1], start=False, stop=True)
                last.then_inc(st_ready.sem, 1)

            heads = [slice(h * DH, (h + 1) * DH) for h in range(HG)]

            def values(i, k):
                c, kt = KU[k % NKU]
                a, off = k // NKU % 2, max(kt - c * TT, 0) * P
                final = k % NKU == LAST_TILE[c]
                if kt == 0:
                    if c == 0:
                        pe.wait_ge(v_loaded[a], 16 * (i + k // (2 * NKU) + 1))
                    pe.wait_ge(o_taken.sem, o_taken.at(i, k // NKU * CPB + c - 1))
                pe.wait_ge(exp_done.sem, exp_done.at(i, HG * k + HG - 1))
                for h, out in enumerate(heads):
                    last = nc.tensor.matmul(o_ps[out, off:], v_sb[a][:, kt, out], probs[:, k % NP, h, off:],
                                            start=(kt == 0), stop=final)
                if k % NKU in POOLED[c]:
                    last.then_inc(pv_done.sem, 1)
                elif final:
                    last.then_inc(o_ready.sem, 1)

            def sums(i, k):
                c, kt = KU[k % NKU]
                off, pooled = max(kt - c * TT, 0) * P, POOLED[c]
                final = k % NKU == LAST_TILE[c]
                if k % NKU in pooled:
                    return
                opens = all(n in pooled for n, (x, _) in enumerate(KU) if x == c and n < k % NKU)
                if opens:
                    pe.wait_ge(den_taken.sem, den_taken.at(i, k // NKU * CPB + c - 1))
                for h, out in enumerate(heads):
                    last = nc.tensor.matmul(den_ps[out, off:], ones[:], probs[:, k % NP, h, off:], start=opens,
                                            stop=final and not pooled)
                if final and pooled:
                    pe.wait_ge(added.sem, added.at(i, adds_upto(k) - 1))
                    for h, out in enumerate(heads):
                        last = nc.tensor.matmul(den_ps[out, :], ones[:], total[:, h], start=False, stop=True)
                last.then_inc(pv_done.sem, 1)

            def step(i, s, first, end):
                p = unit_at(s, 0, first, end)
                if p is not None:
                    scores(i, p)
                todo = aux_at(s, end)
                for n in todo[:1]:
                    aux(i, n)
                k = tile_at(s, VALUES, first, end)
                if k is not None:
                    values(i, k)
                k = tile_at(s, SUMS, first, end)
                if k is not None:
                    sums(i, k)
                for n in todo[1:]:
                    aux(i, n)

            pe.wait_ge(const_ready, 3)
            for n in range(done_by(0)):
                aux(0, n)
            pe.wait_ge(factors_ready, 2)
            laps(pe, step)


def prepare(nc, W, ctxT, wk, bk, wv, bv, weights, centroids, routeT, bout, bo, bq, b1, b2, k_blocks, v_ctx):
    KS = HG * S2
    raws = [wk, wv] + [w for w, _ in weights]
    with ExitStack() as stack:
        sb = lambda *a: stack.enter_context(nc.sbuf_tensor(*a))
        sem = lambda s: stack.enter_context(nc.semaphore(s))
        kv_ps = stack.enter_context(nc.psum_tensor("kv_ps", [P, KT + B, CH], F32))
        t_ps = stack.enter_context(nc.psum_tensor("t_ps", [P, CH], F32))
        ctx_sb = sb("ctx_sb", [P, KT, B * S2], F32)
        bk_sb, bv_bc = sb("bk_sb", [P, KT], F32), sb("bv_bc", [S2, D], F32)
        cent, cent_sq = sb("cent", [E, D], F32), sb("cent_sq", [E, D], F32)
        cent_ss = sb("cent_ss", [E, 1], F32)
        cent_rn = sb("cent_rn", [E, 1], F32)
        blocks = W["soft"][:].rearrange("p j h s -> p (j h s)")[:, 0:B * NG * KS].rearrange(
            "p (b g n) -> p b g n", b=B, g=NG)
        vals = W["x1"][0:S2, 0:B]
        small, cleared, consts = sem("small_loaded"), sem("blocks_cleared"), sem("consts_made")
        raw_loaded = sems(nc, stack, "raw_loaded", len(raws))
        ctx_loaded = sem("ctx_loaded")
        kv_done, keys_done, vals_done, kv_stored = sem("kv_done"), sem("keys_done"), sem("vals_done"), sem("kv_stored")
        hi_done = sem("hi_done")
        squared, norm_ready, cent_ready, cent_turned, route_ready = (
            sem(s) for s in ("squared", "norm_ready", "cent_ready", "cent_turned", "route_ready"))
        block = stack.enter_context(nc.Block())

        NS = len(raws)
        more = sb("staging", [P, NS - 2, TT * D], F32)

        def raw(n):
            return W["work"][:, n] if n < 2 else more[:, n - 2]

        smalls = [(bk_sb[:], bk), (bv_bc[:], bv.partition_broadcast(S2)), (cent[:], centroids),
                  (W["route_raw"][:, :, E:2 * E], routeT.rearrange("(t p) e -> p t e", p=P)),
                  (W["bout_bc"][:], bout.partition_broadcast(P)), (W["bo_bc"][:], bo.partition_broadcast(P)),
                  (W["bq_sb"][:], bq), (W["b1_sb"][:], b1), (W["b2_sb"][:], b2)]

        @block.sync
        def _(sp):
            sp.dma_start(ctx_sb[:], ctxT.rearrange("(t p) n -> p t n", p=P)).then_inc(ctx_loaded, 16)
            for n, src in enumerate(raws):
                sp.dma_start(raw(n).rearrange("p (a b) -> p a b", a=src.shape[1]), src).then_inc(raw_loaded[n], 16)
            for dst, src in smalls:
                sp.dma_start(dst, src).then_inc(small, 16)
            sp.wait_ge(keys_done, NG * HG)
            sp.dma_start(k_blocks.rearrange("b p n -> p b n"), blocks.rearrange("p b g n -> p b (g n)")).then_inc(kv_stored, 16)
            sp.wait_ge(vals_done, B)
            sp.dma_start(v_ctx.rearrange("b p n -> p b n"), vals).then_inc(kv_stored, 16)
            sp.wait_ge(kv_stored, 32)

        @block.gpsimd
        def _(pool):
            nc.gpsimd.memset(W["ident"][:], 0.0).then_inc(consts, 1)
            nc.gpsimd.memset(W["power"][:], -0.5).then_inc(consts, 1)
            pool.wait_ge(consts, 2)
            nc.gpsimd.affine_select(out=W["ident"][:], in_=W["ident"][:], compare_op=ALU.not_equal, fill=1.0, base=0,
                                    pattern=[[-1, P]], channel_multiplier=1).then_inc(consts, 1)
            pool.wait_ge(squared, 2)
            nc.gpsimd.tensor_tensor(cent_rn[:], cent_ss[:], W["power"][0:E, 0:1], ALU.pow).then_inc(norm_ready, 1)

        @block.scalar
        def _(act):
            for n in range(2, NS):
                act.wait_ge(raw_loaded[n], 16)
                nc.scalar.activation(weights[n - 2][1][0], raw(n), ACT.Copy, scale=WS).then_inc(hi_done, 1)
            act.wait_ge(small, 16 * len(smalls))
            nc.scalar.activation(cent_sq[:], cent[:], ACT.Square, accum_out=cent_ss[:]).then_inc(squared, 1)
            act.wait_ge(cleared, 1)
            act.wait_ge(kv_done, 1)
            for g in range(NG):
                for h in range(HG):
                    rows = slice(h * DH, (h + 1) * DH)
                    nc.scalar.activation(blocks[rows, :, g, h * S2:(h + 1) * S2],
                                         kv_ps[rows, g, 0:B * S2].rearrange("p (b s) -> p b s", b=B), ACT.Identity,
                                         bias=bk_sb[rows, g:g + 1]).then_inc(keys_done, 1)

        @block.vector
        def _(dve):
            nc.vector.memset(blocks, 0.0).then_inc(cleared, 1)
            for n in range(2, NS):
                dve.wait_ge(hi_done, n - 1)
                nc.vector.scalar_tensor_tensor(weights[n - 2][1][1], raw(n), WS, weights[n - 2][1][0], ALU.mult,
                                               ALU.subtract)
            dve.wait_ge(squared, 1)
            nc.vector.tensor_scalar(cent_ss[:], cent_ss[:], 1e-24, None, ALU.max).then_inc(squared, 1)
            dve.wait_ge(norm_ready, 1)
            nc.vector.tensor_scalar(cent[:], cent[:], cent_rn[:], None, ALU.mult).then_inc(cent_ready, 1)
            dve.wait_ge(cent_turned, 1)
            nc.vector.tensor_copy(W["route_raw"][:, :, 0:E], t_ps[:, 0:KT * E].rearrange(
                "p (t e) -> p t e", t=KT)).then_inc(route_ready, 1)
            dve.wait_ge(route_ready, 1)
            nc.vector.tensor_scalar(W["route_p"][0][:], W["route_raw"][:], WS, None, ALU.mult).then_inc(route_ready, 1)
            dve.wait_ge(route_ready, 2)
            nc.vector.scalar_tensor_tensor(W["route_p"][1][:], W["route_raw"][:], WS, W["route_p"][0][:], ALU.mult,
                                           ALU.subtract).then_inc(route_ready, 1)
            dve.wait_ge(kv_done, 1)
            for b in range(B):
                nc.vector.tensor_tensor(vals[:, b], kv_ps[0:S2, KT + b], bv_bc[:], ALU.add).then_inc(vals_done, 1)

        @block.tensor
        def _(pe):
            pe.wait_ge(ctx_loaded, 16)
            pe.wait_ge(raw_loaded[0], 16)
            for g in range(NG):
                for t in range(KT):
                    nc.tensor.matmul(kv_ps[:, g, 0:B * S2], raw(0)[:, t * D + g * P:t * D + (g + 1) * P],
                                     ctx_sb[:, t], start=(t == 0), stop=(t == KT - 1))
            pe.wait_ge(raw_loaded[1], 16)
            for b in range(B):
                for t in range(KT):
                    last = nc.tensor.matmul(kv_ps[0:S2, KT + b], ctx_sb[:, t, b * S2:(b + 1) * S2],
                                            raw(1)[:, t * D:(t + 1) * D], start=(t == 0), stop=(t == KT - 1))
            last.then_inc(kv_done, 1)
            pe.wait_ge(consts, 3)
            pe.wait_ge(cent_ready, 1)
            for t in range(KT):
                last = nc.tensor.transpose(t_ps[:, t * E:(t + 1) * E], cent[:, t * P:(t + 1) * P],
                                           W["ident"][0:E, 0:E])
            last.then_inc(cent_turned, 1)


def chains(nc, W, weights, x_rows, o_parts, mask, k_blocks, v_ctx, out):
    KS = HG * S2
    SCALE = DH ** -0.5
    USES = (["dve"] * TT + ["dve"] * TT + ["act"] * KT + ["dve"] * (TT * NG)
            + ["act"] * HG + (["act"] * HG + ["dve"]) * (NG - 1) + ["dve"] + ["dve"] * TT + ["dve"] * TT + ["dve"] + ["act"])
    AT_OUT, AT_T1, AT_Q = 0, TT, 2 * TT
    AT_S = AT_Q + KT
    AT_PV = AT_S + TT * NG
    AT_O = AT_PV + (HG + 1) * NG
    AT_TURN = [AT_PV + max(g * (HG + 1) - 1, 0) for g in range(NG)]
    AT_VAL = [AT_TURN[g + 1] + HG for g in range(NG - 1)] + [AT_O - 1]
    AT_T2 = AT_O + TT
    AT_R = AT_T2 + TT
    AT_G = AT_R + 1
    NUSE, CB, FB = len(USES), 4, 4
    UNITS = [("bias", 0, j) for j in range(TT)]
    for e in range(E + 1):
        UNITS += [("hidden", e, n) for n in range(2) if e < E] + [("expert", e - 1, j) for j in range(TT) if e > 0]
    NUNIT = len(UNITS)
    F_USES = ["act" if kind == "hidden" else "dve" for kind, _, _ in UNITS]
    assert 2 * NUSE % CB == 0 and 2 * NUNIT % FB == 0
    PLAN = [("out", 4), ("norm1", 2), ("turn1", 2), ("query", 0), ("scores0", 4), ("scores1", 5), ("scores2", 6),
            ("scores3", 6), ("probs0", 4), ("probs1", 1), ("pv0", 1), ("probs2", 0), ("pv1", 1), ("probs3", 0),
            ("pv2", 0), ("pv3", 1), ("out2", 4), ("norm2", 3), ("turn2", 2), ("route", 6), ("gate", 0)]
    STAGES, FILL = zip(*PLAN)
    assert sum(FILL) == NUNIT
    FROM = [sum(FILL[:n]) for n in range(len(FILL))]
    APART = {"out": 3, "query": 2, "probs0": 1, "out2": 2}
    assert sum(APART.values()) == len(weights)
    LOOPED = (NC - 2) // 2

    x1, x2, x2T, oT, soft, hT, hidden = (W[k] for k in ("x1", "x2", "x2T", "oT", "soft", "hT", "hidden"))
    x1T = W["work"][:, 0].bitcast(F16).rearrange("p (s t n) -> p s t n", s=2, t=KT)
    xq = W["work"][:, 1].rearrange("p (t n) -> p t n", t=KT)
    ident, power = W["ident"], W["power"]
    raws = [x2[1][:].rearrange("p j n -> p (j n)"), x2T[1][:].rearrange("p s t n -> p (s t n)").bitcast(F32),
            hT[:].rearrange("p s e t n -> p (s e t n)").bitcast(F32)]

    def turned(g):
        return W["work"][0:S2, g % 2].rearrange("p (h n) -> p h n", h=HG)

    def nth(uses, k):
        return uses[:k].count(uses[k])

    with ExitStack() as stack:
        sb = lambda *a: stack.enter_context(nc.sbuf_tensor(*a))
        keys, vals = sb("keys", [P, NG, KS], F32), sb("vals", [S2, D], F32)
        mask_sb = sb("mask_sb", [P, S2], F32)
        stats, agg, rstd = sb("stats", [P, TT, 6], F32), sb("agg", [P, TT, 2], F32), sb("rstd", [P, TT], F32)
        stats3, agg3, rstd3 = sb("stats3", [P, TT, 6], F32), sb("agg3", [P, TT, 2], F32), sb("rstd3", [P, TT], F32)
        smax, ssum = sb("smax", [P, TT, H], F32), sb("ssum", [P, TT, H], F32)
        square, rnorm = sb("square", [P, TT], F32), sb("rnorm", [P, TT], F32)
        logit, weight = sb("logit", [P, TT, E], F32), sb("weight", [P, TT, E], F32)
        top, chosen, gsum = sb("top", [P, TT, 8], F32), sb("chosen", [P, TT, E], F32), sb("gsum", [P, TT], F32)
        gates = sb("gates", [P, TT, E], F32)
        gates_un = [sb(f"gates_un{a}", [P, TT, E], F32) for a in range(2)]
        gT = [sb(f"gT{a}", [E, TT, P], F32) for a in range(2)]
        cps = stack.enter_context(nc.psum_tensor("cps", [P, CB, CH], F32))
        fps = stack.enter_context(nc.psum_tensor("fps", [P, FB, CH], F32))

        def count(name, per):
            return Count(nc, stack, name, 2 * per)

        def sem(name):
            return stack.enter_context(nc.semaphore(name))

        x_loaded, oT_loaded, kv_loaded = sem("x_loaded"), sem("oT_loaded"), sem("kv_loaded")
        stored = sems(nc, stack, "stored", 2)
        raw_loaded = sems(nc, stack, "raw_w_loaded", len(raws))
        w_hi, w_lo = sem("expert_w_hi"), sem("expert_w_lo")
        c_ready = count("c_ready", NUSE)
        act_read = count("act_read", USES.count("act"))
        dve_read = count("dve_read", USES.count("dve"))
        hi_ready = count("hi_ready", TT + NG + TT)
        biased = count("biased", 2)
        summed, spread, varied = count("summed", 2 * TT), count("spread", 2 * TT), count("varied", 2)
        rooted = count("rooted", 2)
        normed = count("normed", 2 * TT)
        masked = count("masked", 1)
        smaxed, shifted, exped = count("smaxed", TT), count("shifted", TT), count("exped", TT)
        ssummed, inverted, probs_ready = count("ssummed", TT), count("inverted", TT), count("probs_ready", TT)
        squared, square_held, norm_rooted = count("squared", TT), count("square_held", 1), count("norm_rooted", 1)
        routed = count("routed", 13)
        gate_exped, gated = count("gate_exped", 1), count("gated", 1)
        f_ready = count("f_ready", NUNIT)
        gelu_done = count("gelu_done", 2 * E)
        h_hi, h_lo = count("h_hi", 2 * E), count("h_lo", 2 * E)
        added = count("acc_added", TT * (E + 1))
        summed3, spread3, varied3 = count("summed3", TT), count("spread3", TT), count("varied3", 1)
        rooted3, normed3 = count("rooted3", 1), count("normed3", TT)
        block = stack.enter_context(nc.Block())

        def at(c, i, u, k):
            return c.at(i, u * (c.per // 2) + k)

        def chunk(i, u):
            return 2 * i + u + 1

        def parity(u):
            return 1 - u

        def program(chain, experts, finish, apart=None):
            def slot(i, u, with_chain=True, with_experts=True):
                taken = 0
                for n, stage in enumerate(STAGES):
                    if apart and not with_experts:
                        for w in range(taken, taken + APART.get(stage, 0)):
                            apart(w, *weights[w])
                        taken += APART.get(stage, 0)
                    if with_chain:
                        chain(i, u, stage)
                    if with_experts:
                        for f in range(FROM[n], FROM[n] + FILL[n]):
                            experts(i, u, f, *UNITS[f])
                if with_experts:
                    finish(i, u)
            return slot

        def run(engine, slot, weights_used=False):
            slot(-1, 1, with_experts=False)
            if weights_used:
                engine.wait_ge(w_lo, len(weights))
            with engine.Fori(0, LOOPED) as i:
                slot(i, 0)
                slot(i, 1)
            slot(LOOPED, 0)
            slot(LOOPED, 1, with_chain=False)

        def lead(engine, chain_counts, expert_counts):
            for c in chain_counts:
                c.lead(engine, made=c.per // 2)
            for c in expert_counts:
                c.lead(engine)

        @block.sync
        def _(sp):
            def load(n):
                rows = bass.ds(n * CH, CH)
                sp.dma_start(x1[:], x_rows[rows, :].rearrange("(j p) d -> p j d", p=P)).then_inc(x_loaded, 16)
                sp.dma_start(oT[:], o_parts[:, :, rows].rearrange("s (t p) n -> p s t n", p=P)).then_inc(oT_loaded, 16)
                b = n // CPB
                sp.dma_start(keys[:].rearrange("p g n -> p (g n)"), k_blocks[bass.ds(b, 1)].rearrange(
                    "b p n -> (b p) n")).then_inc(kv_loaded, 16)
                sp.dma_start(vals[:], v_ctx[bass.ds(b, 1)].rearrange("b p n -> (b p) n")).then_inc(kv_loaded, 16)
                sp.dma_start(mask_sb[:], mask[bass.ds(b, 1)].rearrange("b a c s -> (b a c s)").partition_broadcast(
                    P)).then_inc(kv_loaded, 16)

            def load_next(i, u):
                sp.wait_ge(dve_read.sem, at(dve_read, i, u, nth(USES, AT_O + TT - 1)))
                load(chunk(i, u) + 1)

            def store(i, u):
                sp.wait_ge(normed3.sem, at(normed3, i, u, TT - 1))
                sp.dma_start(out[bass.ds((chunk(i, u) - 1) * CH, CH), :].rearrange("(j p) d -> p j d", p=P),
                             x2[u][:]).then_inc(stored[u], 16)

            load(0)
            for n, (src, _) in enumerate(weights):
                if n >= len(raws):
                    sp.wait_ge(w_lo, n - len(raws) + 1)
                sp.dma_start(raws[n % len(raws)].rearrange("p (a b) -> p a b", a=src.shape[1]), src).then_inc(
                    raw_loaded[n % len(raws)], 16)
            load_next(-1, 1)
            with sp.Fori(0, LOOPED) as i:
                for u in range(2):
                    load_next(i, u)
                    store(i, u)
            store(LOOPED, 0)
            store(LOOPED, 1)
            for s in stored:
                sp.wait_ge(s, 16 * NC // 2)

        @block.gpsimd
        def _(pool):
            lead(pool, (biased, rooted, probs_ready, norm_rooted), (rooted3,))

            def add_row(row, c, k, i, u):
                nc.gpsimd.tensor_tensor(x1[:], x1[:], row[:].rearrange("p (a n) -> p a n", a=1).broadcast_to(
                    [P, TT, D]), ALU.add).then_inc(c.sem, 1)

            def root(var, c, width):
                nc.gpsimd.tensor_tensor(var, var, power[:, 0:width], ALU.pow).then_inc(c.sem, 1)

            def chain(i, u, stage):
                if stage == "out":
                    pool.wait_ge(x_loaded, 16 * (chunk(i, u) + 1))
                    add_row(W["bout_bc"], biased, 0, i, u)
                    pool.wait_ge(varied.sem, at(varied, i, u, 0))
                    root(rstd[:], rooted, TT)
                elif stage == "turn1":
                    pool.wait_ge(c_ready.sem, at(c_ready, i, u, AT_T1 + TT - 1))
                    add_row(W["bo_bc"], biased, 1, i, u)
                elif stage.startswith("scores"):
                    at_end = int(stage[-1])
                    for j in ([at_end - 1] if at_end else []) + ([at_end] if at_end == TT - 1 else []):
                        pool.wait_ge(inverted.sem, at(inverted, i, u, j))
                        nc.gpsimd.tensor_tensor(soft[:, j], soft[:, j], ssum[:, j, :].rearrange(
                            "p (h a) -> p h a", a=1).broadcast_to([P, H, S2]), ALU.mult).then_inc(probs_ready.sem, 1)
                elif stage == "out2":
                    pool.wait_ge(varied.sem, at(varied, i, u, 1))
                    root(rstd[:], rooted, TT)
                elif stage == "route":
                    pool.wait_ge(square_held.sem, at(square_held, i, u, 0))
                    nc.gpsimd.tensor_tensor(rnorm[:], square[:], power[:, 0:TT], ALU.pow).then_inc(norm_rooted.sem, 1)

            def experts(i, u, f, kind, e, j):
                pass

            def finish(i, u):
                pool.wait_ge(varied3.sem, at(varied3, i, u, 0))
                root(rstd3[:], rooted3, TT)

            run(pool, program(chain, experts, finish))

        @block.scalar
        def _(act):
            lead(act, (act_read, hi_ready, exped, squared, gate_exped), (gelu_done,))

            def wait_product(i, u, k):
                act.wait_ge(c_ready.sem, at(c_ready, i, u, k))
                return cps[:, (u * NUSE + k) % CB]

            def chain(i, u, stage):
                p = parity(u)
                if stage in ("turn1", "turn2"):
                    k0, dst = (AT_T1, x1T) if stage == "turn1" else (AT_T2, x2T[p])
                    for j in range(TT):
                        bank = wait_product(i, u, k0 + j)
                        nc.scalar.activation(dst[:, 0, :, j * P:(j + 1) * P], bank.rearrange("p (t n) -> p t n", t=KT),
                                             ACT.Copy, scale=XS).then_inc(hi_ready.sem, 1)
                elif stage == "query":
                    for o in range(KT):
                        bank = wait_product(i, u, AT_Q + o)
                        nc.scalar.activation(xq[:, o], bank, ACT.Identity, bias=W["bq_sb"][:, o:o + 1],
                                             scale=UN).then_inc(act_read.sem, 1)
                elif stage.startswith("scores"):
                    j = int(stage[-1])
                    act.wait_ge(shifted.sem, at(shifted, i, u, j))
                    nc.scalar.activation(soft[:, j], soft[:, j], ACT.Exp).then_inc(exped.sem, 1)
                elif stage.startswith("probs"):
                    g = int(stage[-1])
                    for h in range(HG):
                        bank = wait_product(i, u, AT_TURN[g] + h)
                        nc.scalar.activation(turned(g)[:, h], bank[0:S2], ACT.Copy).then_inc(act_read.sem, 1)
                elif stage.startswith("pv"):
                    g = int(stage[-1])
                    bank = wait_product(i, u, AT_VAL[g])
                    nc.scalar.activation(oT[:, 0, g], bank, ACT.Copy, scale=XS).then_inc(hi_ready.sem, 1)
                elif stage == "route":
                    for j in range(TT):
                        act.wait_ge(normed.sem, at(normed, i, u, TT + j))
                        nc.scalar.activation(soft[:].rearrange("p j h s -> p (j h s)")[:, j * D:(j + 1) * D],
                                             x2[p][:, j], ACT.Square, accum_out=square[:, j:j + 1]).then_inc(squared.sem, 1)
                elif stage == "gate":
                    act.wait_ge(routed.sem, at(routed, i, u, 8))
                    nc.scalar.activation(weight[:], logit[:], ACT.Exp).then_inc(gate_exped.sem, 1)
                    bank = wait_product(i, u, AT_G)
                    nc.scalar.activation(gT[p][:], bank[0:E].rearrange("e (j n) -> e j n", j=TT),
                                         ACT.Copy).then_inc(act_read.sem, 1)

            def experts(i, u, f, kind, e, j):
                if kind == "hidden":
                    n = 2 * e + j
                    act.wait_ge(f_ready.sem, at(f_ready, i, u, f))
                    act.wait_ge(h_lo.sem, at(h_lo, i, u, n - 2))
                    nc.scalar.activation(hidden[:, n % 2], fps[:, (u * NUNIT + f) % FB], ACT.Gelu,
                                         bias=W["b1_sb"][:, n:n + 1], scale=UN).then_inc(gelu_done.sem, 1)

            def finish(i, u):
                pass

            def apart(n, src, dst):
                act.wait_ge(raw_loaded[n % len(raws)], 16 * (n // len(raws) + 1))
                nc.scalar.activation(dst[0], raws[n % len(raws)], ACT.Copy, scale=WS).then_inc(w_hi, 1)

            run(act, program(chain, experts, finish, apart))

        @block.vector
        def _(dve):
            lead(dve, (dve_read, summed, spread, varied, normed, masked, smaxed, shifted, ssummed, inverted,
                       square_held, routed), (h_hi, h_lo, added, summed3, spread3, varied3, normed3))

            def wait_product(i, u, k):
                dve.wait_ge(c_ready.sem, at(c_ready, i, u, k))
                return cps[:, (u * NUSE + k) % CB]

            def lo_part(i, u, k, hi_index, dst, hi):
                bank = cps[:, (u * NUSE + k) % CB]
                if len(dst.shape) == 3:
                    bank = bank.rearrange("p (t n) -> p t n", t=KT)
                dve.wait_ge(hi_ready.sem, at(hi_ready, i, u, hi_index))
                nc.vector.scalar_tensor_tensor(dst, bank, XS, hi, ALU.mult, ALU.subtract).then_inc(dve_read.sem, 1)

            def spreads(rows, st, ag, rs, c, i, u, which, source, k0):
                c_sum, c_spread, c_var, _, _ = c
                for j in range(TT):
                    if j > 0:
                        dve.wait_ge(c_sum.sem, at(c_sum, i, u, which * TT + j - 1))
                    dve.wait_ge(source.sem, at(source, i, u, k0 + j))
                    nc.vector.bn_stats(st[:, j], rows[:, j]).then_inc(c_sum.sem, 1)
                    if j > 0:
                        nc.vector.bn_aggr(ag[:, j - 1], st[:, j - 1]).then_inc(c_spread.sem, 1)
                dve.wait_ge(c_sum.sem, at(c_sum, i, u, which * TT + TT - 1))
                dve.wait_ge(c_spread.sem, at(c_spread, i, u, which * TT + TT - 2))
                nc.vector.tensor_scalar(rs[:, 0:TT - 1], ag[:, 0:TT - 1, 1], EPS, None, ALU.add)
                nc.vector.bn_aggr(ag[:, TT - 1], st[:, TT - 1]).then_inc(c_spread.sem, 1)
                dve.wait_ge(c_spread.sem, at(c_spread, i, u, which * TT + TT - 1))
                nc.vector.tensor_scalar(rs[:, TT - 1:TT], ag[:, TT - 1:TT, 1], EPS, None,
                                        ALU.add).then_inc(c_var.sem, 1)

            def norm(rows, ag, rs, c, i, u, which):
                c_root, c_norm = c[3:]
                dve.wait_ge(c_root.sem, at(c_root, i, u, which))
                for j in range(TT):
                    nc.vector.tensor_scalar(rows[:, j], rows[:, j], ag[:, j, 0:1], rs[:, j:j + 1], ALU.subtract,
                                            ALU.mult).then_inc(c_norm.sem, 1)

            chain_norm = (summed, spread, varied, rooted, normed)

            def softmax_start(i, u, j):
                for g in range(NG):
                    bank = wait_product(i, u, AT_S + j * NG + g)
                    nc.vector.scalar_tensor_tensor(
                        soft[:, j, g * HG:(g + 1) * HG], bank[:, 0:KS].rearrange("p (h s) -> p h s", h=HG), SCALE,
                        mask_sb[:].rearrange("p (a s) -> p a s", a=1).broadcast_to([P, HG, S2]), ALU.mult,
                        ALU.add).then_inc(dve_read.sem, 1)
                dve.wait_ge(dve_read.sem, at(dve_read, i, u, nth(USES, AT_S + j * NG + NG - 1)))
                nc.vector.reduce_max(smax[:, j], soft[:, j], AX.X).then_inc(smaxed.sem, 1)
                dve.wait_ge(smaxed.sem, at(smaxed, i, u, j))
                nc.vector.tensor_tensor(soft[:, j], soft[:, j], smax[:, j].rearrange("p (h a) -> p h a", a=1)
                                        .broadcast_to([P, H, S2]), ALU.subtract).then_inc(shifted.sem, 1)

            def softmax_end(i, u, j):
                dve.wait_ge(exped.sem, at(exped, i, u, j))
                nc.vector.reduce_sum(ssum[:, j], soft[:, j], AX.X).then_inc(ssummed.sem, 1)
                dve.wait_ge(ssummed.sem, at(ssummed, i, u, j))
                nc.vector.reciprocal(ssum[:, j], ssum[:, j]).then_inc(inverted.sem, 1)

            def chain(i, u, stage):
                p = parity(u)
                if stage == "out":
                    dve.wait_ge(biased.sem, at(biased, i, u, 0))
                    for j in range(TT):
                        bank = wait_product(i, u, AT_OUT + j)
                        nc.vector.scalar_tensor_tensor(x1[:, j], bank, UN, x1[:, j], ALU.mult,
                                                       ALU.add).then_inc(dve_read.sem, 1)
                    spreads(x1, stats, agg, rstd, chain_norm, i, u, 0, dve_read, nth(USES, AT_OUT))
                elif stage == "norm1":
                    norm(x1, agg, rstd, chain_norm, i, u, 0)
                elif stage == "turn1":
                    for j in range(TT):
                        cols = slice(j * P, (j + 1) * P)
                        lo_part(i, u, AT_T1 + j, j, x1T[:, 1, :, cols], x1T[:, 0, :, cols])
                elif stage.startswith("scores"):
                    j = int(stage[-1])
                    if j == 0:
                        dve.wait_ge(kv_loaded, 48 * (chunk(i, u) + 1))
                        nc.vector.tensor_scalar(mask_sb[:], mask_sb[:], NEG, None, ALU.mult).then_inc(masked.sem, 1)
                        dve.wait_ge(masked.sem, at(masked, i, u, 0))
                    softmax_start(i, u, j)
                    if j > 0:
                        softmax_end(i, u, j - 1)
                    if j == TT - 1:
                        softmax_end(i, u, j)
                elif stage.startswith("pv"):
                    g = int(stage[-1])
                    lo_part(i, u, AT_VAL[g], TT + g, oT[:, 1, g], oT[:, 0, g])
                elif stage == "out2":
                    dve.wait_ge(biased.sem, at(biased, i, u, 1))
                    dve.wait_ge(stored[p], 16 * (i + u))
                    for j in range(TT):
                        bank = wait_product(i, u, AT_O + j)
                        nc.vector.scalar_tensor_tensor(x2[p][:, j], bank, UN, x1[:, j], ALU.mult,
                                                       ALU.add).then_inc(dve_read.sem, 1)
                    spreads(x2[p], stats, agg, rstd, chain_norm, i, u, 1, dve_read, nth(USES, AT_O))
                elif stage == "norm2":
                    norm(x2[p], agg, rstd, chain_norm, i, u, 1)
                elif stage == "turn2":
                    for j in range(TT):
                        cols = slice(j * P, (j + 1) * P)
                        lo_part(i, u, AT_T2 + j, TT + NG + j, x2T[p][:, 1, :, cols], x2T[p][:, 0, :, cols])
                elif stage == "route":
                    dve.wait_ge(squared.sem, at(squared, i, u, TT - 1))
                    nc.vector.tensor_scalar(square[:], square[:], 1e-24, None, ALU.max).then_inc(square_held.sem, 1)
                    dve.wait_ge(norm_rooted.sem, at(norm_rooted, i, u, 0))
                    bank = wait_product(i, u, AT_R)[:, 0:TT * 2 * E].rearrange("p (j n) -> p j n", j=TT)
                    wide = lambda a: a.rearrange("p (j a) -> p j a", a=1).broadcast_to([P, TT, E])
                    nc.vector.scalar_tensor_tensor(weight[:], bank[:, :, 0:E], UN, wide(rnorm[:]), ALU.mult,
                                                   ALU.mult).then_inc(routed.sem, 1)
                    dve.wait_ge(routed.sem, at(routed, i, u, 0))
                    half = TT // 2
                    nc.vector.scalar_tensor_tensor(logit[:, 0:half], bank[:, 0:half, E:2 * E], UN, weight[:, 0:half],
                                                   ALU.mult, ALU.add).then_inc(routed.sem, 1)
                    dve.wait_ge(routed.sem, at(routed, i, u, 1))
                    nc.vector.scalar_tensor_tensor(logit[:, half:], bank[:, half:, E:2 * E], UN, weight[:, half:],
                                                   ALU.mult, ALU.add).then_inc(dve_read.sem, 1)
                    for r, step in ((0, 4), (half, 7)):
                        for j in range(r, r + half):
                            nc.vector.max(top[:, j], logit[:, j]).then_inc(routed.sem, 1)
                        dve.wait_ge(dve_read.sem, at(dve_read, i, u, nth(USES, AT_R)))
                        dve.wait_ge(routed.sem, at(routed, i, u, step - 1))
                        nc.vector.tensor_tensor(chosen[:, r:r + half], logit[:, r:r + half],
                                                top[:, r:r + half, 1:2].broadcast_to([P, half, E]),
                                                ALU.is_ge).then_inc(routed.sem, 1)
                    dve.wait_ge(routed.sem, at(routed, i, u, 7))
                    nc.vector.tensor_tensor(logit[:], logit[:], top[:, :, 0:1].broadcast_to([P, TT, E]),
                                            ALU.subtract).then_inc(routed.sem, 1)
                elif stage == "gate":
                    dve.wait_ge(gate_exped.sem, at(gate_exped, i, u, 0))
                    nc.vector.tensor_tensor(weight[:], weight[:], chosen[:], ALU.mult).then_inc(routed.sem, 1)
                    dve.wait_ge(routed.sem, at(routed, i, u, 9))
                    nc.vector.reduce_sum(gsum[:], weight[:], AX.X).then_inc(routed.sem, 1)
                    dve.wait_ge(routed.sem, at(routed, i, u, 10))
                    nc.vector.reciprocal(gsum[:], gsum[:]).then_inc(routed.sem, 1)
                    dve.wait_ge(routed.sem, at(routed, i, u, 11))
                    wide = gsum[:].rearrange("p (j a) -> p j a", a=1).broadcast_to([P, TT, E])
                    nc.vector.tensor_tensor(gates[:], weight[:], wide, ALU.mult).then_inc(routed.sem, 1)
                    nc.vector.scalar_tensor_tensor(gates_un[p][:], weight[:], UN, wide, ALU.mult,
                                                   ALU.mult).then_inc(gated.sem, 1)

            def experts(i, u, f, kind, e, j):
                bank = fps[:, (u * NUNIT + f) % FB]
                q = u
                if kind == "hidden":
                    n = 2 * e + j
                    dve.wait_ge(gelu_done.sem, at(gelu_done, i, u, n))
                    if j == 0:
                        dve.wait_ge(f_ready.sem, at(f_ready, i, u, UNITS.index(("expert", e - 2, TT - 1)) if e >= 2
                                                    else UNITS.index(("expert", E + e - 2, TT - 1)) - NUNIT))
                    nc.vector.tensor_scalar(hT[:, 0, e % 2, j], hidden[:, n % 2], XS, None,
                                            ALU.mult).then_inc(h_hi.sem, 1)
                    dve.wait_ge(h_hi.sem, at(h_hi, i, u, n))
                    nc.vector.scalar_tensor_tensor(hT[:, 1, e % 2, j], hidden[:, n % 2], XS, hT[:, 0, e % 2, j],
                                                   ALU.mult, ALU.subtract).then_inc(h_lo.sem, 1)
                    return
                dve.wait_ge(f_ready.sem, at(f_ready, i, u, f))
                if kind == "bias":
                    nc.vector.tensor_tensor(x2[q][:, j], bank, x2[q][:, j], ALU.add).then_inc(added.sem, 1)
                else:
                    dve.wait_ge(added.sem, at(added, i, u, e * TT + j))
                    nc.vector.scalar_tensor_tensor(x2[q][:, j], bank, gates_un[q][:, j, e:e + 1], x2[q][:, j],
                                                   ALU.mult, ALU.add).then_inc(added.sem, 1)

            def finish(i, u):
                c = summed3, spread3, varied3, rooted3, normed3
                spreads(x2[u], stats3, agg3, rstd3, c, i, u, 0, added, E * TT)
                norm(x2[u], agg3, rstd3, c, i, u, 0)

            def apart(n, src, dst):
                dve.wait_ge(w_hi, n + 1)
                nc.vector.scalar_tensor_tensor(dst[1], raws[n % len(raws)], WS, dst[0], ALU.mult,
                                               ALU.subtract).then_inc(w_lo, 1)

            gated.lead(dve, made=1)
            run(dve, program(chain, experts, finish, apart))

        @block.tensor
        def _(pe):
            lead(pe, (c_ready,), (f_ready,))

            def chain_bank(i, u, k):
                if k >= CB:
                    who = USES[k - CB]
                    c, n = (act_read if who == "act" else dve_read), nth(USES, k - CB)
                else:
                    who = USES[NUSE + k - CB]
                    c = act_read if who == "act" else dve_read
                    n = nth(USES, NUSE + k - CB) - c.per // 2
                pe.wait_ge(c.sem, at(c, i, u, n))
                return cps[:, (u * NUSE + k) % CB]

            def experts_bank(i, u, f):
                who = F_USES[f - FB]
                c = gelu_done if who == "act" else added
                n = nth(F_USES, (f - FB) % NUNIT) - (0 if f >= FB else c.per // 2)
                pe.wait_ge(c.sem, at(c, i, u, n))
                return fps[:, (u * NUNIT + f) % FB]

            def product(bank, lhs, rhs, tiles):
                steps = [(t, a, b) for t in range(tiles) for a, b in TERMS]
                for n, (t, a, b) in enumerate(steps):
                    last = nc.tensor.matmul(bank, lhs(a, t), rhs(b, t), start=(n == 0), stop=(n == len(steps) - 1))
                return last

            def chain(i, u, stage):
                p = parity(u)
                if stage in ("out", "out2"):
                    if stage == "out":
                        pe.wait_ge(oT_loaded, 16 * (chunk(i, u) + 1))
                        k0, w = AT_OUT, W["wout_p"]
                    else:
                        pe.wait_ge(dve_read.sem, at(dve_read, i, u, nth(USES, AT_O - 1)))
                        k0, w = AT_O, W["wo_p"]
                    for j in range(TT):
                        bank = chain_bank(i, u, k0 + j)
                        product(bank, lambda a, t: oT[:, a, t, j * P:(j + 1) * P], lambda b, t: w[b][:, t],
                                KT).then_inc(c_ready.sem, 1)
                elif stage in ("turn1", "turn2"):
                    k0, src, done = (AT_T1, x1, 0) if stage == "turn1" else (AT_T2, x2[p], TT)
                    for j in range(TT):
                        pe.wait_ge(normed.sem, at(normed, i, u, done + j))
                        bank = chain_bank(i, u, k0 + j)
                        for t in range(KT):
                            last = nc.tensor.transpose(bank[:, t * P:(t + 1) * P], src[:, j, t * P:(t + 1) * P], ident[:])
                        last.then_inc(c_ready.sem, 1)
                elif stage == "query":
                    pe.wait_ge(dve_read.sem, at(dve_read, i, u, nth(USES, AT_T1 + TT - 1)))
                    for o in range(KT):
                        bank = chain_bank(i, u, AT_Q + o)
                        product(bank, lambda a, t: W["wq_p"][a][:, t, o * P:(o + 1) * P], lambda b, t: x1T[:, b, t],
                                KT).then_inc(c_ready.sem, 1)
                elif stage.startswith("scores"):
                    j = int(stage[-1])
                    if j == 0:
                        pe.wait_ge(kv_loaded, 48 * (chunk(i, u) + 1))
                        pe.wait_ge(act_read.sem, at(act_read, i, u, KT - 1))
                    for g in range(NG):
                        bank = chain_bank(i, u, AT_S + j * NG + g)
                        nc.tensor.matmul(bank[:, 0:KS], xq[:, g, j * P:(j + 1) * P], keys[:, g], start=True,
                                         stop=True).then_inc(c_ready.sem, 1)
                elif stage.startswith("probs"):
                    g = int(stage[-1])
                    pe.wait_ge(probs_ready.sem, at(probs_ready, i, u, TT - 1))
                    for h in range(HG):
                        bank = chain_bank(i, u, AT_TURN[g] + h)
                        for j in range(TT):
                            last = nc.tensor.transpose(bank[0:S2, j * P:(j + 1) * P], soft[:, j, g * HG + h], ident[:])
                        last.then_inc(c_ready.sem, 1)
                elif stage.startswith("pv"):
                    g = int(stage[-1])
                    bank = chain_bank(i, u, AT_VAL[g])
                    pe.wait_ge(act_read.sem, at(act_read, i, u, nth(USES, AT_TURN[g] + HG - 1)))
                    for h in range(HG):
                        f = (g * HG + h) * DH
                        last = nc.tensor.matmul(bank[h * DH:(h + 1) * DH], vals[:, f:f + DH], turned(g)[:, h],
                                                start=True, stop=True)
                    last.then_inc(c_ready.sem, 1)
                elif stage == "route":
                    pe.wait_ge(dve_read.sem, at(dve_read, i, u, nth(USES, AT_T2 + TT - 1)))
                    bank = chain_bank(i, u, AT_R)
                    for j in range(TT):
                        last = product(bank[:, j * 2 * E:(j + 1) * 2 * E],
                                       lambda a, t: x2T[p][:, a, t, j * P:(j + 1) * P],
                                       lambda b, t: W["route_p"][b][:, t], KT)
                    last.then_inc(c_ready.sem, 1)
                elif stage == "gate":
                    pe.wait_ge(routed.sem, at(routed, i, u, 12))
                    bank = chain_bank(i, u, AT_G)
                    for j in range(TT):
                        last = nc.tensor.transpose(bank[0:E, j * P:(j + 1) * P], gates[:, j], ident[:])
                    last.then_inc(c_ready.sem, 1)

            def experts(i, u, f, kind, e, j):
                bank = experts_bank(i, u, f)
                if kind == "bias":
                    pe.wait_ge(act_read.sem, at(act_read, i, u, nth(USES, AT_G) - act_read.per // 2))
                    last = nc.tensor.matmul(bank, gT[u][:, j], W["b2_sb"][:], start=True, stop=True)
                elif kind == "hidden":
                    n = 2 * e + j
                    last = product(bank, lambda a, t: W["w1_p"][a][:, t, n * P:(n + 1) * P],
                                   lambda b, t: x2T[u][:, b, t], KT)
                else:
                    pe.wait_ge(h_lo.sem, at(h_lo, i, u, 2 * e + 1))
                    last = product(bank, lambda a, t: hT[:, a, e % 2, t, j * P:(j + 1) * P],
                                   lambda b, t: W["w2_p"][b][:, 2 * e + t], DE // P)
                last.then_inc(f_ready.sem, 1)

            def finish(i, u):
                pass

            run(pe, program(chain, experts, finish), weights_used=True)


def layer(nc, x_rows, xT, ctxT, mask, wqkvT, woutT, bout, wq, bq, wk, bk, wv, bv, wo, bo, w1, b1, w2, b2, centroids,
          routeT, out):
    dram = lambda name, shape, dt: nc.dram_tensor(name, shape, dt).ap()
    q_parts, k_parts, o_parts = (dram(n, [2, D, N], F16) for n in ("q_parts", "k_parts", "o_parts"))
    v_rows = dram("v_rows", [N, D], F32)
    project_qkv(nc, xT, wqkvT, q_parts, k_parts, v_rows)
    self_attention(nc, q_parts, k_parts, v_rows, o_parts)
    second_half(nc, x_rows, o_parts, ctxT, mask, woutT, bout, wq, bq, wk, bk, wv, bv, wo, bo, w1, b1, w2, b2,
                centroids, routeT, out)


def second_half(nc, x_rows, o_parts, ctxT, mask, woutT, bout, wq, bq, wk, bk, wv, bv, wo, bo, w1, b1, w2, b2,
                centroids, routeT, out):
    dram = lambda name, shape, dt: nc.dram_tensor(name, shape, dt).ap()
    k_blocks, v_ctx = dram("k_blocks", [B, P, NG * HG * S2], F32), dram("v_ctx", [B, S2, D], F32)
    with ExitStack() as stack:
        W = {}

        def resident(name, shape, dt):
            W[name] = stack.enter_context(nc.sbuf_tensor(name, shape, dt))

        def parts(name, shape):
            W[name] = [stack.enter_context(nc.sbuf_tensor(f"{name}_{s}", shape, F16)) for s in ("hi", "lo")]

        for name in ("wout_p", "wq_p", "wo_p"):
            parts(name, [P, KT, D])
        parts("w1_p", [P, KT, E * DE])
        parts("w2_p", [P, FT, D])
        parts("route_p", [P, KT, 2 * E])
        resident("route_raw", [P, KT, 2 * E], F32)
        resident("work", [P, 2, TT * D], F32)
        resident("ident", [P, P], F32)
        resident("power", [P, H], F32)
        resident("oT", [P, 2, KT, CH], F16)
        resident("x1", [P, TT, D], F32)
        resident("soft", [P, TT, H, S2], F32)
        resident("hidden", [P, 2, CH], F32)
        resident("hT", [P, 2, 2, 2, CH], F16)
        resident("bout_bc", [P, D], F32)
        resident("bo_bc", [P, D], F32)
        resident("bq_sb", [P, KT], F32)
        resident("b1_sb", [P, FT], F32)
        resident("b2_sb", [E, D], F32)
        flat = lambda a: a.rearrange("(t p) n -> p t n", p=P)
        cols = lambda t: t.rearrange("p t n -> p (t n)")
        weights = []
        for name, src in (("wout_p", woutT), ("wq_p", wq), ("wo_p", wo)):
            weights.append((flat(src), [cols(part[:]) for part in W[name]]))
        for t in range(KT):
            weights.append((w1[:, t * P:(t + 1) * P, :].rearrange("e p h -> p e h"),
                            [part[:, t] for part in W["w1_p"]]))
        for n in range(FT // KT):
            weights.append((w2.rearrange("e (t p) n -> p (e t) n", p=P)[:, n * KT:(n + 1) * KT],
                            [cols(part[:, n * KT:(n + 1) * KT]) for part in W["w2_p"]]))
        prepare(nc, W, ctxT, flat(wk), bk, flat(wv), bv, weights[:3], centroids, routeT, bout, bo, bq, b1, b2, k_blocks,
                v_ctx)
        for name in ("x2", "x2T"):
            shape, dt = ([P, TT, D], F32) if name == "x2" else ([P, 2, KT, CH], F16)
            W[name] = [stack.enter_context(nc.sbuf_tensor(f"{name}_{a}", shape, dt)) for a in range(2)]
        chains(nc, W, weights[3:], x_rows, o_parts, mask, k_blocks, v_ctx, out)


_INPUTS = ["x", "ctx_1024", "mask_Bx1x1xS2_ff0", "L0_attn_Wqkv", "L0_attn_Wout", "L0_attn_bout", "L0_xattn_Wq",
           "L0_xattn_bq", "L0_xattn_Wk", "L0_xattn_bk", "L0_xattn_Wv", "L0_xattn_bv", "L0_xattn_Wo", "L0_xattn_bo",
           "L0_ffn_w1", "L0_ffn_b1", "L0_ffn_w2", "L0_ffn_b2", "L0_ffn_centroids", "L0_ffn_w_route"]


def kernel(**inputs):
    import numpy as np
    import concourse.bacc as bacc
    from concourse.bass_utils import run_bass_kernel_spmd

    a = {k: np.asarray(inputs[k]) for k in _INPUTS}
    arrays = {
        "x_rows": a["x"].reshape(N, D), "xT": a["x"].reshape(N, D).T, "ctxT": a["ctx_1024"].reshape(B * S2, D).T,
        "mask": a["mask_Bx1x1xS2_ff0"], "wqkvT": a["L0_attn_Wqkv"].T, "woutT": a["L0_attn_Wout"].T,
        "bout": a["L0_attn_bout"], "wq": a["L0_xattn_Wq"], "bq": a["L0_xattn_bq"].reshape(KT, P).T,
        "wk": a["L0_xattn_Wk"], "bk": a["L0_xattn_bk"].reshape(KT, P).T, "wv": a["L0_xattn_Wv"], "bv": a["L0_xattn_bv"], "wo": a["L0_xattn_Wo"],
        "bo": a["L0_xattn_bo"], "w1": a["L0_ffn_w1"], "b1": a["L0_ffn_b1"].reshape(FT, P).T, "w2": a["L0_ffn_w2"],
        "b2": a["L0_ffn_b2"], "centroids": a["L0_ffn_centroids"], "routeT": a["L0_ffn_w_route"].T,
    }
    arrays = {k: np.ascontiguousarray(v) for k, v in arrays.items()}
    nc = bacc.Bacc("TRN2", target_bir_lowering=False, num_devices=1)
    handles = {k: nc.dram_tensor(f"{k}_in", v.shape, F32, kind="ExternalInput").ap() for k, v in arrays.items()}
    out = nc.dram_tensor("out", [N, D], F32, kind="ExternalOutput").ap()
    layer(nc, out=out, **handles)
    r = run_bass_kernel_spmd(nc, [{f"{k}_in": v for k, v in arrays.items()}], core_ids=[0])
    return r.results[0]["out"].reshape(B, T, D)
```

```python
from contextlib import ExitStack

import concourse.bass as bass
from concourse import mybir

F32, F16, BF16 = mybir.dt.float32, mybir.dt.float16, mybir.dt.bfloat16
ALU, ACT, AX = mybir.AluOpType, mybir.ActivationFunctionType, mybir.AxisListType

B, T, D, H, DH = 2, 2048, 512, 16, 32
S2 = 77
E, DE = 8, 256
N = B * T
P = 128
KT = D // P
HG = P // DH
NG = H // HG
CH = 512
NC = N // CH
CPB = T // CH
TT = CH // P
FT = E * DE // P
EPS = 1e-5
NEG = -1e9

XS = 32.0
WS = 512.0
UN = 1.0 / (XS * WS)
QK = XS * XS
MASKED = -1e30
TERMS = ((0, 0), (1, 0), (0, 1))


class Count:

    def __init__(self, nc, stack, name, per):
        self.sem, self.per = stack.enter_context(nc.semaphore(name)), per

    def lead(self, engine, made=0):
        engine.sem_inc(self.sem, self.per - made)

    def at(self, lap, k):
        return (lap + 1) * self.per + k + 1


def sems(nc, stack, name, n):
    return [stack.enter_context(nc.semaphore(f"{name}{s}")) for s in range(n)]


def start_stored(sp, *rings):
    for ring in rings:
        for s in ring:
            sp.sem_inc(s, 1)


def stored_at(n):
    return 16 * n + 1


def project_qkv(nc, xT, wqkvT, q_parts, k_parts, v_rows):
    NU = 2
    LAPS = NC // NU
    OT = 2 * KT
    PER = OT + TT
    NB, NQ, NV = 8, 4, 2
    QL, VL = NU * OT // NQ, NU * TT // NV
    with ExitStack() as stack:
        sb = lambda *a: stack.enter_context(nc.sbuf_tensor(*a))
        w_raw = sb("w_raw", [P, KT, 3 * D], F32)
        w_parts = sb("w_hi", [P, KT, 3 * D], F16), sb("w_lo", [P, KT, 3 * D], F16)
        x_raw = sb("x_raw", [P, NU, KT, CH], F32)
        x_parts = sb("x_hi", [P, NU, KT, CH], F16), sb("x_lo", [P, NU, KT, CH], F16)
        qk_out = sb("qk_out", [P, NQ, 2, CH], F16)
        v_out = sb("v_out", [P, NV, D], F32)
        prod = stack.enter_context(nc.psum_tensor("prod", [P, NB, CH], F32))
        w_loaded = sems(nc, stack, "w_loaded", 3)
        w_hi_ready, w_lo_ready = (stack.enter_context(nc.semaphore(s)) for s in ("w_hi_ready", "w_lo_ready"))
        x_loaded = sems(nc, stack, "x_loaded", NU)
        qk_stored, v_stored = sems(nc, stack, "qk_stored", NQ), sems(nc, stack, "v_stored", NV)
        x_hi_ready = Count(nc, stack, "x_hi_ready", NU)
        x_lo_ready = Count(nc, stack, "x_lo_ready", NU)
        prod_ready = Count(nc, stack, "prod_ready", NU * PER)
        hi_ready = Count(nc, stack, "hi_ready", NU * OT)
        prod_read = Count(nc, stack, "prod_read", NU * PER)
        block = stack.enter_context(nc.Block())

        @block.sync
        def _(sp):
            def load(i, u):
                sp.wait_ge(x_lo_ready.sem, x_lo_ready.at(i, u - NU))
                sp.dma_start(x_raw[:, u], xT[:, bass.ds((NU * i + u) * CH, CH)].rearrange(
                    "(t p) n -> p t n", p=P)).then_inc(x_loaded[u], 16)

            def store(i, u):
                at = (NU * i + u) * CH
                for o in range(OT):
                    sp.wait_ge(prod_read.sem, prod_read.at(i, u * PER + o))
                    parts = q_parts if o < KT else k_parts
                    f = (o % KT) * P
                    sp.dma_start(parts[:, f:f + P, bass.ds(at, CH)].rearrange("s p n -> p s n"),
                                 qk_out[:, o % NQ]).then_inc(qk_stored[o % NQ], 16)
                for j in range(TT):
                    sp.wait_ge(prod_read.sem, prod_read.at(i, u * PER + OT + j))
                    sp.dma_start(v_rows[bass.ds(at + j * P, P), :], v_out[:, j % NV]).then_inc(v_stored[j % NV], 16)

            start_stored(sp, qk_stored, v_stored)
            for n in range(3):
                cols = slice(n * D, (n + 1) * D)
                sp.dma_start(w_raw[:, :, cols], wqkvT[:, cols].rearrange("(t p) n -> p t n", p=P)).then_inc(
                    w_loaded[n], 16)
                if n < NU:
                    load(0, n)
            with sp.Fori(0, LAPS - 1) as i:
                for u in range(NU):
                    store(i, u)
                    load(i + 1, u)
            for u in range(NU):
                store(LAPS - 1, u)
            for s in qk_stored:
                sp.wait_ge(s, stored_at(QL * LAPS))
            for s in v_stored:
                sp.wait_ge(s, stored_at(VL * LAPS))

        @block.scalar
        def _(act):
            x_hi_ready.lead(act)
            hi_ready.lead(act)

            def weights(n):
                act.wait_ge(w_loaded[n], 16)
                cols = slice(n * D, (n + 1) * D)
                nc.scalar.activation(w_parts[0][:, :, cols], w_raw[:, :, cols], ACT.Copy,
                                     scale=WS).then_inc(w_hi_ready, 1)

            def x_hi(i, u):
                act.wait_ge(x_loaded[u % NU], 16 * (i + u // NU) + 16)
                act.wait_ge(prod_ready.sem, prod_ready.at(i, (u - NU) * PER + PER - 1))
                nc.scalar.activation(x_parts[0][:, u % NU], x_raw[:, u % NU], ACT.Copy,
                                     scale=XS).then_inc(x_hi_ready.sem, 1)

            def chunk(i, u, last):
                for o in range(OT):
                    k = u * PER + o
                    act.wait_ge(prod_ready.sem, prod_ready.at(i, k))
                    act.wait_ge(qk_stored[o % NQ], stored_at(QL * i + (u * OT + o) // NQ))
                    nc.scalar.activation(qk_out[:, o % NQ, 0], prod[:, k % NB], ACT.Copy,
                                         scale=UN * XS).then_inc(hi_ready.sem, 1)
                    if o == OT // 2 - 1 and not last:
                        x_hi(i, u + 1)

            weights(0)
            x_hi(0, 0)
            weights(1)
            weights(2)
            with act.Fori(0, LAPS - 1) as i:
                for u in range(NU):
                    chunk(i, u, False)
            for u in range(NU):
                chunk(LAPS - 1, u, u == NU - 1)

        @block.vector
        def _(dve):
            x_lo_ready.lead(dve)
            prod_read.lead(dve)

            def weights(n):
                dve.wait_ge(w_hi_ready, n + 1)
                cols = slice(n * D, (n + 1) * D)
                nc.vector.scalar_tensor_tensor(w_parts[1][:, :, cols], w_raw[:, :, cols], WS, w_parts[0][:, :, cols],
                                               ALU.mult, ALU.subtract).then_inc(w_lo_ready, 1)

            def x_lo(i, u):
                dve.wait_ge(x_hi_ready.sem, x_hi_ready.at(i, u))
                nc.vector.scalar_tensor_tensor(x_parts[1][:, u % NU], x_raw[:, u % NU], XS, x_parts[0][:, u % NU],
                                               ALU.mult, ALU.subtract).then_inc(x_lo_ready.sem, 1)

            def chunk(i, u, last):
                for o in range(OT):
                    k = u * PER + o
                    dve.wait_ge(hi_ready.sem, hi_ready.at(i, u * OT + o))
                    nc.vector.scalar_tensor_tensor(qk_out[:, o % NQ, 1], prod[:, k % NB], UN * XS,
                                                   qk_out[:, o % NQ, 0], ALU.mult,
                                                   ALU.subtract).then_inc(prod_read.sem, 1)
                    if o == OT // 2 and not last:
                        x_lo(i, u + 1)
                for j in range(TT):
                    k = u * PER + OT + j
                    dve.wait_ge(prod_ready.sem, prod_ready.at(i, k))
                    dve.wait_ge(v_stored[j % NV], stored_at(VL * i + (u * TT + j) // NV))
                    nc.vector.tensor_scalar(v_out[:, j % NV], prod[:, k % NB], UN, None,
                                            ALU.mult).then_inc(prod_read.sem, 1)

            weights(0)
            x_lo(0, 0)
            weights(1)
            weights(2)
            with dve.Fori(0, LAPS - 1) as i:
                for u in range(NU):
                    chunk(i, u, False)
            for u in range(NU):
                chunk(LAPS - 1, u, u == NU - 1)

        @block.tensor
        def _(pe):
            prod_ready.lead(pe)
            with pe.Fori(0, LAPS) as i:
                for u in range(NU):
                    pe.wait_ge(x_lo_ready.sem, x_lo_ready.at(i, u))
                    for m in range(PER):
                        k = u * PER + m
                        if m % KT == 0:
                            pe.wait_ge(w_lo_ready, m // KT + 1)
                        pe.wait_ge(prod_read.sem, prod_read.at(i, k - NB))
                        for s, (t, (a, b)) in enumerate((t, ab) for t in range(KT) for ab in TERMS):
                            if m < OT:
                                lhs, rhs = w_parts[a][:, t, m * P:(m + 1) * P], x_parts[b][:, u, t]
                            else:
                                j = m - OT
                                lhs, rhs = x_parts[a][:, u, t, j * P:(j + 1) * P], w_parts[b][:, t, 2 * D:3 * D]
                            last = nc.tensor.matmul(prod[:, k % NB], lhs, rhs, start=(s == 0), stop=(s == 3 * KT - 1))
                        last.then_inc(prod_ready.sem, 1)


def self_attention(nc, q_parts, k_parts, v_rows, o_parts, prefetch=()):
    NR = 3 * DH
    NM = NR + 2
    GROUPS = B * NG
    LAPS = GROUPS // 2
    KU = [(c, kt) for c in range(CPB) for kt in range((c + 1) * TT)]
    VU = [(c, kt, h) for c, kt in KU for h in range(HG)]
    AUX = []
    for c in range(CPB):
        AUX += [("max", c, (j, h, s)) for j in range(TT) for h in range(HG) for s in range(c + 1)] + [("rows", c, None)]
    NKU, NVU, NAUX = len(KU), len(VU), len(AUX)
    POOLED = [[n for n, (k, kt) in enumerate(KU) if k == c and kt < c * TT and kt % 3 != 2]
              for c in range(CPB)]
    ADDS = [n for tiles in POOLED for n in tiles[1:]]
    NP = 5
    RING = 3
    PIECES = 4
    VALUES, SUMS = 4, 6
    TAKEN = VALUES + 1, SUMS + 1
    RECIPS = [SUMS + 3 + 2 * n for n in range(PIECES)]
    SCALED = RECIPS[-1] + 1
    STORED = SCALED + 4
    TAIL = STORED + 1
    READY = 6
    SCALE = DH ** -0.5 / QK
    LAST_TILE = [max(n for n, k in enumerate(KU) if k[0] == c) for c in range(CPB)]
    CHUNK_OF = {t: c for c, t in enumerate(LAST_TILE)}

    def schedule():
        off = lambda c, kt: max(kt - c * TT, 0) * P
        steps = [0.06 + 0.6 * (CH - off(c, kt)) / CH for c, kt, _ in VU]
        busy = [0.0] * NVU
        for t in LAST_TILE:
            for lag in RECIPS:
                busy[(t * HG + HG - 1 + lag) % NVU] += 0.85
        cost = []
        for what, c, unit in AUX:
            if what == "rows":
                cost.append(2.4)
            else:
                j, _, s = unit
                cost.append(0.06 + 0.53 * (1.0 if s < c else (j + 1) / TT))
        rate = (sum(cost) + sum(busy)) / sum(steps)
        ends = [sum(cost[:n + 1]) for n in range(NAUX)]
        spent = [sum(rate * a - b for a, b in zip(steps[:u], busy[:u])) for u in range(NVU + 1)]

        def done(u, lead):
            t = spent[u % NVU] + lead + (u // NVU) * ends[-1]
            laps, rest = divmod(t, ends[-1])
            return int(laps) * NAUX + sum(e <= rest + 1e-9 for e in ends)

        lead = 0.0
        starts = [min(n for n, v in enumerate(VU) if v[0] == c) for c in range(CPB)]
        turns = [n for n, x in enumerate(AUX) if x[0] == "rows"]
        while any(done(starts[c] - READY, lead) <= turns[c] for c in range(CPB)):
            lead += 0.2
        most = 0
        out = []
        for u in range(NVU + 1):
            most = max(most, done(u, lead))
            out.append(most)
        out[NVU] = out[0] + NAUX
        return out

    DONE = schedule()

    def done_by(p):
        return DONE[p % NVU] + p // NVU * NAUX

    def before(n, ring, per):
        k = n % per
        return n - ring if k >= ring else n - k - 1 - (per - 1 - k) % ring

    def adds_upto(k):
        return k // NKU * len(ADDS) + sum(
            max(sum(n <= k % NKU for n in tiles[1:]), tiles[0] <= k % NKU) for tiles in POOLED if tiles)

    def laps(engine, step):
        for s in range(TAIL):
            step(0, s, 0, None)
        with engine.Fori(0, LAPS - 1) as i:
            for s in range(TAIL, TAIL + 2 * NVU):
                step(i, s, None, None)
        for s in range(TAIL, TAIL + 2 * NVU):
            step(LAPS - 1, s, None, 2 * NVU)

    def unit_at(s, lag, first, end):
        p = s - lag
        return None if (first is not None and p < first) or (end is not None and p >= end) else p

    def tile_at(s, lag, first, end):
        p = unit_at(s, lag, first, end)
        return p // HG if p is not None and p % HG == HG - 1 else None

    def chunk_at(s, lag, first, end):
        k = tile_at(s, lag, first, end)
        return k // NKU * CPB + CHUNK_OF[k % NKU] if k is not None and k % NKU in CHUNK_OF else None

    AHEAD = AUX.index(("rows", 0, None)) + 10

    def aux_at(s, first, end):
        if first is not None:
            reached = [AHEAD + (done_by(TAIL) - AHEAD) * n // TAIL for n in (s, s + 1)]
        else:
            reached = done_by(s), done_by(s + 1)
        return [n for n in range(*reached) if end is None or n < 2 * NAUX]

    with ExitStack() as stack:
        sb = lambda *a: stack.enter_context(nc.sbuf_tensor(*a))
        ps = lambda *a: stack.enter_context(nc.psum_tensor(*a))
        q_pair = [sb(f"q_pair{a}", [NM, HG, T], F16) for a in range(2)]
        k_pair = [sb(f"k_pair{a}", [NM, HG, T], F16) for a in range(2)]
        v_sb = [sb(f"v_sb{a}", [P, T // P, P], F32) for a in range(2)]
        probs = sb("probs", [P, NP, HG, CH], F32)
        total = sb("total", [P, HG, CH], F32)
        ones = sb("ones", [P, DH], F32)
        ident_f = sb("ident_f", [P, P], F32)
        ident = sb("ident_bf", [P, P], BF16)
        ident16 = sb("ident16", [P, P], F16)
        future_f = sb("future_f", [P, 2, P], F32)
        future = sb("future", [P, 2, P], BF16)
        seg_max = sb("seg_max", [P, HG, TT, CPB], F32)
        row_max = sb("row_max", [P, HG, TT], F32)
        max_parts = sb("max_parts", [P, 2, HG, TT], F16)
        max_rows = sb("max_rows", [2 * HG, 2, CH], F16)
        o_raw = sb("o_raw", [P, CH], F32)
        den = sb("den", [P, CH], F32)
        o_sb = sb("o_sb", [P, CH], F32)
        o_out = sb("o_out", [P, 2, 2, CH], F16)
        st_ps = ps("st_ps", [P, RING, CH], F32)
        s_ps = ps("s_ps", [P, RING, CH], F32)
        o_ps = ps("o_ps", [P, CH], F32)
        den_ps = ps("den_ps", [P, CH], F32)
        made, const_ready, factors_ready = (stack.enter_context(nc.semaphore(s)) for s in
                                            ("made", "const_ready", "factors_ready"))
        qk_loaded = [sems(nc, stack, f"qk_loaded{a}_", CPB) for a in range(2)]
        v_loaded = sems(nc, stack, "v_loaded", 2)
        o_stored = sems(nc, stack, "o_stored", 2)
        rows_moved = sems(nc, stack, "rows_moved", 2)
        st_ready = Count(nc, stack, "st_ready", 2 * NVU)
        exp_done = Count(nc, stack, "exp_done", 2 * NVU)
        pv_done = Count(nc, stack, "pv_done", 2 * NKU)
        o_ready = Count(nc, stack, "o_ready", 2 * CPB)
        o_taken = Count(nc, stack, "o_taken", 2 * CPB)
        den_taken = Count(nc, stack, "den_taken", 2 * CPB)
        added = Count(nc, stack, "added", 2 * len(ADDS))
        s_ready = Count(nc, stack, "s_ready", 2 * NAUX)
        s_read = Count(nc, stack, "s_read", 2 * NAUX)
        max_ready = Count(nc, stack, "max_ready", 2 * CPB)
        steps = Count(nc, stack, "steps", 2 * 2 * CPB)
        recips = Count(nc, stack, "recips", 2 * CPB * PIECES)
        scaled = Count(nc, stack, "scaled", 2 * CPB)
        o_hi_done = Count(nc, stack, "o_hi_done", 2 * CPB)
        split_done = Count(nc, stack, "split_done", 2 * CPB)
        block = stack.enter_context(nc.Block())

        @block.gpsimd
        def _(pool):
            nc.gpsimd.memset(ones[:], 1.0).then_inc(made, 1)
            nc.gpsimd.memset(ident_f[:], 0.0).then_inc(made, 1)
            nc.gpsimd.memset(future_f[:], 0.0).then_inc(made, 1)
            pool.wait_ge(made, 3)
            nc.gpsimd.affine_select(out=ident_f[:], in_=ident_f[:], compare_op=ALU.not_equal, fill=1.0, base=0,
                                    pattern=[[-1, P]], channel_multiplier=1).then_inc(made, 1)
            for n, sign in enumerate((1, -1)):
                nc.gpsimd.affine_select(out=future_f[:, n], in_=future_f[:, n], compare_op=ALU.is_ge, fill=MASKED,
                                        base=0, pattern=[[-sign, P]], channel_multiplier=sign).then_inc(made, 1)
            pool.wait_ge(made, 6)
            nc.gpsimd.tensor_copy(ident[:], ident_f[:]).then_inc(const_ready, 1)
            nc.gpsimd.tensor_copy(ident16[:], ident_f[:]).then_inc(const_ready, 1)
            nc.gpsimd.tensor_copy(future[:], future_f[:]).then_inc(const_ready, 1)
            pool.wait_ge(const_ready, 3)
            nc.gpsimd.memset(k_pair[0][NR:NM], QK).then_inc(factors_ready, 1)
            pool.wait_ge(factors_ready, 1)
            nc.gpsimd.memset(k_pair[1][NR:NM], QK).then_inc(factors_ready, 1)
            pool.wait_ge(factors_ready, 2)
            added.lead(pool)
            scaled.lead(pool)
            split_done.lead(pool)

            def step(i, s, first, end):
                k = tile_at(s, 1, first, end)
                if k is not None and k % NKU in ADDS:
                    c, n = KU[k % NKU][0], adds_upto(k) - 1
                    starts = k % NKU == POOLED[c][1]
                    pool.wait_ge(exp_done.sem, exp_done.at(i, HG * k + HG - 1))
                    if starts:
                        pool.wait_ge(pv_done.sem, pv_done.at(i, k // NKU * NKU + LAST_TILE[c - 1]))
                        other = probs[:, (k // NKU * NKU + POOLED[c][0]) % NP]
                    else:
                        pool.wait_ge(added.sem, added.at(i, n - 1))
                        other = total[:]
                    nc.gpsimd.tensor_tensor(total[:], other, probs[:, k % NP], ALU.add).then_inc(added.sem, 1)
                c = chunk_at(s, SCALED, first, end)
                if c is not None:
                    pool.wait_ge(recips.sem, recips.at(i, c * PIECES + PIECES - 1))
                    pool.wait_ge(split_done.sem, split_done.at(i, c - 1))
                    nc.gpsimd.tensor_tensor(o_sb[:], o_raw[:], den[:], ALU.mult).then_inc(scaled.sem, 1)
                c = chunk_at(s, SCALED + 3, first, end)
                if c is not None:
                    pool.wait_ge(o_hi_done.sem, o_hi_done.at(i, c))
                    nc.gpsimd.tensor_tensor(o_out[:, c % 2, 1], o_sb[:], o_out[:, c % 2, 0],
                                            ALU.subtract).then_inc(split_done.sem, 1)

            laps(pool, step)

        @block.sync
        def _(sp):
            def load(g, a, c):
                b, f = g // NG, (g % NG) * P
                cols = bass.ds(b * T + c * CH, CH)
                for pair, parts, order in ((k_pair[a], k_parts, (0, 0, 1)), (q_pair[a], q_parts, (0, 1, 0))):
                    for r, part in enumerate(order):
                        sp.dma_start(pair[r * DH:(r + 1) * DH, :, c * CH:(c + 1) * CH],
                                     parts[part, bass.ds(f, P), cols].rearrange("(h p) n -> p h n", p=DH)).then_inc(
                                         qk_loaded[a][c], 16)
                if c == CPB - 1:
                    sp.dma_start(v_sb[a][:], v_rows[bass.ds(b * T, T), bass.ds(f, P)].rearrange(
                        "(t p) f -> p t f", p=P)).then_inc(v_loaded[a], 16)

            def turn(i, n):
                c = n // NAUX * CPB + AUX[n % NAUX][1]
                sp.wait_ge(s_read.sem, s_read.at(i, n))
                at = c % CPB * CH
                for part in range(2):
                    sp.dma_start(q_pair[c // CPB % 2][NR + part:NR + part + 1, :, at:at + CH],
                                 max_rows[part * HG:(part + 1) * HG, c % 2]).then_inc(rows_moved[c % 2], 16)

            def step(i, s, first, end):
                for n in aux_at(s, first, end):
                    if AUX[n % NAUX][0] == "rows":
                        turn(i, n)
                if first is not None and s == TAIL - 1:
                    for dst, src, loaded in prefetch:
                        sp.dma_start(dst, src).then_inc(loaded, 16)
                k = tile_at(s, SUMS, first, end)
                if k is not None and k % NKU == NKU - 1 and end is None:
                    sp.wait_ge(pv_done.sem, pv_done.at(i, k))
                    for c in range(CPB):
                        load(2 * i + k // NKU + 2, k // NKU % 2, c)
                c = chunk_at(s, STORED, first, end)
                if c is not None:
                    sp.wait_ge(split_done.sem, split_done.at(i, c))
                    g = 2 * i + c // CPB
                    b, f = g // NG, (g % NG) * P
                    sp.dma_start(o_parts[:, bass.ds(f, P), bass.ds(b * T + c % CPB * CH, CH)].rearrange(
                        "s p n -> p s n"), o_out[:, c % 2]).then_inc(o_stored[c % 2], 16)

            start_stored(sp, o_stored, rows_moved)
            for c in range(CPB):
                load(0, 0, c)
            for n in range(AHEAD):
                if AUX[n][0] == "rows":
                    turn(0, n)
            for c in range(CPB):
                load(1, 1, c)
            laps(sp, step)
            for a in range(2):
                sp.wait_ge(o_stored[a], stored_at(CPB * LAPS))
                sp.wait_ge(rows_moved[a], stored_at(2 * CPB * LAPS))

        @block.scalar
        def _(act):
            exp_done.lead(act)
            o_taken.lead(act)
            den_taken.lead(act)

            def step(i, s, first, end):
                p = unit_at(s, 0, first, end)
                if p is not None:
                    c, kt, h = VU[p % NVU]
                    off = max(kt - c * TT, 0) * P
                    k = p // HG
                    act.wait_ge(st_ready.sem, st_ready.at(i, p))
                    if h == 0:
                        act.wait_ge(pv_done.sem, pv_done.at(i, k - NP))
                        act.wait_ge(added.sem, added.at(i, adds_upto(k - NP) - 1))
                    nc.scalar.activation(probs[:, k % NP, h, off:], st_ps[:, p % (2 * NVU) % RING, off:], ACT.Exp,
                                         scale=SCALE).then_inc(exp_done.sem, 1)
                c = chunk_at(s, TAKEN[0], first, end)
                if c is not None:
                    act.wait_ge(o_ready.sem, o_ready.at(i, c))
                    act.wait_ge(scaled.sem, scaled.at(i, c - 1))
                    nc.scalar.activation(o_raw[:], o_ps[:], ACT.Copy).then_inc(o_taken.sem, 1)
                c = chunk_at(s, TAKEN[1], first, end)
                if c is not None:
                    act.wait_ge(pv_done.sem, pv_done.at(i, c // CPB * NKU + LAST_TILE[c % CPB]))
                    nc.scalar.activation(den[:], den_ps[:], ACT.Copy, scale=1.0 / XS).then_inc(den_taken.sem, 1)

            laps(act, step)

        @block.vector
        def _(dve):
            for count in (s_read, max_ready, steps, recips, o_hi_done):
                count.lead(dve)

            def aux(i, n):
                what, c, unit = AUX[n % NAUX]
                slot = n % (2 * NAUX) % RING
                k = n // NAUX * CPB + c
                dve.wait_ge(s_ready.sem, s_ready.at(i, n))
                if what == "rows":
                    dve.wait_ge(rows_moved[k % 2], stored_at(2 * (CPB * i + k // 2)))
                    nc.vector.tensor_copy(max_rows[:, k % 2], s_ps[0:2 * HG, slot]).then_inc(s_read.sem, 1)
                    return
                j, h, s = unit
                width = CH if s < c else (j + 1) * P
                nc.vector.reduce_max(seg_max[:, h, j, s:s + 1], s_ps[:, slot, 0:width], AX.X).then_inc(s_read.sem, 1)
                if AUX[(n + 1) % NAUX][0] == "rows":
                    dve.wait_ge(s_read.sem, s_read.at(i, n))
                    nc.vector.reduce_max(row_max[:], seg_max[:, :, :, 0:c + 1], AX.X).then_inc(steps.sem, 1)
                    dve.wait_ge(steps.sem, steps.at(i, 2 * k))
                    nc.vector.tensor_scalar(max_parts[:, 0], row_max[:], -1.0 / QK, None,
                                            ALU.mult).then_inc(steps.sem, 1)
                    dve.wait_ge(steps.sem, steps.at(i, 2 * k + 1))
                    nc.vector.scalar_tensor_tensor(max_parts[:, 1], row_max[:], -1.0 / QK, max_parts[:, 0], ALU.mult,
                                                   ALU.subtract).then_inc(max_ready.sem, 1)

            def step(i, s, first, end):
                for n in aux_at(s, first, end):
                    aux(i, n)
                for n, lag in enumerate(RECIPS):
                    c = chunk_at(s, lag, first, end)
                    if c is not None:
                        if n == 0:
                            dve.wait_ge(den_taken.sem, den_taken.at(i, c))
                        piece = den[:, n * CH // PIECES:(n + 1) * CH // PIECES]
                        nc.vector.reciprocal(piece, piece).then_inc(recips.sem, 1)
                c = chunk_at(s, SCALED + 2, first, end)
                if c is not None:
                    dve.wait_ge(scaled.sem, scaled.at(i, c))
                    dve.wait_ge(o_stored[c % 2], stored_at(CPB * i + c // 2))
                    nc.vector.tensor_copy(o_out[:, c % 2, 0], o_sb[:]).then_inc(o_hi_done.sem, 1)

            for n in range(AHEAD):
                aux(0, n)
            laps(dve, step)

        @block.tensor
        def _(pe):
            for count in (st_ready, pv_done, o_ready, s_ready):
                count.lead(pe)

            def aux(i, n):
                what, c, unit = AUX[n % NAUX]
                k = n // NAUX * CPB + c
                slot, a = n % (2 * NAUX) % RING, k // CPB % 2
                pe.wait_ge(s_read.sem, s_read.at(i, before(n, RING, 2 * NAUX)))
                if what == "rows":
                    pe.wait_ge(max_ready.sem, max_ready.at(i, k))
                    for j in range(TT):
                        last = nc.tensor.matmul(s_ps[0:2 * HG, slot, j * P:(j + 1) * P], max_parts[:, :, :, j],
                                                ident16[:], start=(j == 0), stop=(j == TT - 1), skip_group_check=True)
                    last.then_inc(s_ready.sem, 1)
                    return
                j, h, s = unit
                if j == h == s == 0:
                    pe.wait_ge(qk_loaded[a][c], 6 * 16 * (i + k // (2 * CPB) + 1))
                width = CH if s < c else (j + 1) * P
                q0 = c * CH + j * P
                diagonal = s == c
                last = nc.tensor.matmul(s_ps[:, slot, 0:width], q_pair[a][0:NR, h, q0:q0 + P],
                                        k_pair[a][0:NR, h, s * CH:s * CH + width], start=True, stop=not diagonal)
                if diagonal:
                    last = nc.tensor.matmul(s_ps[:, slot, width - P:width], ident[:], future[:, 0],
                                            start=False, stop=True)
                last.then_inc(s_ready.sem, 1)

            def scores(i, p):
                c, kt, h = VU[p % NVU]
                a, slot = p // NVU % 2, p % (2 * NVU) % RING
                if kt == h == 0:
                    k = p // NVU * CPB + c
                    pe.wait_ge(rows_moved[k % 2], stored_at(2 * (CPB * i + k // 2 + 1)))
                off = max(kt - c * TT, 0) * P
                pe.wait_ge(exp_done.sem, exp_done.at(i, before(p, RING, 2 * NVU)))
                diagonal = kt >= c * TT
                last = nc.tensor.matmul(st_ps[:, slot, off:], k_pair[a][:, h, kt * P:(kt + 1) * P],
                                        q_pair[a][:, h, c * CH + off:(c + 1) * CH], start=True, stop=not diagonal)
                if diagonal:
                    last = nc.tensor.matmul(st_ps[:, slot, off:off + P], ident[:], future[:, 1], start=False, stop=True)
                last.then_inc(st_ready.sem, 1)

            heads = [slice(h * DH, (h + 1) * DH) for h in range(HG)]

            def values(i, k):
                c, kt = KU[k % NKU]
                a, off = k // NKU % 2, max(kt - c * TT, 0) * P
                final = k % NKU == LAST_TILE[c]
                if kt == 0:
                    if c == 0:
                        pe.wait_ge(v_loaded[a], 16 * (i + k // (2 * NKU) + 1))
                    pe.wait_ge(o_taken.sem, o_taken.at(i, k // NKU * CPB + c - 1))
                pe.wait_ge(exp_done.sem, exp_done.at(i, HG * k + HG - 1))
                for h, out in enumerate(heads):
                    last = nc.tensor.matmul(o_ps[out, off:], v_sb[a][:, kt, out], probs[:, k % NP, h, off:],
                                            start=(kt == 0), stop=final)
                if k % NKU in POOLED[c]:
                    last.then_inc(pv_done.sem, 1)
                elif final:
                    last.then_inc(o_ready.sem, 1)

            def sums(i, k):
                c, kt = KU[k % NKU]
                off, pooled = max(kt - c * TT, 0) * P, POOLED[c]
                final = k % NKU == LAST_TILE[c]
                if k % NKU in pooled:
                    return
                opens = all(n in pooled for n, (x, _) in enumerate(KU) if x == c and n < k % NKU)
                if opens:
                    pe.wait_ge(den_taken.sem, den_taken.at(i, k // NKU * CPB + c - 1))
                for h, out in enumerate(heads):
                    last = nc.tensor.matmul(den_ps[out, off:], ones[:], probs[:, k % NP, h, off:], start=opens,
                                            stop=final and not pooled)
                if final and pooled:
                    pe.wait_ge(added.sem, added.at(i, adds_upto(k) - 1))
                    for h, out in enumerate(heads):
                        last = nc.tensor.matmul(den_ps[out, :], ones[:], total[:, h], start=False, stop=True)
                last.then_inc(pv_done.sem, 1)

            def step(i, s, first, end):
                p = unit_at(s, 0, first, end)
                if p is not None:
                    scores(i, p)
                todo = aux_at(s, first, end)
                for n in todo[:1]:
                    aux(i, n)
                k = tile_at(s, VALUES, first, end)
                if k is not None:
                    values(i, k)
                k = tile_at(s, SUMS, first, end)
                if k is not None:
                    sums(i, k)
                for n in todo[1:]:
                    aux(i, n)

            pe.wait_ge(const_ready, 3)
            for n in range(AHEAD):
                aux(0, n)
            pe.wait_ge(factors_ready, 2)
            laps(pe, step)


def load_rows(sp, W, S, x_rows, o_parts, n):
    rows = bass.ds(n * CH, CH)
    sp.dma_start(W["x1"][:], x_rows[rows, :].rearrange("(j p) d -> p j d", p=P)).then_inc(S["x_loaded"], 16)
    sp.dma_start(W["oT"][:], o_parts[:, :, rows].rearrange("s (t p) n -> p s t n", p=P)).then_inc(S["oT_loaded"], 16)


def context_blocks(W):
    return W["soft"][:].rearrange("p j h s -> p (j h s)")[:, 0:B * NG * HG * S2].rearrange(
        "p (b g n) -> p b g n", b=B, g=NG)


def prepare(nc, W, S, x_rows, o_parts, bk, bv, weights, centroids, routeT, bout, bo, bq, b1, b2):
    raws, raw_loaded = S["raws"], S["raw_loaded"]
    with ExitStack() as stack:
        sb = lambda *a: stack.enter_context(nc.sbuf_tensor(*a))
        sem = lambda s: stack.enter_context(nc.semaphore(s))
        t_ps = stack.enter_context(nc.psum_tensor("t_ps", [P, CH], F32))
        cent, cent_sq = sb("cent", [E, D], F32), sb("cent_sq", [E, D], F32)
        cent_ss = sb("cent_ss", [E, 1], F32)
        cent_rn = sb("cent_rn", [E, 1], F32)
        small, consts = sem("small_loaded"), sem("consts_made")
        hi_done = sem("hi_done")
        squared, norm_ready, cent_ready, cent_turned, route_ready = (
            sem(s) for s in ("squared", "norm_ready", "cent_ready", "cent_turned", "route_ready"))
        block = stack.enter_context(nc.Block())

        smalls = [(W["bk_sb"][:], bk), (W["bv_bc"][:], bv.partition_broadcast(S2)), (cent[:], centroids),
                  (W["route_raw"][:, :, E:2 * E], routeT.rearrange("(t p) e -> p t e", p=P)),
                  (W["bout_bc"][:], bout.partition_broadcast(P)), (W["bo_bc"][:], bo.partition_broadcast(P)),
                  (W["bq_sb"][:], bq), (W["b1_sb"][:], b1), (W["b2_sb"][:], b2)]

        @block.sync
        def _(sp):
            for dst, src in smalls:
                sp.dma_start(dst, src).then_inc(small, 16)
            load_rows(sp, W, S, x_rows, o_parts, 0)

        @block.gpsimd
        def _(pool):
            nc.gpsimd.memset(W["ident"][:], 0.0).then_inc(consts, 1)
            nc.gpsimd.memset(W["power"][:], -0.5).then_inc(consts, 1)
            pool.wait_ge(consts, 2)
            nc.gpsimd.affine_select(out=W["ident"][:], in_=W["ident"][:], compare_op=ALU.not_equal, fill=1.0, base=0,
                                    pattern=[[-1, P]], channel_multiplier=1).then_inc(consts, 1)
            pool.wait_ge(squared, 2)
            nc.gpsimd.tensor_tensor(cent_rn[:], cent_ss[:], W["power"][0:E, 0:1], ALU.pow).then_inc(norm_ready, 1)

        @block.scalar
        def _(act):
            for n in range(2, len(raws)):
                act.wait_ge(raw_loaded[n], 16)
                nc.scalar.activation(weights[n - 2][0], raws[n], ACT.Copy, scale=WS).then_inc(hi_done, 1)
            act.wait_ge(small, 16 * len(smalls))
            nc.scalar.activation(cent_sq[:], cent[:], ACT.Square, accum_out=cent_ss[:]).then_inc(squared, 1)

        @block.vector
        def _(dve):
            nc.vector.memset(context_blocks(W), 0.0)
            for n in range(2, len(raws)):
                dve.wait_ge(hi_done, n - 1)
                nc.vector.scalar_tensor_tensor(weights[n - 2][1], raws[n], WS, weights[n - 2][0], ALU.mult,
                                               ALU.subtract)
            dve.wait_ge(squared, 1)
            nc.vector.tensor_scalar(cent_ss[:], cent_ss[:], 1e-24, None, ALU.max).then_inc(squared, 1)
            dve.wait_ge(norm_ready, 1)
            nc.vector.tensor_scalar(cent[:], cent[:], cent_rn[:], None, ALU.mult).then_inc(cent_ready, 1)
            dve.wait_ge(cent_turned, 1)
            nc.vector.tensor_copy(W["route_raw"][:, :, 0:E], t_ps[:, 0:KT * E].rearrange(
                "p (t e) -> p t e", t=KT)).then_inc(route_ready, 1)
            dve.wait_ge(route_ready, 1)
            nc.vector.tensor_scalar(W["route_p"][0][:], W["route_raw"][:], WS, None, ALU.mult).then_inc(route_ready, 1)
            dve.wait_ge(route_ready, 2)
            nc.vector.scalar_tensor_tensor(W["route_p"][1][:], W["route_raw"][:], WS, W["route_p"][0][:], ALU.mult,
                                           ALU.subtract).then_inc(route_ready, 1)

        @block.tensor
        def _(pe):
            pe.wait_ge(consts, 3)
            pe.wait_ge(cent_ready, 1)
            for t in range(KT):
                last = nc.tensor.transpose(t_ps[:, t * E:(t + 1) * E], cent[:, t * P:(t + 1) * P],
                                           W["ident"][0:E, 0:E])
            last.then_inc(cent_turned, 1)


def chains(nc, W, S, weights, x_rows, o_parts, mask, k_blocks, v_ctx, out):
    KS = HG * S2
    SCALE = DH ** -0.5
    USES = (["dve"] * TT + ["dve"] * TT + ["act"] * KT + ["dve"] * (TT * NG)
            + ["act"] * HG + (["act"] * HG + ["dve"]) * (NG - 1) + ["dve"] + ["dve"] * TT + ["dve"] * TT
            + ["dve"] + ["act"])
    AT_OUT, AT_T1, AT_Q = 0, TT, 2 * TT
    AT_S = AT_Q + KT
    AT_PV = AT_S + TT * NG
    AT_O = AT_PV + (HG + 1) * NG
    AT_TURN = [AT_PV + max(g * (HG + 1) - 1, 0) for g in range(NG)]
    AT_VAL = [AT_TURN[g + 1] + HG for g in range(NG - 1)] + [AT_O - 1]
    AT_T2 = AT_O + TT
    AT_R = AT_T2 + TT
    AT_G = AT_R + 1
    NUSE, CB, FB = len(USES), 4, 4
    UNITS = []
    for e in range(E + 1):
        UNITS += [("hidden", e, n) for n in range(2) if e < E]
        UNITS += [("bias", 0, j) for j in range(TT) if e == 1] + [("expert", e - 1, j) for j in range(TT) if e > 0]
    NUNIT = len(UNITS)
    F_USES = ["act" if kind == "hidden" else "dve" for kind, _, _ in UNITS]
    assert 2 * NUSE % CB == 0 and 2 * NUNIT % FB == 0
    PLAN = [("out", 1), ("norm1", 2), ("turn1", 3), ("query", 1), ("scores0", 3), ("scores1", 7), ("scores2", 7),
            ("scores3", 6), ("probs0", 0), ("probs1", 1), ("pv0", 1), ("probs2", 0), ("pv1", 1), ("probs3", 0),
            ("pv2", 3), ("pv3", 1), ("out2", 6), ("norm2", 3), ("turn2", 2), ("route", 4), ("gate", 0)]
    STAGES, FILL = zip(*PLAN)
    assert sum(FILL) == NUNIT
    FROM = [sum(FILL[:n]) for n in range(len(FILL))]
    APART = {"query": 3, "probs0": 2, "out2": 3}
    assert sum(APART.values()) == len(weights)
    LOOPED = (NC - 2) // 2

    x1, x2, x2T, oT, soft, hT, hidden = (W[k] for k in ("x1", "x2", "x2T", "oT", "soft", "hT", "hidden"))
    x1T = W["work"][:, 0].bitcast(F16).rearrange("p (s t n) -> p s t n", s=2, t=KT)
    xq = W["work"][:, 1].rearrange("p (t n) -> p t n", t=KT)
    ident, power = W["ident"], W["power"]
    raws = [x2[1][:].rearrange("p j n -> p (j n)"), x2T[1][:].rearrange("p s t n -> p (s t n)").bitcast(F32),
            hT[:].rearrange("p s e t n -> p (s e t n)").bitcast(F32)]

    def turned(g):
        return W["work"][0:S2, g % 2].rearrange("p (h n) -> p h n", h=HG)

    def nth(uses, k):
        return uses[:k].count(uses[k])

    with ExitStack() as stack:
        sb = lambda *a: stack.enter_context(nc.sbuf_tensor(*a))
        keys, vals = sb("keys", [P, NG, KS], F32), sb("vals", [S2, D], F32)
        mask_sb = sb("mask_sb", [P, S2], F32)
        stats, agg, rstd = sb("stats", [P, TT, 6], F32), sb("agg", [P, TT, 2], F32), sb("rstd", [P, TT], F32)
        stats3, agg3, rstd3 = sb("stats3", [P, TT, 6], F32), sb("agg3", [P, TT, 2], F32), sb("rstd3", [P, TT], F32)
        smax, ssum = sb("smax", [P, TT, H], F32), sb("ssum", [P, TT, H], F32)
        square, rnorm = sb("square", [P, TT], F32), sb("rnorm", [P, TT], F32)
        logit, weight = sb("logit", [P, TT, E], F32), sb("weight", [P, TT, E], F32)
        top, chosen, gsum = sb("top", [P, TT, 8], F32), sb("chosen", [P, TT, E], F32), sb("gsum", [P, TT], F32)
        gates = sb("gates", [P, TT, E], F32)
        gates_un = [sb(f"gates_un{a}", [P, TT, E], F32) for a in range(2)]
        gT = [sb(f"gT{a}", [E, TT, P], F32) for a in range(2)]
        cps = stack.enter_context(nc.psum_tensor("cps", [P, CB, CH], F32))
        fps = stack.enter_context(nc.psum_tensor("fps", [P, FB, CH], F32))

        def count(name, per):
            return Count(nc, stack, name, 2 * per)

        def sem(name):
            return stack.enter_context(nc.semaphore(name))

        x_loaded, oT_loaded, kv_loaded = S["x_loaded"], S["oT_loaded"], sem("kv_loaded")
        stored = sems(nc, stack, "stored", 2)
        raw_loaded = sems(nc, stack, "raw_w_loaded", len(raws))
        w_hi, w_lo = sem("expert_w_hi"), sem("expert_w_lo")
        kv_done, keys_done, vals_done, kv_stored = (sem(n) for n in ("kv_done", "keys_done", "vals_done", "kv_stored"))
        c_ready = count("c_ready", NUSE)
        act_read = count("act_read", USES.count("act"))
        dve_read = count("dve_read", USES.count("dve"))
        hi_ready = count("hi_ready", TT + NG + TT)
        biased = count("biased", 2)
        summed, spread, varied = count("summed", 2 * TT), count("spread", 2 * TT), count("varied", 2)
        rooted = count("rooted", 2)
        normed = count("normed", 2 * TT)
        masked = count("masked", 1)
        smaxed, shifted, exped = count("smaxed", TT), count("shifted", TT), count("exped", TT)
        ssummed, inverted, probs_ready = count("ssummed", TT), count("inverted", TT), count("probs_ready", TT)
        squared, square_held, norm_rooted = count("squared", TT), count("square_held", 1), count("norm_rooted", 1)
        routed = count("routed", 13)
        gate_exped, gated = count("gate_exped", 1), count("gated", 1)
        f_ready = count("f_ready", NUNIT)
        gelu_done = count("gelu_done", 2 * E)
        h_hi, h_lo = count("h_hi", 2 * E), count("h_lo", 2 * E)
        added = count("acc_added", TT * (E + 1))
        summed3, spread3, varied3 = count("summed3", TT), count("spread3", TT), count("varied3", 1)
        rooted3, normed3 = count("rooted3", 1), count("normed3", TT)
        block = stack.enter_context(nc.Block())

        def at(c, i, u, k):
            return c.at(i, u * (c.per // 2) + k)

        def chunk(i, u):
            return 2 * i + u + 1

        def parity(u):
            return 1 - u

        blocks, vals_made = context_blocks(W), hidden[0:S2]

        def key_product(g):
            return fps[:, g // 2, g % 2 * B * S2:(g % 2 + 1) * B * S2]

        def value_product(b):
            return fps[0:S2, NG // 2 + b]

        def program(chain, experts=None, finish=None, apart=None, context=None, after="turn1"):
            def slot(i, u, with_chain=True, with_experts=True):
                taken = 0
                for n, stage in enumerate(STAGES):
                    if apart and not with_experts:
                        for w in range(taken, taken + APART.get(stage, 0)):
                            apart(w, weights[w][1])
                        taken += APART.get(stage, 0)
                    if with_chain:
                        chain(i, u, stage)
                    if context and not with_experts and stage == after:
                        context()
                    if with_experts and experts:
                        for f in range(FROM[n], FROM[n] + FILL[n]):
                            experts(i, u, f, *UNITS[f])
                if with_experts and finish:
                    finish(i, u)
            return slot

        def run(engine, slot, weights_used=False):
            slot(-1, 1, with_experts=False)
            if weights_used:
                engine.wait_ge(w_lo, len(weights))
            with engine.Fori(0, LOOPED) as i:
                slot(i, 0)
                slot(i, 1)
            slot(LOOPED, 0)
            slot(LOOPED, 1, with_chain=False)

        def lead(engine, chain_counts, expert_counts):
            for c in chain_counts:
                c.lead(engine, made=c.per // 2)
            for c in expert_counts:
                c.lead(engine)

        @block.sync
        def _(sp):
            def load_context(n):
                b = n // CPB
                sp.dma_start(keys[:].rearrange("p g n -> p (g n)"), k_blocks[bass.ds(b, 1)].rearrange(
                    "b p n -> (b p) n")).then_inc(kv_loaded, 16)
                sp.dma_start(vals[:], v_ctx[bass.ds(b, 1)].rearrange("b p n -> (b p) n")).then_inc(kv_loaded, 16)
                sp.dma_start(mask_sb[:], mask[bass.ds(b, 1)].rearrange("b a c s -> (b a c s)").partition_broadcast(
                    P)).then_inc(kv_loaded, 16)

            def load_next(i, u):
                sp.wait_ge(dve_read.sem, at(dve_read, i, u, nth(USES, AT_O + TT - 1)))
                load_rows(sp, W, S, x_rows, o_parts, chunk(i, u) + 1)
                load_context(chunk(i, u) + 1)

            def store(i, u):
                sp.wait_ge(normed3.sem, at(normed3, i, u, TT - 1))
                sp.dma_start(out[bass.ds((chunk(i, u) - 1) * CH, CH), :].rearrange("(j p) d -> p j d", p=P),
                             x2[u][:]).then_inc(stored[u], 16)

            start_stored(sp, stored)
            for n, (src, _) in enumerate(weights):
                if n == len(raws):
                    sp.wait_ge(keys_done, NG * HG)
                    sp.dma_start(k_blocks.rearrange("b p n -> p b n"),
                                 blocks.rearrange("p b g n -> p b (g n)")).then_inc(kv_stored, 16)
                    sp.wait_ge(vals_done, B)
                    sp.dma_start(v_ctx.rearrange("b p n -> p b n"), vals_made).then_inc(kv_stored, 16)
                    sp.wait_ge(kv_stored, 32)
                    load_context(0)
                if n >= len(raws):
                    sp.wait_ge(w_lo, n - len(raws) + 1)
                sp.dma_start(raws[n % len(raws)].rearrange("p (a b) -> p a b", a=src.shape[1]), src).then_inc(
                    raw_loaded[n % len(raws)], 16)
            load_next(-1, 1)
            with sp.Fori(0, LOOPED) as i:
                for u in range(2):
                    load_next(i, u)
                    store(i, u)
            store(LOOPED, 0)
            store(LOOPED, 1)
            for s in stored:
                sp.wait_ge(s, stored_at(NC // 2))

        @block.gpsimd
        def _(pool):
            lead(pool, (biased, rooted, probs_ready, norm_rooted), (rooted3,))

            def add_row(row, c):
                nc.gpsimd.tensor_tensor(x1[:], x1[:], row[:].rearrange("p (a n) -> p a n", a=1).broadcast_to(
                    [P, TT, D]), ALU.add).then_inc(c.sem, 1)

            def root(var, c, width):
                nc.gpsimd.tensor_tensor(var, var, power[:, 0:width], ALU.pow).then_inc(c.sem, 1)

            def chain(i, u, stage):
                if stage == "out":
                    pool.wait_ge(x_loaded, 16 * (chunk(i, u) + 1))
                    add_row(W["bout_bc"], biased)
                    pool.wait_ge(varied.sem, at(varied, i, u, 0))
                    root(rstd[:], rooted, TT)
                elif stage == "turn1":
                    pool.wait_ge(c_ready.sem, at(c_ready, i, u, AT_T1 + TT - 1))
                    add_row(W["bo_bc"], biased)
                elif stage.startswith("scores"):
                    at_end = int(stage[-1])
                    for j in ([at_end - 1] if at_end else []) + ([at_end] if at_end == TT - 1 else []):
                        pool.wait_ge(inverted.sem, at(inverted, i, u, j))
                        nc.gpsimd.tensor_tensor(soft[:, j], soft[:, j], ssum[:, j, :].rearrange(
                            "p (h a) -> p h a", a=1).broadcast_to([P, H, S2]), ALU.mult).then_inc(probs_ready.sem, 1)
                elif stage == "out2":
                    pool.wait_ge(varied.sem, at(varied, i, u, 1))
                    root(rstd[:], rooted, TT)
                elif stage == "route":
                    pool.wait_ge(square_held.sem, at(square_held, i, u, 0))
                    nc.gpsimd.tensor_tensor(rnorm[:], square[:], power[:, 0:TT], ALU.pow).then_inc(norm_rooted.sem, 1)

            def finish(i, u):
                pool.wait_ge(varied3.sem, at(varied3, i, u, 0))
                root(rstd3[:], rooted3, TT)

            run(pool, program(chain, finish=finish))

        @block.scalar
        def _(act):
            lead(act, (act_read, hi_ready, exped, squared, gate_exped), (gelu_done,))

            def wait_product(i, u, k):
                act.wait_ge(c_ready.sem, at(c_ready, i, u, k))
                return cps[:, (u * NUSE + k) % CB]

            def chain(i, u, stage):
                p = parity(u)
                if stage in ("turn1", "turn2"):
                    k0, dst = (AT_T1, x1T) if stage == "turn1" else (AT_T2, x2T[p])
                    for j in range(TT):
                        bank = wait_product(i, u, k0 + j)
                        nc.scalar.activation(dst[:, 0, :, j * P:(j + 1) * P], bank.rearrange("p (t n) -> p t n", t=KT),
                                             ACT.Copy, scale=XS).then_inc(hi_ready.sem, 1)
                elif stage == "query":
                    for o in range(KT):
                        bank = wait_product(i, u, AT_Q + o)
                        nc.scalar.activation(xq[:, o], bank, ACT.Identity, bias=W["bq_sb"][:, o:o + 1],
                                             scale=UN).then_inc(act_read.sem, 1)
                elif stage.startswith("scores"):
                    j = int(stage[-1])
                    act.wait_ge(shifted.sem, at(shifted, i, u, j))
                    nc.scalar.activation(soft[:, j], soft[:, j], ACT.Exp).then_inc(exped.sem, 1)
                elif stage.startswith("probs"):
                    g = int(stage[-1])
                    for h in range(HG):
                        bank = wait_product(i, u, AT_TURN[g] + h)
                        nc.scalar.activation(turned(g)[:, h], bank[0:S2], ACT.Copy).then_inc(act_read.sem, 1)
                elif stage.startswith("pv"):
                    g = int(stage[-1])
                    bank = wait_product(i, u, AT_VAL[g])
                    nc.scalar.activation(oT[:, 0, g], bank, ACT.Copy, scale=XS).then_inc(hi_ready.sem, 1)
                elif stage == "route":
                    for j in range(TT):
                        act.wait_ge(normed.sem, at(normed, i, u, TT + j))
                        nc.scalar.activation(soft[:].rearrange("p j h s -> p (j h s)")[:, j * D:(j + 1) * D],
                                             x2[p][:, j], ACT.Square,
                                             accum_out=square[:, j:j + 1]).then_inc(squared.sem, 1)
                elif stage == "gate":
                    act.wait_ge(routed.sem, at(routed, i, u, 8))
                    nc.scalar.activation(weight[:], logit[:], ACT.Exp).then_inc(gate_exped.sem, 1)
                    bank = wait_product(i, u, AT_G)
                    nc.scalar.activation(gT[p][:], bank[0:E].rearrange("e (j n) -> e j n", j=TT),
                                         ACT.Copy).then_inc(act_read.sem, 1)

            def experts(i, u, f, kind, e, j):
                if kind == "hidden":
                    n = 2 * e + j
                    act.wait_ge(f_ready.sem, at(f_ready, i, u, f))
                    act.wait_ge(h_lo.sem, at(h_lo, i, u, n - 2))
                    nc.scalar.activation(hidden[:, n % 2], fps[:, (u * NUNIT + f) % FB], ACT.Gelu,
                                         bias=W["b1_sb"][:, n:n + 1], scale=UN).then_inc(gelu_done.sem, 1)

            def apart(n, dst):
                act.wait_ge(raw_loaded[n % len(raws)], 16 * (n // len(raws) + 1))
                nc.scalar.activation(dst[0], raws[n % len(raws)], ACT.Copy, scale=WS).then_inc(w_hi, 1)

            def context():
                act.wait_ge(kv_done, 1)
                for g in range(NG):
                    for h in range(HG):
                        rows = slice(h * DH, (h + 1) * DH)
                        nc.scalar.activation(blocks[rows, :, g, h * S2:(h + 1) * S2],
                                             key_product(g)[rows].rearrange("p (b s) -> p b s", b=B), ACT.Identity,
                                             bias=W["bk_sb"][rows, g:g + 1]).then_inc(keys_done, 1)

            run(act, program(chain, experts, apart=apart, context=context))

        @block.vector
        def _(dve):
            lead(dve, (dve_read, summed, spread, varied, normed, masked, smaxed, shifted, ssummed, inverted,
                       square_held, routed), (h_hi, h_lo, added, summed3, spread3, varied3, normed3))

            def wait_product(i, u, k):
                dve.wait_ge(c_ready.sem, at(c_ready, i, u, k))
                return cps[:, (u * NUSE + k) % CB]

            def lo_part(i, u, k, hi_index, dst, hi):
                bank = cps[:, (u * NUSE + k) % CB]
                if len(dst.shape) == 3:
                    bank = bank.rearrange("p (t n) -> p t n", t=KT)
                dve.wait_ge(hi_ready.sem, at(hi_ready, i, u, hi_index))
                nc.vector.scalar_tensor_tensor(dst, bank, XS, hi, ALU.mult, ALU.subtract).then_inc(dve_read.sem, 1)

            def spreads(rows, st, ag, rs, c, i, u, which, source, k0):
                c_sum, c_spread, c_var, _, _ = c
                for j in range(TT):
                    if j > 0:
                        dve.wait_ge(c_sum.sem, at(c_sum, i, u, which * TT + j - 1))
                    dve.wait_ge(source.sem, at(source, i, u, k0 + j))
                    nc.vector.bn_stats(st[:, j], rows[:, j]).then_inc(c_sum.sem, 1)
                    if j > 0:
                        nc.vector.bn_aggr(ag[:, j - 1], st[:, j - 1]).then_inc(c_spread.sem, 1)
                dve.wait_ge(c_sum.sem, at(c_sum, i, u, which * TT + TT - 1))
                dve.wait_ge(c_spread.sem, at(c_spread, i, u, which * TT + TT - 2))
                nc.vector.tensor_scalar(rs[:, 0:TT - 1], ag[:, 0:TT - 1, 1], EPS, None, ALU.add)
                nc.vector.bn_aggr(ag[:, TT - 1], st[:, TT - 1]).then_inc(c_spread.sem, 1)
                dve.wait_ge(c_spread.sem, at(c_spread, i, u, which * TT + TT - 1))
                nc.vector.tensor_scalar(rs[:, TT - 1:TT], ag[:, TT - 1:TT, 1], EPS, None,
                                        ALU.add).then_inc(c_var.sem, 1)

            def norm(rows, ag, rs, c, i, u, which):
                c_root, c_norm = c[3:]
                dve.wait_ge(c_root.sem, at(c_root, i, u, which))
                for j in range(TT):
                    nc.vector.tensor_scalar(rows[:, j], rows[:, j], ag[:, j, 0:1], rs[:, j:j + 1], ALU.subtract,
                                            ALU.mult).then_inc(c_norm.sem, 1)

            chain_norm = (summed, spread, varied, rooted, normed)

            def softmax_start(i, u, j):
                for g in range(NG):
                    bank = wait_product(i, u, AT_S + j * NG + g)
                    nc.vector.scalar_tensor_tensor(
                        soft[:, j, g * HG:(g + 1) * HG], bank[:, 0:KS].rearrange("p (h s) -> p h s", h=HG), SCALE,
                        mask_sb[:].rearrange("p (a s) -> p a s", a=1).broadcast_to([P, HG, S2]), ALU.mult,
                        ALU.add).then_inc(dve_read.sem, 1)
                dve.wait_ge(dve_read.sem, at(dve_read, i, u, nth(USES, AT_S + j * NG + NG - 1)))
                nc.vector.reduce_max(smax[:, j], soft[:, j], AX.X).then_inc(smaxed.sem, 1)
                dve.wait_ge(smaxed.sem, at(smaxed, i, u, j))
                nc.vector.tensor_tensor(soft[:, j], soft[:, j], smax[:, j].rearrange("p (h a) -> p h a", a=1)
                                        .broadcast_to([P, H, S2]), ALU.subtract).then_inc(shifted.sem, 1)

            def softmax_end(i, u, j):
                dve.wait_ge(exped.sem, at(exped, i, u, j))
                nc.vector.reduce_sum(ssum[:, j], soft[:, j], AX.X).then_inc(ssummed.sem, 1)
                dve.wait_ge(ssummed.sem, at(ssummed, i, u, j))
                nc.vector.reciprocal(ssum[:, j], ssum[:, j]).then_inc(inverted.sem, 1)

            def chain(i, u, stage):
                p = parity(u)
                if stage == "out":
                    dve.wait_ge(biased.sem, at(biased, i, u, 0))
                    for j in range(TT):
                        bank = wait_product(i, u, AT_OUT + j)
                        nc.vector.scalar_tensor_tensor(x1[:, j], bank, UN, x1[:, j], ALU.mult,
                                                       ALU.add).then_inc(dve_read.sem, 1)
                    spreads(x1, stats, agg, rstd, chain_norm, i, u, 0, dve_read, nth(USES, AT_OUT))
                elif stage == "norm1":
                    norm(x1, agg, rstd, chain_norm, i, u, 0)
                elif stage == "turn1":
                    for j in range(TT):
                        cols = slice(j * P, (j + 1) * P)
                        lo_part(i, u, AT_T1 + j, j, x1T[:, 1, :, cols], x1T[:, 0, :, cols])
                elif stage.startswith("scores"):
                    j = int(stage[-1])
                    if j == 0:
                        dve.wait_ge(kv_loaded, 48 * (chunk(i, u) + 1))
                        nc.vector.tensor_scalar(mask_sb[:], mask_sb[:], NEG, None, ALU.mult).then_inc(masked.sem, 1)
                        dve.wait_ge(masked.sem, at(masked, i, u, 0))
                    softmax_start(i, u, j)
                    if j > 0:
                        softmax_end(i, u, j - 1)
                    if j == TT - 1:
                        softmax_end(i, u, j)
                elif stage.startswith("pv"):
                    g = int(stage[-1])
                    lo_part(i, u, AT_VAL[g], TT + g, oT[:, 1, g], oT[:, 0, g])
                elif stage == "out2":
                    dve.wait_ge(biased.sem, at(biased, i, u, 1))
                    dve.wait_ge(stored[p], stored_at(i + u))
                    for j in range(TT):
                        bank = wait_product(i, u, AT_O + j)
                        nc.vector.scalar_tensor_tensor(x2[p][:, j], bank, UN, x1[:, j], ALU.mult,
                                                       ALU.add).then_inc(dve_read.sem, 1)
                    spreads(x2[p], stats, agg, rstd, chain_norm, i, u, 1, dve_read, nth(USES, AT_O))
                elif stage == "norm2":
                    norm(x2[p], agg, rstd, chain_norm, i, u, 1)
                elif stage == "turn2":
                    for j in range(TT):
                        cols = slice(j * P, (j + 1) * P)
                        lo_part(i, u, AT_T2 + j, TT + NG + j, x2T[p][:, 1, :, cols], x2T[p][:, 0, :, cols])
                elif stage == "route":
                    dve.wait_ge(squared.sem, at(squared, i, u, TT - 1))
                    nc.vector.tensor_scalar(square[:], square[:], 1e-24, None, ALU.max).then_inc(square_held.sem, 1)
                    dve.wait_ge(norm_rooted.sem, at(norm_rooted, i, u, 0))
                    bank = wait_product(i, u, AT_R)[:, 0:TT * 2 * E].rearrange("p (j n) -> p j n", j=TT)
                    wide = lambda a: a.rearrange("p (j a) -> p j a", a=1).broadcast_to([P, TT, E])
                    nc.vector.scalar_tensor_tensor(weight[:], bank[:, :, 0:E], UN, wide(rnorm[:]), ALU.mult,
                                                   ALU.mult).then_inc(routed.sem, 1)
                    dve.wait_ge(routed.sem, at(routed, i, u, 0))
                    half = TT // 2
                    nc.vector.scalar_tensor_tensor(logit[:, 0:half], bank[:, 0:half, E:2 * E], UN, weight[:, 0:half],
                                                   ALU.mult, ALU.add).then_inc(routed.sem, 1)
                    dve.wait_ge(routed.sem, at(routed, i, u, 1))
                    nc.vector.scalar_tensor_tensor(logit[:, half:], bank[:, half:, E:2 * E], UN, weight[:, half:],
                                                   ALU.mult, ALU.add).then_inc(dve_read.sem, 1)
                    for r, step in ((0, 4), (half, 7)):
                        for j in range(r, r + half):
                            nc.vector.max(top[:, j], logit[:, j]).then_inc(routed.sem, 1)
                        dve.wait_ge(dve_read.sem, at(dve_read, i, u, nth(USES, AT_R)))
                        dve.wait_ge(routed.sem, at(routed, i, u, step - 1))
                        nc.vector.tensor_tensor(chosen[:, r:r + half], logit[:, r:r + half],
                                                top[:, r:r + half, 1:2].broadcast_to([P, half, E]),
                                                ALU.is_ge).then_inc(routed.sem, 1)
                    dve.wait_ge(routed.sem, at(routed, i, u, 7))
                    nc.vector.tensor_tensor(logit[:], logit[:], top[:, :, 0:1].broadcast_to([P, TT, E]),
                                            ALU.subtract).then_inc(routed.sem, 1)
                elif stage == "gate":
                    dve.wait_ge(gate_exped.sem, at(gate_exped, i, u, 0))
                    nc.vector.tensor_tensor(weight[:], weight[:], chosen[:], ALU.mult).then_inc(routed.sem, 1)
                    dve.wait_ge(routed.sem, at(routed, i, u, 9))
                    nc.vector.reduce_sum(gsum[:], weight[:], AX.X).then_inc(routed.sem, 1)
                    dve.wait_ge(routed.sem, at(routed, i, u, 10))
                    nc.vector.reciprocal(gsum[:], gsum[:]).then_inc(routed.sem, 1)
                    dve.wait_ge(routed.sem, at(routed, i, u, 11))
                    wide = gsum[:].rearrange("p (j a) -> p j a", a=1).broadcast_to([P, TT, E])
                    nc.vector.tensor_tensor(gates[:], weight[:], wide, ALU.mult).then_inc(routed.sem, 1)
                    nc.vector.scalar_tensor_tensor(gates_un[p][:], weight[:], UN, wide, ALU.mult,
                                                   ALU.mult).then_inc(gated.sem, 1)

            def experts(i, u, f, kind, e, j):
                bank = fps[:, (u * NUNIT + f) % FB]
                q = u
                if kind == "hidden":
                    n = 2 * e + j
                    dve.wait_ge(gelu_done.sem, at(gelu_done, i, u, n))
                    if j == 0:
                        dve.wait_ge(f_ready.sem, at(f_ready, i, u, UNITS.index(("expert", e - 2, TT - 1)) if e >= 2
                                                    else UNITS.index(("expert", E + e - 2, TT - 1)) - NUNIT))
                    nc.vector.tensor_scalar(hT[:, 0, e % 2, j], hidden[:, n % 2], XS, None,
                                            ALU.mult).then_inc(h_hi.sem, 1)
                    dve.wait_ge(h_hi.sem, at(h_hi, i, u, n))
                    nc.vector.scalar_tensor_tensor(hT[:, 1, e % 2, j], hidden[:, n % 2], XS, hT[:, 0, e % 2, j],
                                                   ALU.mult, ALU.subtract).then_inc(h_lo.sem, 1)
                    return
                dve.wait_ge(f_ready.sem, at(f_ready, i, u, f))
                if kind == "bias":
                    nc.vector.tensor_tensor(x2[q][:, j], bank, x2[q][:, j], ALU.add).then_inc(added.sem, 1)
                else:
                    dve.wait_ge(added.sem, at(added, i, u, e * TT + j))
                    nc.vector.scalar_tensor_tensor(x2[q][:, j], bank, gates_un[q][:, j, e:e + 1], x2[q][:, j],
                                                   ALU.mult, ALU.add).then_inc(added.sem, 1)

            def finish(i, u):
                c = summed3, spread3, varied3, rooted3, normed3
                spreads(x2[u], stats3, agg3, rstd3, c, i, u, 0, added, E * TT)
                norm(x2[u], agg3, rstd3, c, i, u, 0)

            def apart(n, dst):
                dve.wait_ge(w_hi, n + 1)
                nc.vector.scalar_tensor_tensor(dst[1], raws[n % len(raws)], WS, dst[0], ALU.mult,
                                               ALU.subtract).then_inc(w_lo, 1)

            gated.lead(dve, made=1)
            def context():
                dve.wait_ge(kv_done, 1)
                for b in range(B):
                    nc.vector.tensor_tensor(vals_made[:, b], value_product(b), W["bv_bc"][:],
                                            ALU.add).then_inc(vals_done, 1)

            run(dve, program(chain, experts, finish, apart, context))

        @block.tensor
        def _(pe):
            lead(pe, (c_ready,), (f_ready,))

            def chain_bank(i, u, k):
                if k >= CB:
                    who = USES[k - CB]
                    c, n = (act_read if who == "act" else dve_read), nth(USES, k - CB)
                else:
                    who = USES[NUSE + k - CB]
                    c = act_read if who == "act" else dve_read
                    n = nth(USES, NUSE + k - CB) - c.per // 2
                pe.wait_ge(c.sem, at(c, i, u, n))
                return cps[:, (u * NUSE + k) % CB]

            def experts_bank(i, u, f):
                who = F_USES[f - FB]
                c = gelu_done if who == "act" else added
                n = nth(F_USES, (f - FB) % NUNIT) - (0 if f >= FB else c.per // 2)
                pe.wait_ge(c.sem, at(c, i, u, n))
                return fps[:, (u * NUNIT + f) % FB]

            def product(bank, lhs, rhs, tiles):
                steps = [(t, a, b) for t in range(tiles) for a, b in TERMS]
                for n, (t, a, b) in enumerate(steps):
                    last = nc.tensor.matmul(bank, lhs(a, t), rhs(b, t), start=(n == 0), stop=(n == len(steps) - 1))
                return last

            def chain(i, u, stage):
                p = parity(u)
                if stage in ("out", "out2"):
                    if stage == "out":
                        pe.wait_ge(oT_loaded, 16 * (chunk(i, u) + 1))
                        k0, w = AT_OUT, W["wout_p"]
                    else:
                        pe.wait_ge(dve_read.sem, at(dve_read, i, u, nth(USES, AT_O - 1)))
                        k0, w = AT_O, W["wo_p"]
                    for j in range(TT):
                        bank = chain_bank(i, u, k0 + j)
                        product(bank, lambda a, t: oT[:, a, t, j * P:(j + 1) * P], lambda b, t: w[b][:, t],
                                KT).then_inc(c_ready.sem, 1)
                elif stage in ("turn1", "turn2"):
                    k0, src, done = (AT_T1, x1, 0) if stage == "turn1" else (AT_T2, x2[p], TT)
                    for j in range(TT):
                        pe.wait_ge(normed.sem, at(normed, i, u, done + j))
                        bank = chain_bank(i, u, k0 + j)
                        for t in range(KT):
                            cols = slice(t * P, (t + 1) * P)
                            last = nc.tensor.transpose(bank[:, cols], src[:, j, cols], ident[:])
                        last.then_inc(c_ready.sem, 1)
                elif stage == "query":
                    pe.wait_ge(dve_read.sem, at(dve_read, i, u, nth(USES, AT_T1 + TT - 1)))
                    for o in range(KT):
                        bank = chain_bank(i, u, AT_Q + o)
                        product(bank, lambda a, t: W["wq_p"][a][:, t, o * P:(o + 1) * P], lambda b, t: x1T[:, b, t],
                                KT).then_inc(c_ready.sem, 1)
                elif stage.startswith("scores"):
                    j = int(stage[-1])
                    if j == 0:
                        pe.wait_ge(kv_loaded, 48 * (chunk(i, u) + 1))
                        pe.wait_ge(act_read.sem, at(act_read, i, u, KT - 1))
                    for g in range(NG):
                        bank = chain_bank(i, u, AT_S + j * NG + g)
                        nc.tensor.matmul(bank[:, 0:KS], xq[:, g, j * P:(j + 1) * P], keys[:, g], start=True,
                                         stop=True).then_inc(c_ready.sem, 1)
                elif stage.startswith("probs"):
                    g = int(stage[-1])
                    pe.wait_ge(probs_ready.sem, at(probs_ready, i, u, TT - 1))
                    for h in range(HG):
                        bank = chain_bank(i, u, AT_TURN[g] + h)
                        for j in range(TT):
                            last = nc.tensor.transpose(bank[0:S2, j * P:(j + 1) * P], soft[:, j, g * HG + h], ident[:])
                        last.then_inc(c_ready.sem, 1)
                elif stage.startswith("pv"):
                    g = int(stage[-1])
                    bank = chain_bank(i, u, AT_VAL[g])
                    pe.wait_ge(act_read.sem, at(act_read, i, u, nth(USES, AT_TURN[g] + HG - 1)))
                    for h in range(HG):
                        f = (g * HG + h) * DH
                        last = nc.tensor.matmul(bank[h * DH:(h + 1) * DH], vals[:, f:f + DH], turned(g)[:, h],
                                                start=True, stop=True)
                    last.then_inc(c_ready.sem, 1)
                elif stage == "route":
                    pe.wait_ge(dve_read.sem, at(dve_read, i, u, nth(USES, AT_T2 + TT - 1)))
                    bank = chain_bank(i, u, AT_R)
                    for j in range(TT):
                        last = product(bank[:, j * 2 * E:(j + 1) * 2 * E],
                                       lambda a, t: x2T[p][:, a, t, j * P:(j + 1) * P],
                                       lambda b, t: W["route_p"][b][:, t], KT)
                    last.then_inc(c_ready.sem, 1)
                elif stage == "gate":
                    pe.wait_ge(routed.sem, at(routed, i, u, 12))
                    bank = chain_bank(i, u, AT_G)
                    for j in range(TT):
                        last = nc.tensor.transpose(bank[0:E, j * P:(j + 1) * P], gates[:, j], ident[:])
                    last.then_inc(c_ready.sem, 1)

            def experts(i, u, f, kind, e, j):
                bank = experts_bank(i, u, f)
                if kind == "bias":
                    pe.wait_ge(act_read.sem, at(act_read, i, u, nth(USES, AT_G) - act_read.per // 2))
                    last = nc.tensor.matmul(bank, gT[u][:, j], W["b2_sb"][:], start=True, stop=True)
                elif kind == "hidden":
                    n = 2 * e + j
                    last = product(bank, lambda a, t: W["w1_p"][a][:, t, n * P:(n + 1) * P],
                                   lambda b, t: x2T[u][:, b, t], KT)
                else:
                    pe.wait_ge(h_lo.sem, at(h_lo, i, u, 2 * e + 1))
                    last = product(bank, lambda a, t: hT[:, a, e % 2, t, j * P:(j + 1) * P],
                                   lambda b, t: W["w2_p"][b][:, 2 * e + t], DE // P)
                last.then_inc(f_ready.sem, 1)

            def context():
                pe.wait_ge(S["ctx_loaded"], 16)
                for n in range(2):
                    pe.wait_ge(S["raw_loaded"][n], 16)
                ctx_sb, raw_k, raw_v = S["ctx_sb"], *S["raws"][0:2]
                for g in range(NG):
                    for t in range(KT):
                        nc.tensor.matmul(key_product(g), raw_k[:, t * D + g * P:t * D + (g + 1) * P], ctx_sb[:, t],
                                         start=(t == 0), stop=(t == KT - 1))
                for b in range(B):
                    for t in range(KT):
                        last = nc.tensor.matmul(value_product(b), ctx_sb[:, t, b * S2:(b + 1) * S2],
                                                raw_v[:, t * D:(t + 1) * D], start=(t == 0), stop=(t == KT - 1))
                last.then_inc(kv_done, 1)

            run(pe, program(chain, experts, context=context, after="out"), weights_used=True)


def layer(nc, x_rows, xT, ctxT, mask, wqkvT, woutT, bout, wq, bq, wk, bk, wv, bv, wo, bo, w1, b1, w2, b2, centroids,
          routeT, out):
    dram = lambda name, shape, dt: nc.dram_tensor(name, shape, dt).ap()
    q_parts, k_parts, o_parts = (dram(n, [2, D, N], F16) for n in ("q_parts", "k_parts", "o_parts"))
    v_rows = dram("v_rows", [N, D], F32)
    project_qkv(nc, xT, wqkvT, q_parts, k_parts, v_rows)
    with ExitStack() as stack:
        S, prefetch = shared(nc, stack, ctxT, wk, wv, woutT, wq, wo)
        self_attention(nc, q_parts, k_parts, v_rows, o_parts, prefetch)
        second_half(nc, S, x_rows, o_parts, mask, bout, bq, bk, bv, bo, w1, b1, w2, b2, centroids, routeT, out)


def shared(nc, stack, ctxT, wk, wv, woutT, wq, wo):
    S = {"work": stack.enter_context(nc.sbuf_tensor("work", [P, 2, TT * D], F32)),
         "ctx_sb": stack.enter_context(nc.sbuf_tensor("ctx_sb", [P, KT, B * S2], F32))}
    for name, shape, dt in (("x2", [P, TT, D], F32), ("x2T", [P, 2, KT, CH], F16)):
        S[name] = [stack.enter_context(nc.sbuf_tensor(f"{name}_{a}", shape, dt)) for a in range(2)]
    for name in ("ctx_loaded", "x_loaded", "oT_loaded"):
        S[name] = stack.enter_context(nc.semaphore("half_" + name))
    S["raws"] = ([S["work"][:, n] for n in range(2)] + [x[:].rearrange("p j n -> p (j n)") for x in S["x2"]]
                 + [S["x2T"][0][:].rearrange("p s t n -> p (s t n)").bitcast(F32)])
    S["raw_loaded"] = sems(nc, stack, "raw_loaded", len(S["raws"]))
    prefetch = [(S["ctx_sb"][:], ctxT.rearrange("(t p) n -> p t n", p=P), S["ctx_loaded"])]
    for raw, loaded, src in zip(S["raws"], S["raw_loaded"], (wk, wv, woutT, wq, wo)):
        prefetch.append((raw.rearrange("p (t n) -> p t n", t=KT), src.rearrange("(t p) n -> p t n", p=P), loaded))
    return S, prefetch


def second_half(nc, S, x_rows, o_parts, mask, bout, bq, bk, bv, bo, w1, b1, w2, b2, centroids, routeT, out):
    dram = lambda name, shape, dt: nc.dram_tensor(name, shape, dt).ap()
    k_blocks, v_ctx = dram("k_blocks", [B, P, NG * HG * S2], F32), dram("v_ctx", [B, S2, D], F32)
    with ExitStack() as stack:
        W = {name: S[name] for name in ("work", "x2", "x2T")}

        def resident(name, shape, dt):
            W[name] = stack.enter_context(nc.sbuf_tensor(name, shape, dt))

        def parts(name, shape):
            W[name] = [stack.enter_context(nc.sbuf_tensor(f"{name}_{s}", shape, F16)) for s in ("hi", "lo")]

        for name in ("wout_p", "wq_p", "wo_p"):
            parts(name, [P, KT, D])
        parts("w1_p", [P, KT, E * DE])
        parts("w2_p", [P, FT, D])
        parts("route_p", [P, KT, 2 * E])
        resident("route_raw", [P, KT, 2 * E], F32)
        resident("ident", [P, P], F32)
        resident("power", [P, H], F32)
        resident("oT", [P, 2, KT, CH], F16)
        resident("x1", [P, TT, D], F32)
        resident("soft", [P, TT, H, S2], F32)
        resident("hidden", [P, 2, CH], F32)
        resident("hT", [P, 2, 2, 2, CH], F16)
        resident("bout_bc", [P, D], F32)
        resident("bo_bc", [P, D], F32)
        resident("bk_sb", [P, KT], F32)
        resident("bv_bc", [S2, D], F32)
        resident("bq_sb", [P, KT], F32)
        resident("b1_sb", [P, FT], F32)
        resident("b2_sb", [E, D], F32)
        cols = lambda t: t.rearrange("p t n -> p (t n)")
        first = [[cols(part[:]) for part in W[name]] for name in ("wout_p", "wq_p", "wo_p")]
        weights = []
        for t in range(KT):
            weights.append((w1[:, t * P:(t + 1) * P, :].rearrange("e p h -> p e h"),
                            [part[:, t] for part in W["w1_p"]]))
        for n in range(FT // KT):
            weights.append((w2.rearrange("e (t p) n -> p (e t) n", p=P)[:, n * KT:(n + 1) * KT],
                            [cols(part[:, n * KT:(n + 1) * KT]) for part in W["w2_p"]]))
        prepare(nc, W, S, x_rows, o_parts, bk, bv, first, centroids, routeT, bout, bo, bq, b1, b2)
        chains(nc, W, S, weights, x_rows, o_parts, mask, k_blocks, v_ctx, out)


_INPUTS = ["x", "ctx_1024", "mask_Bx1x1xS2_ff0", "L0_attn_Wqkv", "L0_attn_Wout", "L0_attn_bout", "L0_xattn_Wq",
           "L0_xattn_bq", "L0_xattn_Wk", "L0_xattn_bk", "L0_xattn_Wv", "L0_xattn_bv", "L0_xattn_Wo", "L0_xattn_bo",
           "L0_ffn_w1", "L0_ffn_b1", "L0_ffn_w2", "L0_ffn_b2", "L0_ffn_centroids", "L0_ffn_w_route"]


def kernel(**inputs):
    import numpy as np
    import concourse.bacc as bacc
    from concourse.bass_utils import run_bass_kernel_spmd

    a = {k: np.asarray(inputs[k]) for k in _INPUTS}
    arrays = {
        "x_rows": a["x"].reshape(N, D), "xT": a["x"].reshape(N, D).T, "ctxT": a["ctx_1024"].reshape(B * S2, D).T,
        "mask": a["mask_Bx1x1xS2_ff0"], "wqkvT": a["L0_attn_Wqkv"].T, "woutT": a["L0_attn_Wout"].T,
        "bout": a["L0_attn_bout"], "wq": a["L0_xattn_Wq"], "bq": a["L0_xattn_bq"].reshape(KT, P).T,
        "wk": a["L0_xattn_Wk"], "bk": a["L0_xattn_bk"].reshape(KT, P).T, "wv": a["L0_xattn_Wv"],
        "bv": a["L0_xattn_bv"], "wo": a["L0_xattn_Wo"],
        "bo": a["L0_xattn_bo"], "w1": a["L0_ffn_w1"], "b1": a["L0_ffn_b1"].reshape(FT, P).T, "w2": a["L0_ffn_w2"],
        "b2": a["L0_ffn_b2"], "centroids": a["L0_ffn_centroids"], "routeT": a["L0_ffn_w_route"].T,
    }
    arrays = {k: np.ascontiguousarray(v) for k, v in arrays.items()}
    nc = bacc.Bacc("TRN2", target_bir_lowering=False, num_devices=1)
    handles = {k: nc.dram_tensor(f"{k}_in", v.shape, F32, kind="ExternalInput").ap() for k, v in arrays.items()}
    out = nc.dram_tensor("out", [N, D], F32, kind="ExternalOutput").ap()
    layer(nc, out=out, **handles)
    r = run_bass_kernel_spmd(nc, [{f"{k}_in": v for k, v in arrays.items()}], core_ids=[0])
    return r.results[0]["out"].reshape(B, T, D)
```
